# Optimizing a Trainium2 kernel written in Bass

```python
import numpy as np
import jax
import jax.numpy as jnp

def _softmax(x, axis=-1):
    return jax.nn.softmax(x, axis=axis)

def _gelu(x):
    return jax.nn.gelu(x, approximate=True)

def _silu(x):
    return jax.nn.silu(x)

def _sigmoid(x):
    return jax.nn.sigmoid(x)

def _layernorm(x, axis=-1, eps=1e-05):
    m = jnp.mean(x, axis=axis, keepdims=True)
    v = jnp.var(x, axis=axis, keepdims=True)
    return (x - m) / jnp.sqrt(v + eps)

def _scatter_add(tgt, idx, src, axis=0):
    return tgt.at[idx].add(src)

def _segment_sum(src, seg, n):
    return jax.ops.segment_sum(src, seg, n)
kernel_name = 'mk_vit_tower_postln_d2_tok_img1024_r4_b00846'

def setup_inputs(seed: int=0):
    np.random.seed(seed)
    _w = jnp.asarray

    def _rec_inputs():
        import jax
        import jax.numpy as jnp
        _rk = jax.random.key(seed)
        x = -0.000169711 + 1.00022 * jax.random.normal(jax.random.fold_in(_rk, 1), (128, 3, 96, 96), jnp.float32)
        return x
    x = _rec_inputs()

    def _L0_tok_setup():
        import jax, jax.numpy as jnp
        import numpy as np
        C = 256
        H8 = 8
        DH = C // H8
        PS = 14
        CS = 3
        IMG = 168
        B = 4

        def _ln(x, g, b):
            mu = jnp.mean(x, axis=-1, keepdims=True)
            xc = x - mu
            var = jnp.mean(xc * xc, axis=-1, keepdims=True)
            return xc * jax.lax.rsqrt(var + 1e-05) * g + b

        def _forward(pixel_values, conv_w, class_emb, la_ln_q_g, la_ln_q_b, la_wq, la_ln_kv_g, la_ln_kv_b, la_wkv, la_proj_w, la_proj_b, ga_ln_q_g, ga_ln_q_b, ga_wq, ga_ln_kv_g, ga_ln_kv_b, ga_wkv, ga_proj_w, ga_proj_b, mod_w, mod_b):
            b = pixel_values.shape[0]
            pe = jax.lax.conv_general_dilated(pixel_values, conv_w, (PS, PS), 'VALID', dimension_numbers=('NCHW', 'OIHW', 'NCHW'))
            HP = pe.shape[2]
            h = HP // CS
            hw, N = (h * h, CS * CS)
            scale = C ** (-0.5)
            grid = pe.reshape(b, C, h, CS, h, CS)
            red = grid.mean(axis=(3, 5)).reshape(b, C, hw).transpose(0, 2, 1)
            win = grid.transpose(0, 2, 4, 3, 5, 1).reshape(b, hw, N, C)
            q = _ln(red, la_ln_q_g, la_ln_q_b) @ la_wq
            q = q.reshape(b, hw, H8, DH).transpose(0, 2, 1, 3)
            kv = _ln(win, la_ln_kv_g, la_ln_kv_b) @ la_wkv
            kv = kv.reshape(b, hw, N, 2, H8, DH).transpose(3, 0, 4, 1, 2, 5)
            k_, v_ = (kv[0], kv[1])
            attn = jax.nn.softmax(jnp.einsum('bhnd,bhnkd->bhnk', q * scale, k_), axis=-1)
            agg = jnp.einsum('bhnk,bhnkd->bhnd', attn, v_)
            agg = agg.transpose(0, 2, 1, 3).reshape(b, hw, C)
            local_out = red + agg @ la_proj_w + la_proj_b
            cls = jnp.broadcast_to(class_emb, (b, 1, C))
            gq = (_ln(cls, ga_ln_q_g, ga_ln_q_b) @ ga_wq).reshape(b, H8, DH)
            gkv = _ln(local_out, ga_ln_kv_g, ga_ln_kv_b) @ ga_wkv
            gkv = gkv.reshape(b, hw, 2, H8, DH).transpose(2, 0, 3, 1, 4)
            gk, gv = (gkv[0], gkv[1])
            gattn = jax.nn.softmax(jnp.einsum('bhd,bhnd->bhn', gq * scale, gk), axis=-1)
            gagg = jnp.einsum('bhn,bhnd->bhd', gattn, gv).reshape(b, 1, C)
            cls_out = cls + gagg @ ga_proj_w + ga_proj_b
            patch_out = local_out @ mod_w + mod_b
            return jnp.concatenate([patch_out, cls_out], axis=1)
        key = jax.random.key(seed)
        ks = jax.random.split(key, 16)
        nrm = lambda k, shape: jax.random.normal(k, shape, jnp.float32) * 0.02
        return {'pixel_values': jax.random.normal(ks[0], (B, 3, IMG, IMG), jnp.float32), 'pixel_masks': jnp.ones((B, 1, IMG, IMG), jnp.float32), 'conv_w': nrm(ks[1], (C, 3, PS, PS)), 'class_emb': nrm(ks[2], (C,)), 'la_ln_q_g': jnp.ones((C,)), 'la_ln_q_b': jnp.zeros((C,)), 'la_wq': nrm(ks[3], (C, C)), 'la_ln_kv_g': jnp.ones((C,)), 'la_ln_kv_b': jnp.zeros((C,)), 'la_wkv': nrm(ks[4], (C, 2 * C)), 'la_proj_w': nrm(ks[5], (C, C)), 'la_proj_b': jnp.zeros((C,)), 'ga_ln_q_g': jnp.ones((C,)), 'ga_ln_q_b': jnp.zeros((C,)), 'ga_wq': nrm(ks[6], (C, C)), 'ga_ln_kv_g': jnp.ones((C,)), 'ga_ln_kv_b': jnp.zeros((C,)), 'ga_wkv': nrm(ks[7], (C, 2 * C)), 'ga_proj_w': nrm(ks[8], (C, C)), 'ga_proj_b': jnp.zeros((C,)), 'mod_w': nrm(ks[9], (C, C)), 'mod_b': jnp.zeros((C,))}
    _L0_tok_all = _L0_tok_setup()
    _L0_tok_in = {k: v for k, v in _L0_tok_all.items() if k in ('pixel_masks', 'conv_w', 'class_emb', 'la_ln_q_g', 'la_ln_q_b', 'la_wq', 'la_ln_kv_g', 'la_ln_kv_b', 'la_wkv', 'la_proj_w', 'la_proj_b', 'ga_ln_q_g', 'ga_ln_q_b', 'ga_wq', 'ga_ln_kv_g', 'ga_ln_kv_b', 'ga_wkv', 'ga_proj_w', 'ga_proj_b', 'mod_w', 'mod_b')}
    del _L0_tok_all

    def _L0_attn_setup():
        import math
        import jax, jax.numpy as jnp
        import numpy as np
        NUM_BUCKETS = 32
        MAX_DISTANCE = 128
        N_HEADS = 16
        D_KV = 64

        def _relative_position_bucket(relative_position, num_buckets=NUM_BUCKETS, max_distance=MAX_DISTANCE):
            nb = num_buckets // 2
            n = -relative_position
            ret = (n < 0).astype(jnp.int32) * nb
            n = jnp.abs(n)
            max_exact = nb // 2
            is_small = n < max_exact
            val_if_large = max_exact + (jnp.log(jnp.maximum(n, 1).astype(jnp.float32) / max_exact) / math.log(max_distance / max_exact) * (nb - max_exact)).astype(jnp.int32)
            val_if_large = jnp.minimum(val_if_large, nb - 1)
            return ret + jnp.where(is_small, n, val_if_large)
        key = jax.random.key(seed)
        ks = jax.random.split(key, 6)
        d_model = 256
        inner = N_HEADS * D_KV
        scale = 1.0 / math.sqrt(d_model)
        x = jax.random.normal(ks[0], (2, 512, d_model), dtype=jnp.float32)
        wq = jax.random.normal(ks[1], (d_model, inner), dtype=jnp.float32) * scale
        wk = jax.random.normal(ks[2], (d_model, inner), dtype=jnp.float32) * scale
        wv = jax.random.normal(ks[3], (d_model, inner), dtype=jnp.float32) * scale
        wo = jax.random.normal(ks[4], (inner, d_model), dtype=jnp.float32) * scale
        rel_emb = jax.random.normal(ks[5], (NUM_BUCKETS, N_HEADS), dtype=jnp.float32)
        return {'x': x, 'wq': wq, 'wk': wk, 'wv': wv, 'wo': wo, 'rel_emb': rel_emb}
    _L0_attn_all = _L0_attn_setup()
    _L0_attn_in = {k: v for k, v in _L0_attn_all.items() if k in ('wq', 'wk', 'wv', 'wo', 'rel_emb')}
    del _L0_attn_all

    def _L0_ffn_setup():
        import jax, jax.numpy as jnp
        import numpy as np
        BLOCK = 32
        W_BITS = 4
        ACT_BITS = 16

        def act_qdq(x):
            qmax = 2.0 ** (ACT_BITS - 1) - 1.0
            scale = jnp.maximum(jnp.max(jnp.abs(x)) / qmax, 1e-12)
            return jnp.clip(jnp.round(x / scale), -qmax - 1.0, qmax) * scale

        def fixed_qdq_u16(x):
            scale = 1.0 / 65536.0
            return jnp.clip(jnp.round(x / scale), 0.0, 65535.0) * scale

        def lpbq_dequant(w):
            O, I = w.shape
            qmax = 2.0 ** (W_BITS - 1) - 1.0
            wb = w.reshape(O, I // BLOCK, BLOCK)
            s = jnp.maximum(jnp.max(jnp.abs(wb), axis=-1, keepdims=True) / qmax, 1e-12)
            wq = jnp.clip(jnp.round(wb / s), -qmax - 1.0, qmax) * s
            return wq.reshape(O, I)
        key = jax.random.key(seed)
        k1, k2, k3, k4 = jax.random.split(key, 4)
        B, S, H, I = (2, 1024, 256, 768)
        x = jax.random.normal(k1, (B, S, H), jnp.float32)
        w_gate = jax.random.normal(k2, (I, H), jnp.float32) * 0.02
        w_up = jax.random.normal(k3, (I, H), jnp.float32) * 0.02
        w_down = jax.random.normal(k4, (H, I), jnp.float32) * 0.02
        return {'x': x, 'w_gate': w_gate, 'w_up': w_up, 'w_down': w_down}
    _L0_ffn_all = _L0_ffn_setup()
    _L0_ffn_in = {k: v for k, v in _L0_ffn_all.items() if k in ('w_gate', 'w_up', 'w_down')}
    del _L0_ffn_all

    def _L1_attn_setup():
        import jax, jax.numpy as jnp
        import numpy as np
        KEY_DIM = 256
        SCALE = KEY_DIM ** (-0.5)
        key = jax.random.key(seed)
        k1, k2, k3, k4 = jax.random.split(key, 4)
        B, S, E = (4, 512, 256)
        x = jax.random.normal(k1, (B, S, E), dtype=jnp.float32)
        WQ = jax.random.normal(k2, (KEY_DIM, E), dtype=jnp.float32) * E ** (-0.5)
        WK = jax.random.normal(k3, (KEY_DIM, E), dtype=jnp.float32) * E ** (-0.5)
        WV = jax.random.normal(k4, (KEY_DIM, E), dtype=jnp.float32) * E ** (-0.5)
        return {'x': x, 'WQ': WQ, 'WK': WK, 'WV': WV}
    _L1_attn_all = _L1_attn_setup()
    _L1_attn_in = {k: v for k, v in _L1_attn_all.items() if k in ('WQ', 'WK', 'WV')}
    del _L1_attn_all

    def _L1_ffn_setup():
        import jax, jax.numpy as jnp
        import numpy as np
        E = 16
        G = 4
        EPG = E // G
        K = 4
        TOPK_GROUP = 2
        PER_GROUP_K = K // TOPK_GROUP

        def _route(xf, router_w, correction_bias):
            S = xf.shape[0]
            logits = xf @ router_w.T
            scores = jax.nn.sigmoid(logits)
            sb = scores + correction_bias
            grp_top = jax.lax.top_k(sb.reshape(S, G, EPG), PER_GROUP_K)[0]
            group_scores = grp_top.sum(axis=-1)
            _, group_idx = jax.lax.top_k(group_scores, TOPK_GROUP)
            group_mask = jnp.zeros((S, G), sb.dtype).at[jnp.arange(S)[:, None], group_idx].set(1.0)
            score_mask = jnp.broadcast_to(group_mask[:, :, None], (S, G, EPG)).reshape(S, E)
            masked = jnp.where(score_mask > 0, sb, -jnp.inf)
            _, topk_idx = jax.lax.top_k(masked, K)
            w = jnp.take_along_axis(scores, topk_idx, axis=1)
            w = w / (w.sum(axis=-1, keepdims=True) + 1e-20)
            return (topk_idx, w, scores)
        key = jax.random.key(seed)
        ks = jax.random.split(key, 9)
        B, T, C, H, HS = (2, 256, 256, 64, 512)
        std = 0.02
        return {'x': jax.random.normal(ks[0], (B, T, C), jnp.float32), 'router_w': jax.random.normal(ks[1], (E, C), jnp.float32) * std, 'correction_bias': jnp.zeros((E,), jnp.float32), 'gate_w': jax.random.normal(ks[2], (E, C, H), jnp.float32) * std, 'up_w': jax.random.normal(ks[3], (E, C, H), jnp.float32) * std, 'down_w': jax.random.normal(ks[4], (E, H, C), jnp.float32) * std, 'shared_gate_w': jax.random.normal(ks[5], (HS, C), jnp.float32) * std, 'shared_up_w': jax.random.normal(ks[6], (HS, C), jnp.float32) * std, 'shared_down_w': jax.random.normal(ks[7], (C, HS), jnp.float32) * std}
    _L1_ffn_all = _L1_ffn_setup()
    _L1_ffn_in = {k: v for k, v in _L1_ffn_all.items() if k in ('router_w', 'correction_bias', 'gate_w', 'up_w', 'down_w', 'shared_gate_w', 'shared_up_w', 'shared_down_w')}
    del _L1_ffn_all
    return {'x': x, 'L0_tok_pixel_masks': _L0_tok_in['pixel_masks'], 'L0_tok_conv_w': _L0_tok_in['conv_w'], 'L0_tok_class_emb': _L0_tok_in['class_emb'], 'L0_tok_la_ln_q_g': _L0_tok_in['la_ln_q_g'], 'L0_tok_la_ln_q_b': _L0_tok_in['la_ln_q_b'], 'L0_tok_la_wq': _L0_tok_in['la_wq'], 'L0_tok_la_ln_kv_g': _L0_tok_in['la_ln_kv_g'], 'L0_tok_la_ln_kv_b': _L0_tok_in['la_ln_kv_b'], 'L0_tok_la_wkv': _L0_tok_in['la_wkv'], 'L0_tok_la_proj_w': _L0_tok_in['la_proj_w'], 'L0_tok_la_proj_b': _L0_tok_in['la_proj_b'], 'L0_tok_ga_ln_q_g': _L0_tok_in['ga_ln_q_g'], 'L0_tok_ga_ln_q_b': _L0_tok_in['ga_ln_q_b'], 'L0_tok_ga_wq': _L0_tok_in['ga_wq'], 'L0_tok_ga_ln_kv_g': _L0_tok_in['ga_ln_kv_g'], 'L0_tok_ga_ln_kv_b': _L0_tok_in['ga_ln_kv_b'], 'L0_tok_ga_wkv': _L0_tok_in['ga_wkv'], 'L0_tok_ga_proj_w': _L0_tok_in['ga_proj_w'], 'L0_tok_ga_proj_b': _L0_tok_in['ga_proj_b'], 'L0_tok_mod_w': _L0_tok_in['mod_w'], 'L0_tok_mod_b': _L0_tok_in['mod_b'], 'L0_attn_wq': _L0_attn_in['wq'], 'L0_attn_wk': _L0_attn_in['wk'], 'L0_attn_wv': _L0_attn_in['wv'], 'L0_attn_wo': _L0_attn_in['wo'], 'L0_attn_rel_emb': _L0_attn_in['rel_emb'], 'L0_ffn_w_gate': _L0_ffn_in['w_gate'], 'L0_ffn_w_up': _L0_ffn_in['w_up'], 'L0_ffn_w_down': _L0_ffn_in['w_down'], 'L1_attn_WQ': _L1_attn_in['WQ'], 'L1_attn_WK': _L1_attn_in['WK'], 'L1_attn_WV': _L1_attn_in['WV'], 'L1_ffn_router_w': _L1_ffn_in['router_w'], 'L1_ffn_correction_bias': _L1_ffn_in['correction_bias'], 'L1_ffn_gate_w': _L1_ffn_in['gate_w'], 'L1_ffn_up_w': _L1_ffn_in['up_w'], 'L1_ffn_down_w': _L1_ffn_in['down_w'], 'L1_ffn_shared_gate_w': _L1_ffn_in['shared_gate_w'], 'L1_ffn_shared_up_w': _L1_ffn_in['shared_up_w'], 'L1_ffn_shared_down_w': _L1_ffn_in['shared_down_w']}

def reference(x, L0_tok_pixel_masks, L0_tok_conv_w, L0_tok_class_emb, L0_tok_la_ln_q_g, L0_tok_la_ln_q_b, L0_tok_la_wq, L0_tok_la_ln_kv_g, L0_tok_la_ln_kv_b, L0_tok_la_wkv, L0_tok_la_proj_w, L0_tok_la_proj_b, L0_tok_ga_ln_q_g, L0_tok_ga_ln_q_b, L0_tok_ga_wq, L0_tok_ga_ln_kv_g, L0_tok_ga_ln_kv_b, L0_tok_ga_wkv, L0_tok_ga_proj_w, L0_tok_ga_proj_b, L0_tok_mod_w, L0_tok_mod_b, L0_attn_wq, L0_attn_wk, L0_attn_wv, L0_attn_wo, L0_attn_rel_emb, L0_ffn_w_gate, L0_ffn_w_up, L0_ffn_w_down, L1_attn_WQ, L1_attn_WK, L1_attn_WV, L1_ffn_router_w, L1_ffn_correction_bias, L1_ffn_gate_w, L1_ffn_up_w, L1_ffn_down_w, L1_ffn_shared_gate_w, L1_ffn_shared_up_w, L1_ffn_shared_down_w):
    import jax
    import jax.numpy as jnp

    def _L0_tok_ref(pixel_values, pixel_masks, conv_w, class_emb, la_ln_q_g, la_ln_q_b, la_wq, la_ln_kv_g, la_ln_kv_b, la_wkv, la_proj_w, la_proj_b, ga_ln_q_g, ga_ln_q_b, ga_wq, ga_ln_kv_g, ga_ln_kv_b, ga_wkv, ga_proj_w, ga_proj_b, mod_w, mod_b):
        import jax, jax.numpy as jnp
        import numpy as np
        C = 256
        H8 = 8
        DH = C // H8
        PS = 14
        CS = 3
        IMG = 168
        B = 4

        def _ln(x, g, b):
            mu = jnp.mean(x, axis=-1, keepdims=True)
            xc = x - mu
            var = jnp.mean(xc * xc, axis=-1, keepdims=True)
            return xc * jax.lax.rsqrt(var + 1e-05) * g + b

        def _forward(pixel_values, conv_w, class_emb, la_ln_q_g, la_ln_q_b, la_wq, la_ln_kv_g, la_ln_kv_b, la_wkv, la_proj_w, la_proj_b, ga_ln_q_g, ga_ln_q_b, ga_wq, ga_ln_kv_g, ga_ln_kv_b, ga_wkv, ga_proj_w, ga_proj_b, mod_w, mod_b):
            b = pixel_values.shape[0]
            pe = jax.lax.conv_general_dilated(pixel_values, conv_w, (PS, PS), 'VALID', dimension_numbers=('NCHW', 'OIHW', 'NCHW'))
            HP = pe.shape[2]
            h = HP // CS
            hw, N = (h * h, CS * CS)
            scale = C ** (-0.5)
            grid = pe.reshape(b, C, h, CS, h, CS)
            red = grid.mean(axis=(3, 5)).reshape(b, C, hw).transpose(0, 2, 1)
            win = grid.transpose(0, 2, 4, 3, 5, 1).reshape(b, hw, N, C)
            q = _ln(red, la_ln_q_g, la_ln_q_b) @ la_wq
            q = q.reshape(b, hw, H8, DH).transpose(0, 2, 1, 3)
            kv = _ln(win, la_ln_kv_g, la_ln_kv_b) @ la_wkv
            kv = kv.reshape(b, hw, N, 2, H8, DH).transpose(3, 0, 4, 1, 2, 5)
            k_, v_ = (kv[0], kv[1])
            attn = jax.nn.softmax(jnp.einsum('bhnd,bhnkd->bhnk', q * scale, k_), axis=-1)
            agg = jnp.einsum('bhnk,bhnkd->bhnd', attn, v_)
            agg = agg.transpose(0, 2, 1, 3).reshape(b, hw, C)
            local_out = red + agg @ la_proj_w + la_proj_b
            cls = jnp.broadcast_to(class_emb, (b, 1, C))
            gq = (_ln(cls, ga_ln_q_g, ga_ln_q_b) @ ga_wq).reshape(b, H8, DH)
            gkv = _ln(local_out, ga_ln_kv_g, ga_ln_kv_b) @ ga_wkv
            gkv = gkv.reshape(b, hw, 2, H8, DH).transpose(2, 0, 3, 1, 4)
            gk, gv = (gkv[0], gkv[1])
            gattn = jax.nn.softmax(jnp.einsum('bhd,bhnd->bhn', gq * scale, gk), axis=-1)
            gagg = jnp.einsum('bhn,bhnd->bhd', gattn, gv).reshape(b, 1, C)
            cls_out = cls + gagg @ ga_proj_w + ga_proj_b
            patch_out = local_out @ mod_w + mod_b
            return jnp.concatenate([patch_out, cls_out], axis=1)
        del pixel_masks
        return _forward(pixel_values, conv_w, class_emb, la_ln_q_g, la_ln_q_b, la_wq, la_ln_kv_g, la_ln_kv_b, la_wkv, la_proj_w, la_proj_b, ga_ln_q_g, ga_ln_q_b, ga_wq, ga_ln_kv_g, ga_ln_kv_b, ga_wkv, ga_proj_w, ga_proj_b, mod_w, mod_b)

    def _L0_attn_ref(x, wq, wk, wv, wo, rel_emb):
        import math
        import jax, jax.numpy as jnp
        import numpy as np
        NUM_BUCKETS = 32
        MAX_DISTANCE = 128
        N_HEADS = 16
        D_KV = 64

        def _relative_position_bucket(relative_position, num_buckets=NUM_BUCKETS, max_distance=MAX_DISTANCE):
            nb = num_buckets // 2
            n = -relative_position
            ret = (n < 0).astype(jnp.int32) * nb
            n = jnp.abs(n)
            max_exact = nb // 2
            is_small = n < max_exact
            val_if_large = max_exact + (jnp.log(jnp.maximum(n, 1).astype(jnp.float32) / max_exact) / math.log(max_distance / max_exact) * (nb - max_exact)).astype(jnp.int32)
            val_if_large = jnp.minimum(val_if_large, nb - 1)
            return ret + jnp.where(is_small, n, val_if_large)
        B, S, D = x.shape
        q = (x @ wq).reshape(B, S, N_HEADS, D_KV)
        k = (x @ wk).reshape(B, S, N_HEADS, D_KV)
        v = (x @ wv).reshape(B, S, N_HEADS, D_KV)
        scores = jnp.einsum('bqhd,bkhd->bhqk', q, k)
        ctx = jnp.arange(S)[:, None]
        mem = jnp.arange(S)[None, :]
        buckets = _relative_position_bucket(mem - ctx)
        bias = rel_emb[buckets]
        bias = jnp.transpose(bias, (2, 0, 1))[None]
        scores = scores + bias
        weights = jax.nn.softmax(scores.astype(jnp.float32), axis=-1).astype(scores.dtype)
        context = jnp.einsum('bhqk,bkhd->bqhd', weights, v).reshape(B, S, N_HEADS * D_KV)
        return context @ wo

    def _L0_ffn_ref(x, w_gate, w_up, w_down):
        import jax, jax.numpy as jnp
        import numpy as np
        BLOCK = 32
        W_BITS = 4
        ACT_BITS = 16

        def act_qdq(x):
            qmax = 2.0 ** (ACT_BITS - 1) - 1.0
            scale = jnp.maximum(jnp.max(jnp.abs(x)) / qmax, 1e-12)
            return jnp.clip(jnp.round(x / scale), -qmax - 1.0, qmax) * scale

        def fixed_qdq_u16(x):
            scale = 1.0 / 65536.0
            return jnp.clip(jnp.round(x / scale), 0.0, 65535.0) * scale

        def lpbq_dequant(w):
            O, I = w.shape
            qmax = 2.0 ** (W_BITS - 1) - 1.0
            wb = w.reshape(O, I // BLOCK, BLOCK)
            s = jnp.maximum(jnp.max(jnp.abs(wb), axis=-1, keepdims=True) / qmax, 1e-12)
            wq = jnp.clip(jnp.round(wb / s), -qmax - 1.0, qmax) * s
            return wq.reshape(O, I)
        x = act_qdq(x)
        up = act_qdq(x @ lpbq_dequant(w_up).T)
        gate = act_qdq(x @ lpbq_dequant(w_gate).T)
        sig = fixed_qdq_u16(jax.nn.sigmoid(gate))
        gate = act_qdq(gate * sig)
        o = act_qdq(gate * up)
        return o @ lpbq_dequant(w_down).T

    def _L1_attn_ref(x, WQ, WK, WV):
        import jax, jax.numpy as jnp
        import numpy as np
        KEY_DIM = 256
        SCALE = KEY_DIM ** (-0.5)
        q = jnp.einsum('bse,ke->bsk', x, WQ)
        k = jnp.einsum('bse,ke->bsk', x, WK)
        v = jnp.einsum('bse,ve->bsv', x, WV)
        scores = jnp.einsum('bsk,btk->bst', q, k) * SCALE
        masked = jnp.where(jnp.tril(scores) == 0, -jnp.inf, scores)
        attn = jax.nn.softmax(masked, axis=-1)
        return jnp.einsum('bst,btv->bsv', attn, v)

    def _L1_ffn_ref(x, router_w, correction_bias, gate_w, up_w, down_w, shared_gate_w, shared_up_w, shared_down_w):
        import jax, jax.numpy as jnp
        import numpy as np
        E = 16
        G = 4
        EPG = E // G
        K = 4
        TOPK_GROUP = 2
        PER_GROUP_K = K // TOPK_GROUP

        def _route(xf, router_w, correction_bias):
            S = xf.shape[0]
            logits = xf @ router_w.T
            scores = jax.nn.sigmoid(logits)
            sb = scores + correction_bias
            grp_top = jax.lax.top_k(sb.reshape(S, G, EPG), PER_GROUP_K)[0]
            group_scores = grp_top.sum(axis=-1)
            _, group_idx = jax.lax.top_k(group_scores, TOPK_GROUP)
            group_mask = jnp.zeros((S, G), sb.dtype).at[jnp.arange(S)[:, None], group_idx].set(1.0)
            score_mask = jnp.broadcast_to(group_mask[:, :, None], (S, G, EPG)).reshape(S, E)
            masked = jnp.where(score_mask > 0, sb, -jnp.inf)
            _, topk_idx = jax.lax.top_k(masked, K)
            w = jnp.take_along_axis(scores, topk_idx, axis=1)
            w = w / (w.sum(axis=-1, keepdims=True) + 1e-20)
            return (topk_idx, w, scores)
        B, T, C = x.shape
        S = B * T
        xf = x.reshape(S, C)
        sg = xf @ shared_gate_w.T
        su = xf @ shared_up_w.T
        shared_out = jax.nn.silu(sg) * su @ shared_down_w.T
        topk_idx, w, _scores = _route(xf, router_w, correction_bias)
        combine = jnp.zeros((S, E), xf.dtype).at[jnp.arange(S)[:, None], topk_idx].add(w)
        g = jnp.einsum('sc,ech->esh', xf, gate_w)
        u = jnp.einsum('sc,ech->esh', xf, up_w)
        h = jax.nn.silu(g) * u
        hw = h * combine.T[:, :, None]
        routed = jnp.einsum('esh,ehc->sc', hw, down_w)
        return (shared_out + routed).reshape(B, T, C)
    h = _L0_tok_ref(x, L0_tok_pixel_masks, L0_tok_conv_w, L0_tok_class_emb, L0_tok_la_ln_q_g, L0_tok_la_ln_q_b, L0_tok_la_wq, L0_tok_la_ln_kv_g, L0_tok_la_ln_kv_b, L0_tok_la_wkv, L0_tok_la_proj_w, L0_tok_la_proj_b, L0_tok_ga_ln_q_g, L0_tok_ga_ln_q_b, L0_tok_ga_wq, L0_tok_ga_ln_kv_g, L0_tok_ga_ln_kv_b, L0_tok_ga_wkv, L0_tok_ga_proj_w, L0_tok_ga_proj_b, L0_tok_mod_w, L0_tok_mod_b)
    h = _layernorm(h + _L0_attn_ref(h, L0_attn_wq, L0_attn_wk, L0_attn_wv, L0_attn_wo, L0_attn_rel_emb), axis=-1)
    h = _layernorm(h + _L0_ffn_ref(h, L0_ffn_w_gate, L0_ffn_w_up, L0_ffn_w_down), axis=-1)
    h = _layernorm(h + _L1_attn_ref(h, L1_attn_WQ, L1_attn_WK, L1_attn_WV), axis=-1)
    h = _layernorm(h + _L1_ffn_ref(h, L1_ffn_router_w, L1_ffn_correction_bias, L1_ffn_gate_w, L1_ffn_up_w, L1_ffn_down_w, L1_ffn_shared_gate_w, L1_ffn_shared_up_w, L1_ffn_shared_down_w), axis=-1)
    return h

_drawn_inputs = setup_inputs


def setup_inputs(seed=0):
    import zlib

    import numpy as np

    out = dict(_drawn_inputs(seed))
    spreads = {'L0_tok_pixel_masks': (1.0, 0.2),
     'L0_tok_la_ln_q_g': (1.0, 0.6),
     'L0_tok_la_ln_q_b': (0.0, 0.8),
     'L0_tok_la_ln_kv_g': (1.0, 0.6),
     'L0_tok_la_ln_kv_b': (0.0, 0.1),
     'L0_tok_la_proj_b': (0.0, 0.1),
     'L0_tok_ga_ln_q_g': (1.0, 0.6),
     'L0_tok_ga_ln_q_b': (0.0, 0.8),
     'L0_tok_ga_ln_kv_g': (1.0, 0.2),
     'L0_tok_ga_ln_kv_b': (0.0, 0.1),
     'L0_tok_ga_proj_b': (0.0, 0.1),
     'L0_tok_mod_b': (0.0, 0.1),
     'L1_ffn_correction_bias': (0.0, 0.8)}
    factors = {'L0_tok_la_wq': 8.0,
     'L0_tok_ga_wq': 8.0,
     'L1_ffn_router_w': 8.0,
     'L1_ffn_gate_w': 8.0,
     'L1_ffn_up_w': 8.0,
     'L1_ffn_down_w': 8.0,
     'L1_ffn_shared_gate_w': 7.297,
     'L1_ffn_shared_up_w': 7.796,
     'L1_ffn_shared_down_w': 7.012}
    for name, (base, spread) in spreads.items():
        noise = np.random.default_rng([zlib.crc32(name.encode()), seed]).standard_normal(out[name].shape)
        drawn = base * np.exp(spread * noise) if base else spread * noise
        out[name] = jnp.asarray(drawn.astype(out[name].dtype))
    for name, factor in factors.items():
        out[name] = (out[name] * factor).astype(out[name].dtype)
    return out
```

```python
from contextlib import ExitStack

import numpy as np

import concourse.bass as bass
from concourse import mybir

F32 = mybir.dt.float32
ALU = mybir.AluOpType
ACT = mybir.ActivationFunctionType
AX = mybir.AxisListType

P = 128
C = 256
KC = C // P
IMG, CH, PS = 96, 3, 14
GP = IMG // PS
NP_ = GP * GP
WS = 3
NW = (GP // WS) ** 2
NPOS = WS * WS
S = NW + 1
LH, LD = 8, 32
NH, DK = 16, 64
INNER = NH * DK
FF = 768
QB, NB = 32, 48
NE, EH, SH = 16, 64, 512
GI = 6
NG = 24
NT = 6
SLOTS = NG * 32
FULLG = P // GI
RESTI = P - FULLG * GI
EPS = 1e-5
MAGIC = 1.5 * 2.0 ** 23
BIG = 1e30
RW = 35200
XROWS = 2

PIX = CH * PS * PS
NK = -(-PIX // P)
CK = -(-PIX // NK)
PIXP = NK * CK
NBATCH = NP_ * NK // 4
XT = 4
ZSLOTS = 27


def window_of(t):
    return (t // GP // WS) * (GP // WS) + (t % GP) // WS


def pos_of(t):
    return (t // GP % WS) * WS + t % WS


def last_batch(t):
    return (t * NK + NK - 1) // 4


def tok_schedule():
    def window(w):
        return ([("red", w), ("redT", w), ("q", w)] + [("kv", w * KVN + m) for m in range(KVN)]
                + [("soft", w), ("pv", w), ("aggT", w), ("proj", w), ("loT", w), ("mod", w),
                   ("loz", w), ("lozT", w), ("gkv", w)])

    def pair(a, b):
        x, y = window(a), window(b)
        lag = 7
        out = []
        for i in range(len(x) + lag):
            if i < len(x):
                out.append(x[i])
            if i >= lag:
                out.append(y[i - lag])
        return out

    steps = [("cls", 0), ("clsT", 0), ("gq", 0)]
    first = pair(0, 1)
    per = 4
    batch = 0
    for t in range(NP_ + 6):
        if t < NP_:
            if t == 0:
                steps.append(("pack", 0))
            if t % WS == 0 and t // WS + 1 < NP_ // WS:
                steps.append(("pack", t // WS + 1))
            while batch <= last_batch(min(t + 1, NP_ - 1)):
                steps.append(("turn", batch))
                batch += 1
            steps.append(("conv", t))
            if t % WS == WS - 1:
                steps.append(("stat", t // WS))
        if t % 2 == 0 and t >= 6:
            steps.append(("zturn", (t - 6) // 2))
        if t >= 23:
            steps += first[:per]
            first = first[per:]
    steps += first + pair(2, 3)
    steps += [("gsoft", 0), ("gaggT", 0), ("gproj", 0)]
    return steps


KVN = -(-NPOS // 2)
TOK = tok_schedule()
READERS = {"clsT": "d", "gq": "d", "redT": "d", "q": "d", "aggT": "a", "proj": "d", "loT": "a",
           "mod": "d", "lozT": "d", "gkv": "d", "gaggT": "d", "gproj": "d"}
SHARED = [s for s in TOK if s[0] in READERS]
SHARED_NO = {s: n for n, s in enumerate(SHARED)}


def bass_vit_tower(nc, a, out):
    with ExitStack() as ctx:
        def sb(name, cols):
            return ctx.enter_context(nc.sbuf_tensor(name, [P, cols], F32))

        names = {}

        def sem(name):
            names[name] = ctx.enter_context(nc.semaphore(name))
            return names[name]

        ident = sb("ident", P)
        own = sb("own", GI)
        ties = sb("ties", NE * NE)
        ties4 = sb("ties4", 16)
        ones = sb("ones", P)
        H = [sb("HA", S * C), sb("HB", S * C)]
        vec_rows = sb("vec_rows", P)
        vec = sb("vec", 16)
        proj_b = sb("proj_b", C)
        gproj_b = sb("gproj_b", C)
        mod_b = sb("mod_b", C)
        cls = sb("cls_row", C)
        corr = sb("corr", NE)
        relb = sb("relb", NE)
        small = sb("small", 840)
        small_at = [0]

        def tiny(n):
            at = small_at[0]
            small_at[0] += n
            assert small_at[0] <= 840
            return small[:, at:at + n]

        wattn = sb("wattn", 4 * 2048)
        ffn_nat = sb("ffn_nat", 3 * NB * QB)
        R = sb("R", RW)

        def area(start):
            at = [start]

            def take(n):
                v = R[:, at[0]:at[0] + n]
                at[0] += n
                assert at[0] <= RW, at[0]
                return v
            return take

        take = area(0)
        xring = [take(CH * PS * IMG).rearrange("p (c r x) -> p c r x", c=CH, r=PS) for _ in range(XROWS)]
        xpack = [take(WS * PIXP) for _ in range(2)]
        zT = take(ZSLOTS * C).rearrange("p (t k n) -> p t k n", t=ZSLOTS, k=KC)
        xT = [take(4 * P) for _ in range(XT)]
        pes = [take(WS * C) for _ in range(2)]
        convT = take(NK * C).rearrange("p (k n) -> p k n", k=NK)
        prod = take(NPOS * C)
        vwin = take(NPOS * C)
        def tok_weight(at, n):
            return wattn[:, 4096 + at:4096 + at + KC * n].rearrange("p (k n) -> p k n", k=KC)

        g_wq, t_wq, t_proj, g_proj = (tok_weight(i * KC * C, C) for i in range(4))
        t_wkv, g_wkv = tok_weight(4 * KC * C, 2 * C), tok_weight(6 * KC * C, 2 * C)
        t_mod = take(KC * C).rearrange("p (k n) -> p k n", k=KC)
        conv_nat = zT.rearrange("p t k n -> p (t k n)")[:, (ZSLOTS - 1) * C - KC * PIXP:(ZSLOTS - 1) * C].rearrange("p (k n) -> p k n", k=KC)
        zgrp = [take(WS * C) for _ in range(2)]
        red = take(NW * C).rearrange("p (w n) -> p w n", w=NW)
        tmp = take(C)
        lnz = take(C)
        trn = take(C).rearrange("p (k n) -> p k n", k=KC)
        trn2 = take(C).rearrange("p (k n) -> p k n", k=KC)
        trn3 = take(C).rearrange("p (k n) -> p k n", k=KC)
        qwin = take(C)
        agg = take(C)
        lo = take(C)
        gq = take(C)
        gv = take(NW * C)

        psum = ctx.enter_context(nc.psum_tensor("psum", [P, 8 * 512], F32))

        def bank(b, n=512, at=0):
            return psum[:, b * 512 + at:b * 512 + at + n]

        st3, mv3, rs3 = tiny(WS * 6), tiny(WS * 2), tiny(WS)
        rc3 = tiny(WS)
        st1, mv1, rc1, rs1 = tiny(6), tiny(2), tiny(1), tiny(1)
        sc = tiny(NPOS * LH)
        mx8, sm8, rs8 = tiny(LH), tiny(LH), tiny(LH)
        gs = tiny(NW * LH)
        eps_unused = tiny(1)

        ld_conv, ld_ident, ld_vec = sem("ld_conv"), sem("ld_ident"), sem("ld_vec")
        ld_x = [sem(f"ld_x{i}") for i in range(XROWS)]
        ld_cls, ld_tokw, ld_small, ld_attnw, ld_ffn = sem("ld_cls"), sem("ld_tokw"), sem("ld_small"), sem("ld_attnw"), sem("ld_ffn")
        dve_chain, act_chain = sem("dve_chain"), sem("act_chain")
        ones_set = sem("ones_set")
        conv_turned, conv_kept = sem("conv_turned"), sem("conv_kept")
        vec_turned, vec_kept = sem("vec_turned"), sem("vec_kept")
        pads_zero = sem("pads_zero")
        turned, turned_kept_act, turned_kept_dve = sem("turned"), sem("turned_kept_act"), sem("turned_kept_dve")
        packed = sem("packed")
        conv_done, conv_kept_sb = sem("conv_done"), sem("conv_kept_sb")
        var_ready, rstd_ready = sem("var_ready"), sem("rstd_ready")
        z_ready, z_turned, z_kept = sem("z_ready"), sem("z_turned"), sem("z_kept")
        win_ready, win_read = sem("win_ready"), sem("win_read")
        k_ready, k_read, v_ready, v_read = sem("k_ready"), sem("k_read"), sem("v_ready"), sem("v_read")
        ln_var, ln_rstd, ln_z, ln_kept = sem("ln_var"), sem("ln_rstd"), sem("ln_z"), sem("ln_kept")
        shifted, exp_done, probs_ready = sem("shifted"), sem("exp_done"), sem("probs_ready")
        pv_done, agg_ready = sem("pv_done"), sem("agg_ready")
        aggT_kept, lo_ready, loT_kept = sem("aggT_kept"), sem("lo_ready"), sem("loT_kept")
        tok_tail = sem("tok_tail")

        block = ctx.enter_context(nc.Block())

        LN = {s: n for n, s in enumerate(s for s in TOK if s[0] in ("cls", "red", "loz"))}
        LNT = {"clsT": "cls", "redT": "red", "lozT": "loz"}
        SM = {s: n for n, s in enumerate(s for s in TOK if s[0] in ("soft", "gsoft"))}
        AGG = {s: n for n, s in enumerate(s for s in TOK if s[0] in ("pv", "gsoft"))}
        AGGT = {s: n for n, s in enumerate(s for s in TOK if s[0] in ("aggT", "gaggT"))}

        def shared(step):
            return SHARED_NO[step], bank(7)

        def pixels(chunk):
            t, j = chunk // NK, chunk % NK
            at = t % WS * PIXP + j * CK
            return xpack[t // WS % 2][:, at:at + CK]

        def batch_kept(eng, b):
            if b >= 1:
                eng.wait_ge(turned_kept_dve, (b + 1) // 2)
            eng.wait_ge(turned_kept_act, b // 2 + 1)

        def window_patch(w, k):
            per = GP // WS
            return ((w // per) * WS + k // WS) * GP + (w % per) * WS + k % WS

        def attn_view(ap, n):
            return ap.rearrange("p (k h d) -> p k h d", h=LH, d=LD)[:, 0:n]

        take = area(0)
        hT = take(KC * SLOTS).rearrange("p (k n) -> p k n", k=KC)
        qT = take(8 * SLOTS).rearrange("p (k n) -> p k n", k=8)
        kT = take(8 * SLOTS).rearrange("p (k n) -> p k n", k=8)
        V = take(NT * INNER).rearrange("p (t n) -> p t n", t=NT)
        ctx_area = take(8 * S * P)
        ctxT = ctx_area.rearrange("p (c s n) -> p c s n", c=8, s=S)
        onehot = ctx_area[:, 0:S * P]
        smask = take(NH * 30)
        pexp = [take(NH * 32) for _ in range(2)]
        pT = [take(NH * 32) for _ in range(2)]
        bias = take(S * NH)
        att = take(NH * S)
        att_mx, att_sm = take(NH), take(NH)
        ffnT = take(3 * 12 * P)
        w_q = wattn[:, 0:2048].rearrange("p (k n) -> p k n", k=KC)
        w_k = wattn[:, 2048:4096].rearrange("p (k n) -> p k n", k=KC)
        w_v = wattn[:, 4096:6144].rearrange("p (k n) -> p k n", k=KC)
        w_o = wattn[:, 6144:8192].rearrange("p (k n) -> p k n", k=8)
        upT = ffnT[:, 0:1536].rearrange("p (k n) -> p k n", k=KC)
        gateT = ffnT[:, 1536:3072].rearrange("p (k n) -> p k n", k=KC)
        downT = ffnT[:, 3072:4608].rearrange("p (k n) -> p k n", k=6)
        ffn_abs = tiny(3 * NB)
        ffn_inv = tiny(3 * NB)

        take = area(0)
        h1T = take(KC * S * P).rearrange("p (k n) -> p k n", k=KC)
        h1q = take(S * C)
        up = take(6 * S * P)
        gate = take(6 * S * P)
        sig = take(6 * S * P)
        l1nat = take(3 * KC * C)
        shnat = take(3 * 4 * C)
        rnat = take(C)
        l1T = take(KC * 3 * C).rearrange("p (k n) -> p k n", k=KC)
        assert 0 < 1536 + 2 * 6144 + 6144 + 5120, "layout"
        lay3 = (KC * S * P + S * C + 3 * 6 * S * P + 3 * KC * C + 3 * 4 * C + C + KC * 3 * C)
        lay2 = KC * SLOTS + 16 * SLOTS + NT * INNER + 8 * S * P + NH * 30 + 4 * NH * 32 + S * NH + NH * S + 2 * NH
        assert lay3 <= lay2, (lay3, lay2)
        take = area(lay2 + 4608)
        shT = take(2 * KC * SH).rearrange("p (a k n) -> p a k n", a=2, k=KC)
        rT = take(KC * NE).rearrange("p (k n) -> p k n", k=KC)
        e_gate = wattn[:, 0:2048].rearrange("p (k e n) -> p k e n", k=KC, e=NE)
        e_up = wattn[:, 2048:4096].rearrange("p (k e n) -> p k e n", k=KC, e=NE)
        e_down = wattn[:, 4096:6144].rearrange("p (k n) -> p k n", k=8)
        sdT = wattn[:, 6144:7168].rearrange("p (k n) -> p k n", k=4)
        pick = wattn[:, 7168:8192].rearrange("p (k n) -> p k n", k=8)
        take = area(0)
        h2T = take(KC * S * P).rearrange("p (k n) -> p k n", k=KC)
        qkv = take(S * 3 * C).rearrange("p (s n) -> p s n", s=S)
        scr = take(C)
        h3T = take(KC * S * P).rearrange("p (k n) -> p k n", k=KC)
        hid = take(12 * S * P).rearrange("p (k n) -> p k n", k=12)
        sil = [take(320) for _ in range(2)]
        cmp_a = take(S * NE * NE)
        cmp_b = take(S * NE * NE)
        combT = take(S * P)
        assert KC * S * P * 2 + S * 3 * C + C + 12 * S * P + 640 + 2 * S * NE * NE + S * P <= lay3 - KC * 3 * C
        msc = tiny(S * S)
        mmx, msm = tiny(S), tiny(S)
        st5, mv5, rc5, rs5 = tiny(6), tiny(2), tiny(1), tiny(1)
        pmax, gm, qsc, qinv = tiny(12), tiny(1), tiny(5), tiny(5)

        tok_end_act, tok_end_dve = sem("tok_end_act"), sem("tok_end_dve")
        hT_zero, hT_turned, hT_kept = sem("hT_zero"), sem("hT_turned"), sem("hT_kept")
        bias_mm, bias_ready = sem("bias_mm"), sem("bias_ready")
        qkv_mm, qkv_kept_act, qkv_kept_dve = sem("qkv_mm"), sem("qkv_kept_act"), sem("qkv_kept_dve")
        score_mm, score_read = sem("score_mm"), sem("score_read")
        att_shift, att_exp, pT_ready = sem("att_shift"), sem("att_exp"), sem("pT_ready")
        ctx_mm, ctx_kept_act, ctx_kept_dve = sem("ctx_mm"), sem("ctx_kept_act"), sem("ctx_kept_dve")
        wo_mm, wo_read = sem("wo_mm"), sem("wo_read")
        ffn_scale, ffn_quant = sem("ffn_scale"), sem("ffn_quant")
        pexp_zero = sem("pexp_zero")
        wt_turned, wt_kept_act, wt_kept_dve = sem("wt_turned"), sem("wt_kept_act"), sem("wt_kept_dve")
        rln_var, rln_rstd, h_ready = sem("rln_var"), sem("rln_rstd"), sem("h_ready")
        ld_l1, ld_moe = sem("ld_l1"), sem("ld_moe")
        gmax_part, gmax_row, gmax_one, gmax_all = sem("gmax_part"), sem("gmax_row"), sem("gmax_one"), sem("gmax_all")
        hq_ready, hT2_turned, hT2_kept = sem("hq_ready"), sem("hT2_turned"), sem("hT2_kept")
        ff_mm, ff_kept, ff_max = sem("ff_mm"), sem("ff_kept"), sem("ff_max")
        gate_q, sig_ready, o_ready = sem("gate_q"), sem("sig_ready"), sem("o_ready")
        down_mm, down_read = sem("down_mm"), sem("down_read")
        l1_mm, l1_kept, l1_shift, l1_exp = sem("l1_mm"), sem("l1_kept"), sem("l1_shift"), sem("l1_exp")
        r_mm, r_sig, comb_ready, combT_mm, combT_kept = (sem("r_mm"), sem("r_sig"), sem("comb_ready"), sem("combT_mm"),
                                                         sem("combT_kept"))
        moe_mm, moe_sil, moe_hid = sem("moe_mm"), sem("moe_sil"), sem("moe_hid")
        stored = sem("stored")

        def weight_turns():
            turns = []
            for m, dst in ((0, upT), (1, gateT)):
                for o in range(6):
                    for k in range(KC):
                        turns.append((ffn_nat[:, m * 1536 + o * C + k * P:m * 1536 + o * C + (k + 1) * P],
                                      dst[:, k, o * P:(o + 1) * P]))
            for o in range(KC):
                for k in range(6):
                    turns.append((ffn_nat[:, 2 * 1536 + o * FF + k * P:2 * 1536 + o * FF + (k + 1) * P],
                                  downT[:, k, o * P:(o + 1) * P]))
            n_ffn = len(turns)
            for m in range(3):
                for o in range(KC):
                    for k in range(KC):
                        turns.append((l1nat[:, (m * KC + o) * C + k * P:(m * KC + o) * C + (k + 1) * P],
                                      l1T[:, k, m * C + o * P:m * C + (o + 1) * P]))
            for m in range(2):
                for o in range(4):
                    for k in range(KC):
                        turns.append((shnat[:, (m * 4 + o) * C + k * P:(m * 4 + o) * C + (k + 1) * P],
                                      shT[:, m, k, o * P:(o + 1) * P]))
            for o in range(KC):
                for k in range(4):
                    turns.append((shnat[:, 8 * C + o * SH + k * P:8 * C + o * SH + (k + 1) * P],
                                  sdT[:, k, o * P:(o + 1) * P]))
            for k in range(KC):
                turns.append((rnat[0:NE, k * P:(k + 1) * P], rT[:, k, :]))
            return turns, n_ffn

        TURNS, N_FFN = weight_turns()

        def turn_bank(n):
            return n // 4 % 2

        MOE = [(kind, c, hf) for c in range(12) for hf in range(2)
               for kind in (("gate", "up") if c < 4 else ("gate", "up", "comb"))]

        def moe_count(n, kind):
            return sum(m[0] == kind for m in MOE[:n])

        comb_w = tiny(S * NE)

        def wt_batches(lo_, hi_):
            return [(n, (n // 4 - lo_ // 4) % 2) for n in range(lo_, hi_, 4)]

        BATCHES = wt_batches(0, N_FFN) + wt_batches(N_FFN, len(TURNS))

        def wt_target(n):
            par = dict(BATCHES)[n]
            return sum(1 for m, q in BATCHES if m <= n and q == par)

        def wt_target_all(n):
            return (sum(1 for m, q in BATCHES if m < n and q == 0), sum(1 for m, q in BATCHES if m < n and q == 1))

        def keep_weights(eng, copy, par, lo_, hi_, done, banks):
            for n, q in BATCHES:
                if q == par and lo_ <= n < hi_:
                    eng.wait_ge(wt_turned, BATCHES.index((n, q)) + 1)
                    for i in range(n, min(n + 4, hi_)):
                        src, dst = TURNS[i]
                        m = copy(dst, bank(banks[q], src.shape[0], (i - n) * P))
                    m.then_inc(done, 1)

        def qkv_copy(copy, n):
            if n < 32:
                c, w, hf = n // 4, n // 2 % 2, n % 2
                return copy((qT, kT)[w][:, c, hf * 384:(hf + 1) * 384], bank(2 + n % 4, 384))
            t, hf = (n - 32) // 2, n % 2
            return copy(V[:, t, hf * 512:(hf + 1) * 512], bank(2 + n % 4))

        def ctx_copy(copy, eng, done, t, g):
            grp = 4 * t + g
            k = GI if grp < FULLG else (RESTI if grp == FULLG else 0)
            src = bank(2 + g, 256).rearrange("p (c x) -> p c x", x=32)
            if k == 0:
                eng.sem_inc(done, 1)
                return
            src = src[:, :, 0:k * S].rearrange("p c (i s) -> p c i s", s=S)
            dst = ctxT[:, :, :, grp * GI:grp * GI + k].rearrange("p c s i -> p c i s")
            copy(dst, src).then_inc(done, 1)

        sb_ = tiny(S * NE)
        pairs = cmp_b
        gsum, grank = tiny(S * 4), tiny(S * 4)
        rank, wsum = tiny(S * NE), tiny(S)

        def route(dve, link):
            s3 = comb_w.rearrange("p (s e) -> p s e", e=NE)
            b3 = sb_.rearrange("p (s e) -> p s e", e=NE)
            b4 = sb_.rearrange("p (g e) -> p g e", e=4)
            link(nc.vector.tensor_tensor(b3, s3, corr[:, :].unsqueeze(1).to_broadcast([P, S, NE]), ALU.add))
            pr = pairs[:, 0:S * 4 * 6].rearrange("p (g x) -> p g x", x=6)
            nc.vector.tensor_tensor(pr[:, :, 0:3], b4[:, :, 0:3], b4[:, :, 1:4], ALU.add)
            nc.vector.tensor_tensor(pr[:, :, 3:5], b4[:, :, 0:2], b4[:, :, 2:4], ALU.add)
            link(nc.vector.tensor_tensor(pr[:, :, 5:6], b4[:, :, 0:1], b4[:, :, 3:4], ALU.add))
            link(nc.vector.tensor_reduce(gsum, pr, AX.X, ALU.max))

            def ranks(v, n, tie, out_):
                x = v.rearrange("p (s e) -> p s e", e=n)
                for s in range(S):
                    ga = cmp_a[:, s * n * n:(s + 1) * n * n].rearrange("p (i j) -> p i j", j=n)
                    gb = cmp_b[:, s * n * n:(s + 1) * n * n].rearrange("p (i j) -> p i j", j=n)
                    other = x[:, s, :].unsqueeze(1).to_broadcast([P, n, n])
                    mine = x[:, s, :].unsqueeze(2).to_broadcast([P, n, n])
                    nc.vector.tensor_tensor(ga, other, mine, ALU.is_gt)
                    m = nc.vector.tensor_tensor(gb, other, mine, ALU.is_equal)
                link(m)
                gb = cmp_b[:, 0:S * n * n].rearrange("p (s x) -> p s x", s=S)
                link(nc.vector.tensor_tensor(gb, gb, tie[:, 0:n * n].unsqueeze(1).to_broadcast([P, S, n * n]), ALU.mult))
                ga = cmp_a[:, 0:S * n * n]
                link(nc.vector.tensor_tensor(ga, ga, cmp_b[:, 0:S * n * n], ALU.add))
                link(nc.vector.tensor_reduce(out_, ga.rearrange("p (i j) -> p i j", j=n), AX.X, ALU.add))

            ranks(gsum, 4, ties4, grank)
            link(nc.vector.tensor_scalar(grank, grank, 2.0, -BIG, ALU.is_ge, ALU.mult))
            link(nc.vector.tensor_tensor(b4, b4, grank.unsqueeze(2).to_broadcast([P, S * 4, 4]), ALU.add))
            ranks(sb_, NE, ties, rank)
            link(nc.vector.tensor_scalar(rank, rank, 4.0, None, ALU.is_lt))
            link(nc.vector.tensor_tensor(comb_w, comb_w, rank, ALU.mult))
            link(nc.vector.tensor_reduce(wsum, s3, AX.X, ALU.add))
            link(nc.vector.tensor_scalar(wsum, wsum, 1e-20, None, ALU.add))
            link(nc.vector.reciprocal(wsum, wsum))
            nc.vector.tensor_tensor(s3, s3, wsum.unsqueeze(2).to_broadcast([P, S, NE]), ALU.mult).then_inc(comb_ready, 1)

        @block.sync
        def _(sp):
            sp.dma_start(ident[:, :], a["c_ident"]).then_inc(ld_ident, 16)
            sp.dma_start(conv_nat[:, :, 0:PIX], a["L0_tok_conv_w"].rearrange("(k p) c r x -> p k (c r x)", p=P)).then_inc(ld_conv, 16)

            def row(r):
                x = a["x"][:, :, r * PS:(r + 1) * PS, :].rearrange("b c r x -> b c (r x)")
                sp.dma_start(xring[r % XROWS].rearrange("p c r x -> p c (r x)"), x).then_inc(ld_x[r % XROWS], 16)

            row(0)
            for i, n in enumerate(("la_ln_q_g", "la_ln_q_b", "la_ln_kv_g", "la_ln_kv_b", "ga_ln_q_g", "ga_ln_q_b",
                                   "ga_ln_kv_g", "ga_ln_kv_b")):
                sp.dma_start(vec_rows[2 * i:2 * i + 2, :], a["L0_tok_" + n].rearrange("(k p) -> k p", p=P)).then_inc(ld_vec, 16)
            sp.dma_start(cls[:, :], a["L0_tok_class_emb"].partition_broadcast(P)).then_inc(ld_cls, 16)
            sp.dma_start(g_wq, a["L0_tok_ga_wq"].rearrange("(k p) n -> p k n", p=P)).then_inc(ld_cls, 16)
            row(1)
            for t, n in ((proj_b, "la_proj_b"), (gproj_b, "ga_proj_b"), (mod_b, "mod_b")):
                sp.dma_start(t[:, :], a["L0_tok_" + n].partition_broadcast(P)).then_inc(ld_tokw, 16)
            for t, n in ((t_wq, "la_wq"), (t_wkv, "la_wkv"), (t_proj, "la_proj_w"), (g_wkv, "ga_wkv"),
                         (g_proj, "ga_proj_w"), (t_mod, "mod_w")):
                sp.dma_start(t, a["L0_tok_" + n].rearrange("(k p) n -> p k n", p=P)).then_inc(ld_tokw, 16)
            for r in range(XROWS, GP):
                sp.wait_ge(packed, (r - XROWS + 1) * GP // WS)
                row(r)
            sp.dma_start(corr[:, :], a["L1_ffn_correction_bias"].partition_broadcast(P)).then_inc(ld_small, 16)
            sp.dma_start(relb[0:32, :], a["L0_attn_rel_emb"]).then_inc(ld_small, 16)
            sp.dma_start(own[:, :], a["c_own"]).then_inc(ld_small, 16)
            sp.dma_start(ties[:, :], a["c_ties"].rearrange("a n -> (a n)").partition_broadcast(P)).then_inc(ld_small, 16)
            sp.dma_start(ties4[:, :], a["c_ties4"].rearrange("a n -> (a n)").partition_broadcast(P)).then_inc(ld_small, 16)
            for i, n in enumerate(("w_up", "w_gate")):
                sp.dma_start(ffn_nat[:, i * 1536:(i + 1) * 1536].rearrange("p (k n) -> p k n", n=C),
                             a["L0_ffn_" + n].rearrange("(k p) n -> p k n", p=P)).then_inc(ld_ffn, 16)
            sp.dma_start(ffn_nat[:, 3072:4608].rearrange("p (k n) -> p k n", n=FF),
                         a["L0_ffn_w_down"].rearrange("(k p) n -> p k n", p=P)).then_inc(ld_ffn, 16)
            for t, n in ((w_q, "wq"), (w_k, "wk")):
                sp.dma_start(t, a["L0_attn_" + n].rearrange("(k p) n -> p k n", p=P)).then_inc(ld_attnw, 16)
            sp.wait_ge(tok_end_dve, 1)
            sp.wait_ge(tok_end_act, 1)
            sp.dma_start(onehot[0:32, :], a["c_onehot"]).then_inc(ld_small, 16)
            sp.dma_start(w_v, a["L0_attn_wv"].rearrange("(k p) n -> p k n", p=P)).then_inc(ld_attnw, 16)
            sp.dma_start(w_o, a["L0_attn_wo"].rearrange("(k p) n -> p k n", p=P)).then_inc(ld_attnw, 16)
            sp.wait_ge(ctx_mm, NT)
            sp.wait_ge(wo_mm, S)
            for i, n in enumerate(("WQ", "WK", "WV")):
                sp.dma_start(l1nat[:, i * 512:(i + 1) * 512].rearrange("p (k n) -> p k n", n=C),
                             a["L1_attn_" + n].rearrange("(k p) n -> p k n", p=P)).then_inc(ld_l1, 16)
            for i, n in enumerate(("gate", "up")):
                sp.dma_start(shnat[:, i * 1024:(i + 1) * 1024].rearrange("p (k n) -> p k n", n=C),
                             a[f"L1_ffn_shared_{n}_w"].rearrange("(k p) n -> p k n", p=P)).then_inc(ld_l1, 16)
            sp.dma_start(shnat[:, 2048:3072].rearrange("p (k n) -> p k n", n=SH),
                         a["L1_ffn_shared_down_w"].rearrange("(k p) n -> p k n", p=P)).then_inc(ld_l1, 16)
            sp.dma_start(rnat[0:NE, :], a["L1_ffn_router_w"]).then_inc(ld_l1, 16)
            for k in range(KC):
                for t, n in ((e_gate, "gate_w"), (e_up, "up_w")):
                    sp.dma_start(t[:, k], a["L1_ffn_" + n][:, k * P:(k + 1) * P, :].rearrange("e p n -> p e n")).then_inc(ld_moe, 16)
            sp.dma_start(e_down, a["L1_ffn_down_w"].rearrange("(k e) h n -> (e h) k n", e=2)).then_inc(ld_moe, 16)
            sp.dma_start(pick[0:NE], a["c_pick"].rearrange("e (k n) -> e k n", k=8)).then_inc(ld_moe, 16)
            for s in range(S):
                sp.wait_ge(h_ready, 3 * S + s + 1)
                sp.dma_start(out[:, s, :], H[0][:, s * C:(s + 1) * C]).then_inc(stored, 16)
            sp.wait_ge(stored, 16 * S)

        @block.gpsimd
        def _(pool):
            nc.gpsimd.memset(ones[:, :], 1.0).then_inc(ones_set, 1)
            for x in xpack:
                nc.gpsimd.memset(x.rearrange("p (t y) -> p t y", t=WS)[:, :, PIX:PIXP], 0.0).then_inc(pads_zero, 1)
            nc.gpsimd.memset(conv_nat[:, :, PIX:PIXP], 0.0).then_inc(pads_zero, 1)
            for step, i in TOK:
                if step == "pack":
                    row = i * WS // GP
                    pool.wait_ge(ld_x[row % XROWS], 16 * (row // XROWS + 1))
                    if i >= 2:
                        pool.wait_ge(turned, last_batch(WS * (i - 1) - 1) + 1)
                    x = i * WS % GP * PS
                    src = xring[row % XROWS].rearrange("p c r x -> p (c r) x")[:, :, x:x + WS * PS]
                    dst = xpack[i % 2].rearrange("p (t y) -> p t y", t=WS)[:, :, 0:PIX]
                    nc.gpsimd.tensor_copy(dst.rearrange("p t (cr x) -> p t cr x", x=PS),
                                          src.rearrange("p cr (t x) -> p t cr x", x=PS)).then_inc(packed, 1)
                if step == "pv":
                    pool.wait_ge(probs_ready, SM[("soft", i)] + 1)
                    pool.wait_ge(v_read, (i + 1) * KVN)
                    v = vwin.rearrange("p (kh d) -> p kh d", d=LD)
                    nc.gpsimd.tensor_tensor(prod.rearrange("p (kh d) -> p kh d", d=LD), v,
                                            sc[:, :].unsqueeze(2).to_broadcast([P, NPOS * LH, LD]),
                                            ALU.mult).then_inc(pv_done, 1)
            pool.wait_ge(ffn_scale, 1)
            pool.wait_ge(ld_ffn, 48)
            w = ffn_nat[:, :].rearrange("p (b n) -> p b n", n=QB)
            wf = ffn_nat[:, :]
            nc.gpsimd.tensor_tensor(w, w, ffn_inv.unsqueeze(2).to_broadcast([P, 3 * NB, QB]), ALU.mult).then_inc(ffn_quant, 1)
            pool.wait_ge(ffn_quant, 1)
            nc.gpsimd.tensor_scalar(wf, wf, MAGIC, MAGIC, ALU.add, ALU.subtract).then_inc(ffn_quant, 1)
            pool.wait_ge(ffn_quant, 2)
            nc.gpsimd.tensor_tensor(w, w, ffn_abs.unsqueeze(2).to_broadcast([P, 3 * NB, QB]), ALU.mult).then_inc(ffn_quant, 1)
            pool.wait_ge(turned, NBATCH)
            nc.gpsimd.memset(hT, 0.0).then_inc(hT_zero, 1)
            pool.wait_ge(tok_end_dve, 1)
            pool.wait_ge(tok_end_act, 1)
            for b in range(2):
                nc.gpsimd.memset(pexp[b], 0.0).then_inc(pexp_zero, 1)

        @block.tensor
        def _(pe):
            pe.wait_ge(ld_ident, 16)
            pe.wait_ge(ld_conv, 16)
            pe.wait_ge(pads_zero, 3)
            for j in range(NK):
                for k in range(KC):
                    w = conv_nat[:, k, j * CK:(j + 1) * CK]
                    m = pe.transpose(bank(j)[0:CK, k * P:(k + 1) * P], w, ident[:, :])
                m.then_inc(conv_turned, 1)
            pe.wait_ge(ld_vec, 16 * 8)
            pe.transpose(bank(5, 16), vec_rows[0:16, :], ident[0:16, 0:16]).then_inc(vec_turned, 1)
            pe.wait_ge(conv_kept, NK)
            pe.wait_ge(vec_kept, 1)
            for step, i in TOK:
                if step == "turn":
                    pe.wait_ge(packed, (4 * i + 3) // NK // WS + 1)
                    if i >= 2:
                        pe.wait_ge(turned_kept_dve if i % 2 else turned_kept_act, i // 2)
                    for j in range(4):
                        m = pe.transpose(bank(i % 2, P, j * P)[0:CK, :], pixels(4 * i + j), ident[:, :])
                    m.then_inc(turned, 1)
                elif step == "conv":
                    batch_kept(pe, last_batch(i))
                    if i >= 2:
                        pe.wait_ge(conv_kept_sb, i - 1)
                    for j in range(NK):
                        b, at = (i * NK + j) // 4, (i * NK + j) % 4 * P
                        m = pe.matmul(bank(2 + i % 2, C), xT[b % XT][0:CK, at:at + P], convT[0:CK, j, :],
                                      start=(j == 0), stop=(j == NK - 1))
                    m.then_inc(conv_done, 1)
                elif step == "zturn":
                    pe.wait_ge(z_ready, (2 * i + 1) // WS + 1)
                    if i >= 1:
                        pe.wait_ge(z_kept, i)
                    for x in range(2):
                        t = 2 * i + x
                        for k in range(KC):
                            m = pe.transpose(bank(4, P, (k * 2 + x) * P),
                                             zgrp[t // WS % 2][:, (t % WS) * C + k * P:(t % WS) * C + (k + 1) * P], ident[:, :])
                    m.then_inc(z_turned, 1)
                elif step == "kv":
                    w, first = i // KVN, i % KVN * 2
                    ks = range(first, min(first + 2, NPOS))
                    pe.wait_ge(z_kept, window_patch(w, ks[-1]) // 2 + 1)
                    pe.wait_ge(ld_tokw, 16 * 9)
                    for b, ready, read, at in ((5, k_ready, k_read, 0), (6, v_ready, v_read, C)):
                        if i >= 1:
                            pe.wait_ge(read, i)
                        for x, pos in enumerate(ks):
                            for k in range(KC):
                                m = pe.matmul(bank(b, C, x * C), zT[:, window_patch(w, pos) % ZSLOTS, k, :],
                                              t_wkv[:, k, at:at + C], start=(k == 0), stop=(k == KC - 1))
                        m.then_inc(ready, 1)
                elif (step, i) in SHARED_NO:
                    n, o = shared((step, i))
                    if n >= 1:
                        pe.wait_ge(win_read, n)
                    if step in LNT:
                        pe.wait_ge(ln_z, LN[(LNT[step], i)] + 1)
                        for k in range(KC):
                            m = pe.transpose(o[:, k * P:(k + 1) * P], lnz[:, k * P:(k + 1) * P], ident[:, :])
                    elif step in ("gq", "q", "gkv"):
                        if step == "gq":
                            pe.wait_ge(ld_cls, 32)
                        else:
                            pe.wait_ge(ld_tokw, 16 * 9)
                        pe.wait_ge(ln_kept, LN[({"gq": "cls", "q": "red", "gkv": "loz"}[step], i)] + 1)
                        w = {"gq": g_wq, "q": t_wq, "gkv": g_wkv}[step]
                        for k in range(KC):
                            m = pe.matmul(o[:, 0:w.shape[2]], trn[:, k, :], w[:, k, :], start=(k == 0), stop=(k == KC - 1))
                    elif step in ("aggT", "gaggT"):
                        pe.wait_ge(agg_ready, AGG[({"aggT": "pv", "gaggT": "gsoft"}[step], i)] + 1)
                        for k in range(KC):
                            m = pe.transpose(o[:, k * P:(k + 1) * P], agg[:, k * P:(k + 1) * P], ident[:, :])
                    elif step in ("proj", "gproj"):
                        pe.wait_ge(aggT_kept, AGGT[({"proj": "aggT", "gproj": "gaggT"}[step], i)] + 1)
                        pe.wait_ge(ld_tokw, 16 * 9)
                        w = t_proj if step == "proj" else g_proj
                        for k in range(KC):
                            m = pe.matmul(o[:, 0:C], trn2[:, k, :], w[:, k, :], start=(k == 0), stop=(k == KC - 1))
                    elif step == "loT":
                        pe.wait_ge(lo_ready, i + 1)
                        for k in range(KC):
                            m = pe.transpose(o[:, k * P:(k + 1) * P], lo[:, k * P:(k + 1) * P], ident[:, :])
                    elif step == "mod":
                        pe.wait_ge(loT_kept, i + 1)
                        for k in range(KC):
                            m = pe.matmul(o[:, 0:C], trn3[:, k, :], t_mod[:, k, :], start=(k == 0), stop=(k == KC - 1))
                    m.then_inc(win_ready, 1)
            pe.wait_ge(tok_end_dve, 1)
            pe.wait_ge(tok_end_act, 1)
            pe.wait_ge(ld_small, 16 * 6)
            for j in range(S):
                m = pe.matmul(bank(2, NH, j * NH), onehot[0:32, j * P:(j + 1) * P], relb[0:32, :], start=True, stop=True)
            m.then_inc(bias_mm, 1)

            def turn_weights(lo_, hi_, banks):
                for n in range(lo_, hi_, 4):
                    q = n // 4 - lo_ // 4
                    if q >= 2:
                        pe.wait_ge(wt_kept_dve if q % 2 else wt_kept_act, wt_target(n - 8))
                    for i in range(n, min(n + 4, hi_)):
                        src, dst = TURNS[i]
                        rows = src.shape[0]
                        m = pe.transpose(bank(banks[q % 2], rows, (i - n) * P), src, ident[0:rows, 0:rows])
                    m.then_inc(wt_turned, 1)

            for s in range(S):
                if s >= 2:
                    pe.wait_ge(hT_kept, s - 1)
                for k in range(KC):
                    m = pe.transpose(bank(s % 2, P, k * P), H[0][:, s * C + k * P:s * C + (k + 1) * P], ident[:, :])
                m.then_inc(hT_turned, 1)
            pe.wait_ge(ffn_quant, 3)
            turn_weights(0, N_FFN, (6, 7))
            pe.wait_ge(hT_kept, S)
            pe.wait_ge(ld_attnw, 64)
            pe.wait_ge(bias_ready, 1)
            n = 0
            for c in range(8):
                for w in (w_q, w_k):
                    for hf in range(2):
                        if n >= 4:
                            pe.wait_ge(qkv_kept_dve if n % 2 else qkv_kept_act, (n - 4) // 2 + 1)
                        o = bank(2 + n % 4, SLOTS // 2)
                        for k in range(KC):
                            m = pe.matmul(o, w[:, k, c * P:(c + 1) * P], hT[:, k, hf * 384:(hf + 1) * 384],
                                          start=(k == 0), stop=(k == KC - 1))
                        m.then_inc(qkv_mm, 1)
                        n += 1
            for t in range(NT):
                for hf in range(2):
                    pe.wait_ge(qkv_kept_dve if n % 2 else qkv_kept_act, (n - 4) // 2 + 1)
                    o = bank(2 + n % 4)
                    for k in range(KC):
                        m = pe.matmul(o, hT[:, k, t * P:(t + 1) * P], w_v[:, k, hf * 512:(hf + 1) * 512],
                                      start=(k == 0), stop=(k == KC - 1))
                    m.then_inc(qkv_mm, 1)
                    n += 1
            pe.wait_ge(qkv_kept_act, n // 2)
            pe.wait_ge(qkv_kept_dve, n // 2)

            def scores(t):
                if t >= 2:
                    pe.wait_ge(score_read, t - 1)
                for h in range(NH):
                    r = (h % 2) * DK
                    for g in range(4):
                        sl = slice(t * P + g * 32, t * P + (g + 1) * 32)
                        at = (6 * (t % 2) + h % 2) * 512 + (h // 2) * 32
                        m = pe.matmul(psum[g * 32:(g + 1) * 32, at:at + 32], qT[r:r + DK, h // 2, sl],
                                      kT[r:r + DK, h // 2, sl], start=True, stop=True)
                m.then_inc(score_mm, 1)

            def contexts(t):
                pe.wait_ge(pT_ready, t + 1)
                if t >= 1:
                    pe.wait_ge(ctx_kept_act, 2 * t)
                    pe.wait_ge(ctx_kept_dve, 2 * t)
                for h in range(NH):
                    r = (h % 2) * DK
                    col = ((h % 2) * 8 + h // 2) * 32
                    for g in range(4):
                        at = (2 + g) * 512 + (h // 2) * 32
                        m = pe.matmul(psum[r:r + DK, at:at + 32], V[g * 32:(g + 1) * 32, t, h * DK:(h + 1) * DK],
                                      pT[t % 2][g * 32:(g + 1) * 32, col:col + 32], start=True, stop=True)
                m.then_inc(ctx_mm, 1)

            for t in range(NT + 1):
                if t < NT:
                    scores(t)
                if t >= 1:
                    contexts(t - 1)
            pe.wait_ge(ctx_kept_act, 2 * NT)
            pe.wait_ge(ctx_kept_dve, 2 * NT)
            for s in range(S):
                if s >= 2:
                    pe.wait_ge(wo_read, s - 1)
                for c in range(8):
                    m = pe.matmul(bank(6 + s % 2, C), ctxT[:, c, s, :], w_o[:, c, :], start=(c == 0), stop=(c == 7))
                m.then_inc(wo_mm, 1)

            def global_max(i):
                pe.wait_ge(gmax_part, i + 1)
                pe.transpose(bank(6)[0:1, 0:P], gm[:, :], ident[:, :]).then_inc(gmax_row, 1)
                pe.wait_ge(gmax_one, i + 1)
                pe.matmul(bank(7, 1), ones[0:1, :], gm[0:1, :], start=True, stop=True).then_inc(gmax_all, 1)

            def turn_tokens(src, stage):
                for s in range(S):
                    if s >= 2:
                        pe.wait_ge(hT2_kept, stage * S + s - 1)
                    for k in range(KC):
                        m = pe.transpose(bank(s % 2, P, k * P), src[:, s * C + k * P:s * C + (k + 1) * P], ident[:, :])
                    m.then_inc(hT2_turned, 1)

            global_max(0)
            pe.wait_ge(hq_ready, 1)
            turn_tokens(h1q, 0)
            pe.wait_ge(wt_kept_act, wt_target_all(N_FFN)[0])
            pe.wait_ge(wt_kept_dve, wt_target_all(N_FFN)[1])
            pe.wait_ge(hT2_kept, S)
            n = 0
            for w in (upT, gateT):
                for c in range(6):
                    for hf in range(2):
                        if n >= 6:
                            pe.wait_ge(ff_kept, n - 5)
                        for k in range(KC):
                            m = pe.matmul(bank(n % 6, 320), w[:, k, c * P:(c + 1) * P], h1T[:, k, hf * 320:(hf + 1) * 320],
                                          start=(k == 0), stop=(k == KC - 1))
                        m.then_inc(ff_mm, 1)
                        n += 1
                if w is upT:
                    global_max(1)
            global_max(2)
            pe.wait_ge(ff_kept, 24)
            pe.wait_ge(ld_l1, 16 * 7)
            turn_weights(N_FFN, len(TURNS), (0, 1))
            global_max(3)
            global_max(4)
            pe.wait_ge(o_ready, 1)
            for s in range(S):
                if s >= 2:
                    pe.wait_ge(down_read, s - 1)
                for c in range(6):
                    m = pe.matmul(bank(2 + s % 2, C), sig.rearrange("p (c n) -> p c n", c=6)[:, c, s * P:(s + 1) * P],
                                  downT[:, c, :], start=(c == 0), stop=(c == 5))
                m.then_inc(down_mm, 1)

            pe.wait_ge(wt_kept_act, wt_target_all(len(TURNS))[0])
            pe.wait_ge(wt_kept_dve, wt_target_all(len(TURNS))[1])
            pe.wait_ge(h_ready, 2 * S)
            turn_tokens(H[0], 1)
            for s in range(S):
                pe.wait_ge(hT2_kept, S + s + 1)
                if s >= 2:
                    pe.wait_ge(l1_kept, 2 * (s - 1))
                for hf, (at, width) in enumerate(((0, 512), (512, 256))):
                    for k in range(KC):
                        m = pe.matmul(bank(2 + 2 * (s % 2) + hf, width), h2T[:, k, s * P:(s + 1) * P],
                                      l1T[:, k, at:at + width], start=(k == 0), stop=(k == KC - 1))
                    m.then_inc(l1_mm, 1)

            pe.wait_ge(h_ready, 3 * S)
            turn_tokens(H[1], 2)
            for s in range(S):
                pe.wait_ge(hT2_kept, 2 * S + s + 1)
                for k in range(KC):
                    m = pe.matmul(bank(7, NE, s * NE), h3T[:, k, s * P:(s + 1) * P], rT[:, k, :],
                                  start=(k == 0), stop=(k == KC - 1))
            m.then_inc(r_mm, 1)
            pe.wait_ge(ld_moe, 16 * 6)
            n = 0

            def moe_bank(n):
                return bank(n % 6, 320)

            for n, (kind, c, hf) in enumerate(MOE):
                if n >= 6:
                    q = n - 6
                    if MOE[q][0] == "gate":
                        pe.wait_ge(moe_sil, moe_count(q + 1, "gate"))
                    else:
                        pe.wait_ge(moe_hid, moe_count(q + 1, "up") + moe_count(q + 1, "comb"))
                o = moe_bank(n)
                sl = slice(hf * 320, (hf + 1) * 320)
                if kind == "comb":
                    if c == 4:
                        pe.wait_ge(combT_kept, 1)
                    m = pe.matmul(o, pick[0:NE, c - 4, :], combT[0:NE, sl], start=True, stop=True)
                else:
                    for k in range(KC):
                        if c < 4:
                            w = shT[:, 0 if kind == "gate" else 1, k, c * P:(c + 1) * P]
                        else:
                            w = (e_gate if kind == "gate" else e_up)[:, k, 2 * (c - 4):2 * (c - 4) + 2, :]
                        m = pe.matmul(o, w, h3T[:, k, sl], start=(k == 0), stop=(k == KC - 1))
                m.then_inc(moe_mm, 1)
                if n == 15:
                    pe.wait_ge(comb_ready, 1)
                    pe.wait_ge(r_sig, 1)
                    for s in range(S):
                        b, at = (6, s * P) if s < 4 else (7, 0)
                        m = pe.transpose(bank(b)[0:NE, at:at + P], comb_w[:, s * NE:(s + 1) * NE], ident[:, :])
                    m.then_inc(combT_mm, 1)
            pe.wait_ge(moe_hid, moe_count(len(MOE), "up") + moe_count(len(MOE), "comb"))
            pe.wait_ge(moe_sil, moe_count(len(MOE), "gate"))
            for s in range(S):
                if s >= 2:
                    pe.wait_ge(down_read, S + s - 1)
                for c in range(12):
                    w = sdT[:, c, :] if c < 4 else e_down[:, c - 4, :]
                    m = pe.matmul(bank(s % 2, C), hid[:, c, s * P:(s + 1) * P], w, start=(c == 0), stop=(c == 11))
                m.then_inc(down_mm, 1)

        @block.scalar
        def _(act):
            chain = [0]

            def link(ins):
                chain[0] += 1
                ins.then_inc(act_chain, 1)
                act.wait_ge(act_chain, chain[0])

            for j in range(0, NK, 2):
                act.wait_ge(conv_turned, j + 1)
                nc.scalar.copy(convT[0:CK, j, :], bank(j, C)[0:CK]).then_inc(conv_kept, 1)
            for step, i in TOK:
                if step == "turn" and i % 2 == 0:
                    act.wait_ge(turned, i + 1)
                    if i >= XT:
                        act.wait_ge(conv_done, (4 * (i - XT) + 3) // NK + 1)
                    nc.scalar.copy(xT[i % XT][0:CK, :], bank(i % 2)[0:CK]).then_inc(turned_kept_act, 1)
                elif step == "conv":
                    act.wait_ge(conv_done, i + 1)
                    if i // WS >= 2:
                        act.wait_ge(z_ready, i // WS - 1)
                    nc.scalar.copy(pes[i // WS % 2][:, (i % WS) * C:(i % WS + 1) * C], bank(2 + i % 2, C)).then_inc(conv_kept_sb, 1)
                elif step == "stat":
                    act.wait_ge(var_ready, i + 1)
                    nc.scalar.activation(rs3, rc3, ACT.Sqrt).then_inc(rstd_ready, 1)
                elif step in ("cls", "red", "loz"):
                    act.wait_ge(ln_var, LN[(step, i)] + 1)
                    nc.scalar.activation(rs1, rc1, ACT.Sqrt).then_inc(ln_rstd, 1)
                elif step == "kv":
                    if i % KVN == 0 and i >= KVN:
                        act.wait_ge(pv_done, i // KVN)
                    act.wait_ge(v_ready, i + 1)
                    n = min(2, NPOS - i % KVN * 2) * C
                    nc.scalar.copy(vwin[:, i % KVN * 2 * C:i % KVN * 2 * C + n], bank(6, n)).then_inc(v_read, 1)
                elif step == "soft":
                    act.wait_ge(shifted, SM[(step, i)] + 1)
                    nc.scalar.activation(sc, sc, ACT.Exp).then_inc(exp_done, 1)
                elif step == "gsoft":
                    act.wait_ge(shifted, SM[(step, i)] + 1)
                    nc.scalar.activation(gs, gs, ACT.Exp).then_inc(exp_done, 1)
                elif step == "aggT":
                    n, o = shared((step, i))
                    act.wait_ge(win_ready, n + 1)
                    nc.scalar.copy(trn2, o[:, 0:C].rearrange("p (k n) -> p k n", k=KC)).then_inc(win_read, 1)
                    act.wait_ge(win_read, n + 1)
                    act.sem_inc(aggT_kept, 1)
                elif step == "loT":
                    n, o = shared((step, i))
                    act.wait_ge(win_ready, n + 1)
                    nc.scalar.copy(trn3, o[:, 0:C].rearrange("p (k n) -> p k n", k=KC)).then_inc(win_read, 1)
                    act.wait_ge(win_read, n + 1)
                    act.sem_inc(loT_kept, 1)
            act.wait_ge(win_read, len(SHARED))
            act.sem_inc(tok_end_act, 1)

            keep_weights(act, nc.scalar.copy, 0, 0, N_FFN, wt_kept_act, (6, 7))
            for n in range(0, 44, 2):
                act.wait_ge(qkv_mm, n + 1)
                qkv_copy(nc.scalar.copy, n).then_inc(qkv_kept_act, 1)
            for t in range(NT + 1):
                if t < NT:
                    act.wait_ge(att_shift, t + 1)
                    nc.scalar.activation(att, att, ACT.Exp).then_inc(att_exp, 1)
                if t >= 1:
                    act.wait_ge(ctx_mm, t)
                    for g in (0, 2):
                        ctx_copy(nc.scalar.copy, act, ctx_kept_act, t - 1, g)
            for s in range(S):
                act.wait_ge(rln_var, s + 1)
                nc.scalar.activation(rs5, rc5, ACT.Sqrt).then_inc(rln_rstd, 1)
            for n in range(24):
                act.wait_ge(ff_mm, n + 1)
                dst = (up if n < 12 else gate)[:, (n % 12) * 320:(n % 12 + 1) * 320]
                nc.scalar.copy(dst, bank(n % 6, 320)).then_inc(ff_kept, 1)
            act.wait_ge(gate_q, 1)
            nc.scalar.activation(sig, gate, ACT.Sigmoid).then_inc(sig_ready, 1)
            keep_weights(act, nc.scalar.copy, 0, N_FFN, len(TURNS), wt_kept_act, (0, 1))
            for s in range(S):
                act.wait_ge(rln_var, S + s + 1)
                nc.scalar.activation(rs5, rc5, ACT.Sqrt).then_inc(rln_rstd, 1)
            for s in range(S):
                for hf, (at, width) in enumerate(((0, 512), (512, 256))):
                    act.wait_ge(l1_mm, 2 * s + hf + 1)
                    nc.scalar.copy(qkv[:, s, at:at + width], bank(2 + 2 * (s % 2) + hf, width)).then_inc(l1_kept, 1)
            act.wait_ge(l1_shift, 1)
            nc.scalar.activation(msc, msc, ACT.Exp).then_inc(l1_exp, 1)
            for s in range(S):
                act.wait_ge(rln_var, 2 * S + s + 1)
                nc.scalar.activation(rs5, rc5, ACT.Sqrt).then_inc(rln_rstd, 1)
            act.wait_ge(r_mm, 1)
            nc.scalar.activation(comb_w, bank(7, S * NE), ACT.Sigmoid).then_inc(r_sig, 1)
            g = 0
            for n, (kind, c, hf) in enumerate(MOE):
                if kind == "gate":
                    act.wait_ge(moe_mm, n + 1)
                    if g >= 2:
                        q = [m for m, x in enumerate(MOE) if x[0] == "up"][g - 2]
                        act.wait_ge(moe_hid, moe_count(q + 1, "up") + moe_count(q + 1, "comb"))
                    nc.scalar.activation(sil[g % 2], bank(n % 6, 320), ACT.Silu).then_inc(moe_sil, 1)
                    g += 1
            for s in range(S):
                act.wait_ge(rln_var, 3 * S + s + 1)
                nc.scalar.activation(rs5, rc5, ACT.Sqrt).then_inc(rln_rstd, 1)

        @block.vector
        def _(dve):
            chain = [0]

            def link(ins):
                chain[0] += 1
                ins.then_inc(dve_chain, 1)
                dve.wait_ge(dve_chain, chain[0])

            def moments(x, st, mv, rc, n=1):
                for k in range(n):
                    m = nc.vector.bn_stats(st[:, 6 * k:6 * k + 6], x[:, k * C:(k + 1) * C])
                link(m)
                for k in range(n):
                    m = nc.vector.bn_aggr(mv[:, 2 * k:2 * k + 2], st[:, 6 * k:6 * k + 6])
                link(m)
                v = mv.rearrange("p (k two) -> p k two", two=2)[:, :, 1]
                link(nc.vector.tensor_scalar(rc, v, EPS, None, ALU.add))
                return nc.vector.reciprocal(rc, rc)

            for j in range(1, NK, 2):
                dve.wait_ge(conv_turned, j + 1)
                nc.vector.tensor_copy(convT[0:CK, j, :], bank(j, C)[0:CK]).then_inc(conv_kept, 1)
            dve.wait_ge(vec_turned, 1)
            nc.vector.tensor_copy(vec[:, :], bank(5, 16)).then_inc(vec_kept, 1)
            dve.wait_ge(vec_kept, 1)

            def softmax_part1(s, n):
                link(nc.vector.tensor_reduce(mx8, s.rearrange("p k h -> p h k"), AX.X, ALU.max))
                nc.vector.tensor_tensor(s, s, mx8.unsqueeze(1).to_broadcast([P, n, LH]), ALU.subtract).then_inc(shifted, 1)

            def softmax_part2(s, n):
                link(nc.vector.tensor_reduce(sm8, s.rearrange("p k h -> p h k"), AX.X, ALU.add))
                link(nc.vector.reciprocal(rs8, sm8))
                return nc.vector.tensor_tensor(s, s, rs8.unsqueeze(1).to_broadcast([P, n, LH]), ALU.mult)

            for step, i in TOK:
                if step == "turn" and i % 2 == 1:
                    dve.wait_ge(turned, i + 1)
                    if i >= XT:
                        dve.wait_ge(conv_done, (4 * (i - XT) + 3) // NK + 1)
                    nc.vector.tensor_copy(xT[i % XT][0:CK, :], bank(i % 2)[0:CK]).then_inc(turned_kept_dve, 1)
                elif step == "stat":
                    w, first = window_of(i * WS), (i * WS // GP) % WS == 0
                    dve.wait_ge(conv_kept_sb, WS * (i + 1))
                    emb = pes[i % 2]
                    moments(emb, st3, mv3, rc3, WS).then_inc(var_ready, 1)
                    v = emb.rearrange("p (k n) -> p n k", k=WS)
                    if first:
                        link(nc.vector.tensor_reduce(red[:, w, :], v, AX.X, ALU.add))
                    else:
                        link(nc.vector.tensor_reduce(tmp[:, :], v, AX.X, ALU.add))
                        link(nc.vector.tensor_tensor(red[:, w, :], red[:, w, :], tmp[:, :], ALU.add))
                    dve.wait_ge(rstd_ready, i + 1)
                    if i >= 2:
                        dve.wait_ge(z_turned, (WS * (i - 1) - 1) // 2 + 1)
                    for k in range(WS):
                        m = nc.vector.tensor_scalar(zgrp[i % 2][:, k * C:(k + 1) * C], emb[:, k * C:(k + 1) * C],
                                                    mv3[:, 2 * k:2 * k + 1], rs3[:, k:k + 1], ALU.subtract, ALU.mult)
                    m.then_inc(z_ready, 1)
                    dve.wait_ge(z_ready, i + 1)
                elif step == "zturn":
                    dve.wait_ge(z_turned, i + 1)
                    for x in range(2):
                        old = 2 * i + x - ZSLOTS
                        if old >= 0:
                            dve.wait_ge(v_ready, window_of(old) * KVN + pos_of(old) // 2 + 1)
                    slots = [(2 * i + x) % ZSLOTS for x in range(2)]
                    for k in range(KC):
                        for x, n in ((0, 2),) if slots[1] == slots[0] + 1 else ((0, 1), (1, 1)):
                            m = nc.vector.tensor_scalar(zT[:, slots[x]:slots[x] + n, k, :],
                                                        bank(4, n * P, (k * 2 + x) * P).rearrange("p (t n) -> p t n", n=P),
                                                        vec[:, 4 + k:5 + k], vec[:, 6 + k:7 + k], ALU.mult, ALU.add)
                    m.then_inc(z_kept, 1)
                elif step in ("cls", "red", "loz"):
                    n = LN[(step, i)]
                    if step == "cls":
                        dve.wait_ge(ld_cls, 32)
                        x = cls[:, :]
                    elif step == "red":
                        link(nc.vector.tensor_scalar(red[:, i, :], red[:, i, :], 1.0 / NPOS, None, ALU.mult))
                        x = red[:, i, :]
                    else:
                        x = lo[:, :]
                    moments(x, st1, mv1, rc1).then_inc(ln_var, 1)
                    dve.wait_ge(ln_rstd, n + 1)
                    if n >= 1:
                        dve.wait_ge(ln_kept, n)
                    nc.vector.tensor_scalar(lnz[:, :], x, mv1[:, 0:1], rs1[:, 0:1], ALU.subtract, ALU.mult).then_inc(ln_z, 1)
                    dve.wait_ge(ln_z, n + 1)
                elif step == "kv":
                    if i % KVN == 0 and i >= KVN:
                        dve.wait_ge(agg_ready, i // KVN)
                    dve.wait_ge(k_ready, i + 1)
                    at, n = i % KVN * 2 * C, min(2, NPOS - i % KVN * 2)
                    nc.vector.tensor_tensor(prod[:, at:at + n * C].rearrange("p (k n) -> p k n", n=C),
                                            bank(5, n * C).rearrange("p (k n) -> p k n", n=C),
                                            qwin[:, :].unsqueeze(1).to_broadcast([P, n, C]), ALU.mult).then_inc(k_read, 1)
                elif (step, i) in SHARED_NO and "d" in READERS[step]:
                    n, o = shared((step, i))
                    dve.wait_ge(win_ready, n + 1)
                    if step in LNT:
                        v = {"clsT": 8, "redT": 0, "lozT": 12}[step]
                        for k in range(KC):
                            m = nc.vector.tensor_scalar(trn[:, k, :], o[:, k * P:(k + 1) * P], vec[:, v + k:v + k + 1],
                                                        vec[:, v + 2 + k:v + 3 + k], ALU.mult, ALU.add)
                        m.then_inc(win_read, 1)
                        dve.wait_ge(win_read, n + 1)
                        dve.sem_inc(ln_kept, 1)
                    elif step == "gq":
                        nc.vector.tensor_scalar(gq[:, :], o[:, 0:C], C ** -0.5, None, ALU.mult).then_inc(win_read, 1)
                    elif step == "q":
                        if i >= 1:
                            dve.wait_ge(k_read, i * KVN)
                        nc.vector.tensor_scalar(qwin[:, :], o[:, 0:C], C ** -0.5, None, ALU.mult).then_inc(win_read, 1)
                        dve.wait_ge(win_read, n + 1)
                    elif step == "proj":
                        dve.wait_ge(ld_tokw, 16 * 9)
                        link(nc.vector.tensor_tensor(tmp[:, :], o[:, 0:C], red[:, i, :], ALU.add))
                        nc.vector.tensor_tensor(lo[:, :], tmp[:, :], proj_b[:, :], ALU.add).then_inc(lo_ready, 1)
                        dve.wait_ge(lo_ready, i + 1)
                        dve.sem_inc(win_read, 1)
                    elif step == "mod":
                        nc.vector.tensor_tensor(H[0][:, i * C:(i + 1) * C], o[:, 0:C], mod_b[:, :], ALU.add).then_inc(win_read, 1)
                    elif step == "gkv":
                        link(nc.vector.tensor_tensor(tmp[:, :], o[:, 0:C], gq[:, :], ALU.mult))
                        link(nc.vector.tensor_reduce(gs[:, i * LH:(i + 1) * LH], tmp[:, :].rearrange("p (h d) -> p h d", d=LD),
                                                     AX.X, ALU.add))
                        nc.vector.tensor_copy(gv[:, i * C:(i + 1) * C], o[:, C:2 * C]).then_inc(win_read, 1)
                    elif step == "gaggT":
                        nc.vector.tensor_copy(trn2, o[:, 0:C].rearrange("p (k n) -> p k n", k=KC)).then_inc(win_read, 1)
                        dve.wait_ge(win_read, n + 1)
                        dve.sem_inc(aggT_kept, 1)
                    elif step == "gproj":
                        link(nc.vector.tensor_tensor(tmp[:, :], o[:, 0:C], cls[:, :], ALU.add))
                        nc.vector.tensor_tensor(H[0][:, NW * C:S * C], tmp[:, :], gproj_b[:, :], ALU.add).then_inc(win_read, 1)
                elif step == "soft":
                    dve.wait_ge(k_read, (i + 1) * KVN)
                    if i >= 1:
                        dve.wait_ge(pv_done, i)
                    s = sc.rearrange("p (k h) -> p k h", h=LH)
                    link(nc.vector.tensor_reduce(sc, prod.rearrange("p (kh d) -> p kh d", d=LD), AX.X, ALU.add))
                    softmax_part1(s, NPOS)
                    dve.wait_ge(exp_done, SM[(step, i)] + 1)
                    softmax_part2(s, NPOS).then_inc(probs_ready, 1)
                elif step == "pv":
                    dve.wait_ge(pv_done, i + 1)
                    if i >= 1:
                        dve.wait_ge(aggT_kept, i)
                    nc.vector.tensor_reduce(agg[:, :], prod.rearrange("p (k n) -> p n k", k=NPOS), AX.X, ALU.add).then_inc(agg_ready, 1)
                elif step == "gsoft":
                    s = gs.rearrange("p (k h) -> p k h", h=LH)
                    softmax_part1(s, NW)
                    dve.wait_ge(exp_done, SM[(step, i)] + 1)
                    link(softmax_part2(s, NW))
                    dve.wait_ge(win_read, SHARED_NO[("gkv", NW - 1)] + 1)
                    g4 = gv[:, :].rearrange("p (kh d) -> p kh d", d=LD)
                    link(nc.vector.tensor_tensor(g4, g4, gs.unsqueeze(2).to_broadcast([P, NW * LH, LD]), ALU.mult))
                    nc.vector.tensor_reduce(agg[:, :], gv[:, :].rearrange("p (k n) -> p n k", k=NW), AX.X, ALU.add).then_inc(agg_ready, 1)
                if (step, i) == ("conv", 31):
                    dve.wait_ge(ld_ffn, 48)
                    link(nc.vector.tensor_reduce(ffn_abs, ffn_nat[:, :].rearrange("p (b n) -> p b n", n=QB), AX.X, ALU.max,
                                                 apply_absolute_value=True))
                    link(nc.vector.tensor_scalar(ffn_abs, ffn_abs, 1.0 / 7.0, 1e-12, ALU.mult, ALU.max))
                    nc.vector.reciprocal(ffn_inv, ffn_abs).then_inc(ffn_scale, 1)
            dve.wait_ge(win_read, len(SHARED))
            dve.sem_inc(tok_end_dve, 1)

            dve.wait_ge(hT_zero, 1)
            hv = hT.rearrange("p k (g x) -> p k g x", x=32)
            for s in range(S):
                dve.wait_ge(hT_turned, s + 1)
                for k in range(KC):
                    dst = hv[:, k, 0:FULLG, 0:30].rearrange("p g (i s) -> p g i s", s=S)[:, :, :, s]
                    m = nc.vector.tensor_copy(dst, bank(s % 2, P, k * P)[:, 0:FULLG * GI].rearrange("p (g i) -> p g i", i=GI))
                nc.vector.tensor_copy(hv[:, :, FULLG, s:s + S + 1:S],
                                      bank(s % 2, C).rearrange("p (k n) -> p k n", k=KC)[:, :, FULLG * GI:P]).then_inc(hT_kept, 1)
            dve.wait_ge(bias_mm, 1)
            nc.vector.tensor_copy(bias.rearrange("p (a c j) -> p a c j", a=2, j=S),
                                  bank(2, S * NH).rearrange("p (j c a) -> p a c j", j=S, a=2)).then_inc(bias_ready, 1)
            keep_weights(dve, nc.vector.tensor_copy, 1, 0, N_FFN, wt_kept_dve, (6, 7))
            for n in range(1, 44, 2):
                dve.wait_ge(qkv_mm, n + 1)
                qkv_copy(nc.vector.tensor_copy, n).then_inc(qkv_kept_dve, 1)
            dve.wait_ge(bias_ready, 1)
            dve.wait_ge(ld_small, 16 * 6)
            dve.wait_ge(pexp_zero, 2)
            a3 = att.rearrange("p (h j) -> p h j", j=S)

            def att_soft(t):
                dve.wait_ge(score_mm, t + 1)
                for par in range(2):
                    o = smask[:, par * 240:(par + 1) * 240].rearrange("p (h i j) -> p h i j", i=GI, j=S)
                    s = bank(6 * (t % 2) + par, 256).rearrange("p (h x) -> p h x", x=32)[:, :, 0:30]
                    m = nc.vector.tensor_tensor(o, s.rearrange("p h (i j) -> p h i j", j=S),
                                                own[:, :].unsqueeze(1).unsqueeze(3).to_broadcast([P, 8, GI, S]), ALU.mult)
                m.then_inc(score_read, 1)
                dve.wait_ge(score_read, t + 1)
                link(nc.vector.tensor_reduce(a3, smask.rearrange("p (h i j) -> p h j i", i=GI, j=S), AX.X, ALU.add))
                link(nc.vector.tensor_tensor(att, att, bias, ALU.add))
                link(nc.vector.tensor_reduce(att_mx, a3, AX.X, ALU.max))
                nc.vector.tensor_tensor(a3, a3, att_mx.unsqueeze(2).to_broadcast([P, NH, S]), ALU.subtract).then_inc(att_shift, 1)
                dve.wait_ge(att_exp, t + 1)
                link(nc.vector.tensor_reduce(att_sm, a3, AX.X, ALU.add))
                link(nc.vector.reciprocal(att_sm, att_sm))
                link(nc.vector.tensor_tensor(a3, a3, att_sm.unsqueeze(2).to_broadcast([P, NH, S]), ALU.mult))
                o = pexp[t % 2].rearrange("p (h x) -> p h x", x=32)[:, :, 0:30].rearrange("p h (i j) -> p h i j", j=S)
                link(nc.vector.tensor_tensor(o, a3.unsqueeze(2).to_broadcast([P, NH, GI, S]),
                                             own[:, :].unsqueeze(1).unsqueeze(3).to_broadcast([P, NH, GI, S]), ALU.mult))
                if t >= 2:
                    dve.wait_ge(ctx_mm, t - 1)
                nc.vector.transpose(pT[t % 2], pexp[t % 2]).then_inc(pT_ready, 1)
                dve.wait_ge(pT_ready, t + 1)

            for t in range(NT + 1):
                if t < NT:
                    att_soft(t)
                if t >= 1:
                    dve.wait_ge(ctx_mm, t)
                    for g in (1, 3):
                        ctx_copy(nc.vector.tensor_copy, dve, ctx_kept_dve, t - 1, g)

            def res_ln(n, x, dst):
                moments(x, st5, mv5, rc5).then_inc(rln_var, 1)
                dve.wait_ge(rln_rstd, n + 1)
                nc.vector.tensor_scalar(dst, x, mv5[:, 0:1], rs5[:, 0:1], ALU.subtract, ALU.mult).then_inc(h_ready, 1)
                dve.wait_ge(h_ready, n + 1)

            def tok(h, s):
                return h[:, s * C:(s + 1) * C]

            for s in range(S):
                dve.wait_ge(wo_mm, s + 1)
                nc.vector.tensor_tensor(tok(H[1], s), bank(6 + s % 2, C), tok(H[0], s), ALU.add).then_inc(wo_read, 1)
                dve.wait_ge(wo_read, s + 1)
                res_ln(s, tok(H[1], s), tok(H[1], s))

            def global_max(i):
                dve.wait_ge(gmax_row, i + 1)
                nc.vector.tensor_reduce(gm[0:1, :], bank(6)[0:1, 0:P], AX.X, ALU.max).then_inc(gmax_one, 1)
                dve.wait_ge(gmax_all, i + 1)
                link(nc.vector.tensor_scalar(qsc[:, i:i + 1], bank(7, 1), 1.0 / 32767.0, 1e-12, ALU.mult, ALU.max))
                link(nc.vector.reciprocal(qinv[:, i:i + 1], qsc[:, i:i + 1]))

            def qdq(dst, src, i):
                link(nc.vector.tensor_scalar(src, src, qinv[:, i:i + 1], MAGIC, ALU.mult, ALU.add))
                return nc.vector.tensor_scalar(dst, src, MAGIC, qsc[:, i:i + 1], ALU.subtract, ALU.mult)

            nc.vector.tensor_reduce(gm, H[1][:, :], AX.X, ALU.max, apply_absolute_value=True).then_inc(gmax_part, 1)
            global_max(0)
            link(nc.vector.tensor_scalar(h1q, H[1][:, :], qinv[:, 0:1], MAGIC, ALU.mult, ALU.add))
            nc.vector.tensor_scalar(h1q, h1q, MAGIC, qsc[:, 0:1], ALU.subtract, ALU.mult).then_inc(hq_ready, 1)

            def keep_tokens(dst, stage):
                for s in range(S):
                    dve.wait_ge(hT2_turned, stage * S + s + 1)
                    nc.vector.tensor_copy(dst[:, :, s * P:(s + 1) * P],
                                          bank(s % 2, C).rearrange("p (k n) -> p k n", k=KC)).then_inc(hT2_kept, 1)

            keep_tokens(h1T, 0)
            for n in range(24):
                dve.wait_ge(ff_kept, n + 1)
                nc.vector.tensor_reduce(pmax[:, n % 12:n % 12 + 1], (up, gate)[n // 12][:, n % 12 * 320:(n % 12 + 1) * 320], AX.X, ALU.max,
                                        apply_absolute_value=True).then_inc(ff_max, 1)
                if n % 12 == 11:
                    dve.wait_ge(ff_max, n + 1)
                    nc.vector.tensor_reduce(gm, pmax, AX.X, ALU.max).then_inc(gmax_part, 1)
                    global_max(1 + n // 12)
            dve.wait_ge(ff_kept, 24)
            qdq(gate, gate, 2).then_inc(gate_q, 1)
            link(qdq(up, up, 1))
            keep_weights(dve, nc.vector.tensor_copy, 1, N_FFN, len(TURNS), wt_kept_dve, (0, 1))
            dve.wait_ge(sig_ready, 1)
            link(nc.vector.tensor_scalar(sig, sig, 65536.0, MAGIC, ALU.mult, ALU.add))
            link(nc.vector.tensor_scalar(sig, sig, MAGIC, 65535.0, ALU.subtract, ALU.min))
            link(nc.vector.scalar_tensor_tensor(out=sig, in0=sig, scalar=1.0 / 65536.0, in1=gate, op0=ALU.mult, op1=ALU.mult))
            nc.vector.tensor_reduce(gm, sig, AX.X, ALU.max, apply_absolute_value=True).then_inc(gmax_part, 1)
            global_max(3)
            link(qdq(sig, sig, 3))
            link(nc.vector.tensor_tensor(sig, sig, up, ALU.mult))
            nc.vector.tensor_reduce(gm, sig, AX.X, ALU.max, apply_absolute_value=True).then_inc(gmax_part, 1)
            global_max(4)
            qdq(sig, sig, 4).then_inc(o_ready, 1)
            for s in range(S):
                dve.wait_ge(down_mm, s + 1)
                nc.vector.tensor_tensor(tok(H[0], s), bank(2 + s % 2, C), tok(H[1], s), ALU.add).then_inc(down_read, 1)
                dve.wait_ge(down_read, s + 1)
                res_ln(S + s, tok(H[0], s), tok(H[0], s))

            link(nc.vector.memset(msc, 0.0))
            keep_tokens(h2T, 1)
            dve.wait_ge(l1_kept, 2 * S)
            for q in range(S):
                for k in range(q + 1):
                    m = nc.vector.tensor_tensor_reduce(out=scr, in0=qkv[:, q, 0:C], in1=qkv[:, k, C:2 * C], scale=C ** -0.5,
                                                       scalar=0.0, op0=ALU.mult, op1=ALU.add,
                                                       accum_out=msc[:, q * S + k:q * S + k + 1])
                    link(m)
            m3 = msc.rearrange("p (q k) -> p q k", k=S)
            zero = comb_w[:, 0:S * S]
            link(nc.vector.tensor_scalar(zero, msc, 0.0, -BIG, ALU.is_equal, ALU.mult))
            link(nc.vector.tensor_tensor(msc, msc, zero, ALU.add))
            link(nc.vector.tensor_reduce(mmx, m3, AX.X, ALU.max))
            nc.vector.tensor_tensor(m3, m3, mmx.unsqueeze(2).to_broadcast([P, S, S]), ALU.subtract).then_inc(l1_shift, 1)
            dve.wait_ge(l1_exp, 1)
            link(nc.vector.tensor_reduce(msm, m3, AX.X, ALU.add))
            link(nc.vector.reciprocal(msm, msm))
            link(nc.vector.tensor_tensor(m3, m3, msm.unsqueeze(2).to_broadcast([P, S, S]), ALU.mult))
            for k in range(S):
                for q in range(k, S):
                    prev = tok(H[0], q) if k == 0 else tok(H[1], q)
                    m = nc.vector.scalar_tensor_tensor(out=tok(H[1], q), in0=qkv[:, k, 2 * C:3 * C],
                                                       scalar=msc[:, q * S + k:q * S + k + 1], in1=prev,
                                                       op0=ALU.mult, op1=ALU.add)
                link(m)
            for s in range(S):
                res_ln(2 * S + s, tok(H[1], s), tok(H[1], s))

            keep_tokens(h3T, 2)
            dve.wait_ge(r_sig, 1)
            route(dve, link)
            hcount = 0
            g = 0
            for n, (kind, c, hf) in enumerate(MOE):
                o = hid[:, c, hf * 320:(hf + 1) * 320]
                if n == 16:
                    dve.wait_ge(combT_mm, 1)
                    link(nc.vector.tensor_copy(combT[0:NE, 0:512], bank(6)[0:NE, :]))
                    nc.vector.tensor_copy(combT[0:NE, 512:640], bank(7)[0:NE, 0:P]).then_inc(combT_kept, 1)
                if kind == "up":
                    dve.wait_ge(moe_mm, n + 1)
                    dve.wait_ge(moe_sil, g + 1)
                    nc.vector.tensor_tensor(o, bank(n % 6, 320), sil[g % 2], ALU.mult).then_inc(moe_hid, 1)
                    g += 1
                    hcount += 1
                elif kind == "comb":
                    dve.wait_ge(moe_mm, n + 1)
                    dve.wait_ge(moe_hid, hcount)
                    nc.vector.tensor_tensor(o, bank(n % 6, 320), o, ALU.mult).then_inc(moe_hid, 1)
                    hcount += 1
            for s in range(S):
                dve.wait_ge(down_mm, S + s + 1)
                nc.vector.tensor_tensor(tok(H[0], s), bank(s % 2, C), tok(H[1], s), ALU.add).then_inc(down_read, 1)
                dve.wait_ge(down_read, S + s + 1)
                res_ln(3 * S + s, tok(H[0], s), tok(H[0], s))


def constants():
    p = np.arange(P)
    slot = p % 32
    own = ((slot[:, None] // S == np.arange(GI)[None]) & (slot[:, None] < GI * S)).astype(np.float32)
    onehot = np.zeros((32, S, P), np.float32)
    for j in range(S):
        n = slot % S - j
        bucket = np.where(n < 0, 16, 0) + np.abs(n)
        onehot[bucket, j, p] = 1.0
    lower = np.tril(np.ones((NE, NE), np.float32), -1)
    pick = np.zeros((NE, NE // 2, P), np.float32)
    for e in range(NE):
        pick[e, e // 2, (e % 2) * EH:(e % 2 + 1) * EH] = 1.0
    return {"c_ident": np.eye(P, dtype=np.float32), "c_own": own, "c_onehot": onehot.reshape(32, S * P),
            "c_ties": lower, "c_ties4": lower[0:4, 0:4].copy(), "c_pick": pick.reshape(NE, NE // 2 * P)}


_UNUSED = ("L0_tok_pixel_masks",)


def kernel(**inputs):
    import concourse.bacc as _bacc
    from concourse.bass_utils import run_bass_kernel_spmd as _run

    nc = _bacc.Bacc("TRN2", target_bir_lowering=False, num_devices=1)
    arrays, args = {}, {}
    for name, value in list(inputs.items()) + list(constants().items()):
        if name in _UNUSED:
            continue
        v = np.ascontiguousarray(value)
        arrays[f"in_{name}_dram"] = v
        args[name] = nc.dram_tensor(f"in_{name}_dram", v.shape, mybir.dt.from_np(v.dtype), kind="ExternalInput").ap()
    out = nc.dram_tensor("out_0_dram", (P, S, C), F32, kind="ExternalOutput").ap()
    bass_vit_tower(nc, args, out)
    r = _run(nc, [arrays], core_ids=[0])
    return r.results[0]["out_0_dram"]
```

```python
from contextlib import ExitStack

import numpy as np

import concourse.bass as bass
from concourse import mybir

F32 = mybir.dt.float32
ALU = mybir.AluOpType
ACT = mybir.ActivationFunctionType
AX = mybir.AxisListType

P = 128
C = 256
KC = C // P
IMG, CH, PS = 96, 3, 14
GP = IMG // PS
NP_ = GP * GP
WS = 3
NW = (GP // WS) ** 2
NPOS = WS * WS
S = NW + 1
LH, LD = 8, 32
NH, DK = 16, 64
INNER = NH * DK
FF = 768
QB, NB = 32, 48
NE, EH, SH = 16, 64, 512
GI = 6
NG = 24
NT = 6
SLOTS = NG * 32
FULLG = P // GI
RESTI = P - FULLG * GI
EPS = 1e-5
MAGIC = 1.5 * 2.0 ** 23
BIG = 1e30
RW = 35200
XROWS = 3

PIX = CH * PS * PS
NK = -(-PIX // P)
CK = -(-PIX // NK)
PIXP = NK * CK
NBATCH = NP_ * NK // 4
XT = 4
ZSLOTS = 2 * NPOS


KVN = -(-NPOS // 2)

def group_place(g):
    w = g // WS
    return w // (GP // WS) * WS + g % WS, w % (GP // WS) * WS


def last_batch(t):
    return (t * NK + NK - 1) // 4


def patches_of(i):
    first = i // KVN * NPOS + i % KVN * 2
    return range(first, min(first + 2, (i // KVN + 1) * NPOS))


def pair_of(t):
    return t // NPOS * KVN + t % NPOS // 2


def tok_schedule():
    at = [(-1.0, "cls", 0), (-0.99, "cls root", 0), (-0.98, "cls z", 0), (0.05, "clsT", 0), (0.5, "gq", 0)]
    batch = 0
    for t in range(NP_):
        if t == 0:
            at.append((-0.9, "pack", 0))
        if t % WS == 0 and t // WS + 1 < NP_ // WS:
            at.append((t + 0.0, "pack", t // WS + 1))
        while batch <= last_batch(min(t + 1, NP_ - 1)):
            at.append((t + 0.1, "turn", batch))
            batch += 1
        at.append((t + 0.3, "conv", t))
        if t % WS == WS - 1:
            at += [(t + 0.6, "stat", t // WS), (t + 0.6 + 0.55, "stat root", t // WS), (t + 0.6 + 0.6, "stat z", t // WS)]
    turned = []
    for i in range(NW * KVN):
        t = patches_of(i)[-1] // WS * WS + WS - 1 + 2 + 0.7
        turned.append(max(t, turned[-1] + 1) if turned else t)
        at.append((turned[i], "zturn", i))
    for w in range(NW):
        end = (w + 1) * NPOS
        red = end - 0.4 + 1.0
        at += [(red, "red", w), (red + 0.25, "red root", w), (red + 0.3, "red z", w),
               (end + 1.2, "redT", w), (end + 1.5, "q", w)]
        for m in range(KVN):
            kv = turned[w * KVN + m] + 0.7
            at.append((kv, "kv", w * KVN + m))
        agg = kv + 2.6
        at += [(kv + 0.3, "qk", w), (kv + 0.9, "soft", w), (kv + 1.2, "soft exp", w), (kv + 1.25, "soft norm", w),
               (kv + 1.26, "pv", w), (agg, "agg", w), (agg + 0.4, "aggT", w), (agg + 1.1, "proj", w),
               (agg + 1.15, "loz", w), (agg + 1.4, "loz root", w), (agg + 1.42, "loz z", w), (agg + 1.44, "loT", w),
               (agg + 2.1, "lozT", w), (agg + 2.4, "mod", w), (agg + 3.1, "gkv", w)]
    at += [(agg + 4, "gsoft", 0), (agg + 4.1, "gsoft exp", 0), (agg + 4.2, "gsoft norm", 0), (agg + 5, "gaggT", 0), (agg + 6, "gproj", 0)]
    for m in range(3):
        at += [(21.9 + 3 * m, "quant", m), (21.9 + 2 + 3 * m, "round", m)]
    for b in range(FFN_BATCHES):
        at.append((kv + 0.1 if b < 2 else kv + 1.36 if b < 7 else agg + 1.6, "turnw", b))
    at.sort(key=lambda e: e[0])
    return [(name, i) for _, name, i in at]


FFN_BATCHES = 3 * NB * QB // (4 * P)
PV_POOL = [NPOS] * (NW - 1) + [3]


def DVE_TURNS(batch):
    return batch % 2 == 1


TOK = tok_schedule()
READERS = {"clsT": "d", "gq": "d", "redT": "d", "q": "d", "aggT": "a", "proj": "d", "loT": "a",
           "mod": "d", "lozT": "d", "gkv": "d", "gaggT": "d", "gproj": "d"}
SHARED = [s for s in TOK if s[0] in READERS]
SHARED_NO = {s: n for n, s in enumerate(SHARED)}


def bass_vit_tower(nc, a, out):
    with ExitStack() as ctx:
        def sb(name, cols):
            return ctx.enter_context(nc.sbuf_tensor(name, [P, cols], F32))

        names = {}

        def sem(name):
            names[name] = ctx.enter_context(nc.semaphore(name))
            return names[name]

        ident = sb("ident", P)
        own = sb("own", GI)
        ties = sb("ties", NE * NE)
        ties4 = sb("ties4", 16)
        ones = sb("ones", P)
        H = [sb("HA", S * C), sb("HB", S * C)]
        vec_rows = sb("vec_rows", P)
        vec = sb("vec", 16)
        proj_b = sb("proj_b", C)
        gproj_b = sb("gproj_b", C)
        mod_b = sb("mod_b", C)
        cls = sb("cls_row", C)
        corr = sb("corr", NE)
        relb = sb("relb", NE)
        small = sb("small", 880)
        small_at = [0]

        def tiny(n):
            at = small_at[0]
            small_at[0] += n
            assert small_at[0] <= 880
            return small[:, at:at + n]

        wattn = sb("wattn", 4 * 2048)
        ffn_nat = sb("ffn_nat", 3 * NB * QB)
        R = sb("R", RW)

        def area(start):
            at = [start]

            def take(n):
                v = R[:, at[0]:at[0] + n]
                at[0] += n
                assert at[0] <= RW, at[0]
                return v
            return take

        take = area(0)
        xring = [take(CH * PS * IMG), take(CH * PS * IMG), wattn[:, 0:CH * PS * IMG]]
        xring = [v.rearrange("p (c r x) -> p c r x", c=CH, r=PS) for v in xring]
        xpack = [take(WS * PIXP) for _ in range(2)]
        zT = take(ZSLOTS * C).rearrange("p (t k n) -> p t k n", t=ZSLOTS, k=KC)
        xT = [take(4 * P) for _ in range(XT)]
        pes = [take(WS * C) for _ in range(2)]
        convT = take(NK * C).rearrange("p (k n) -> p k n", k=NK)
        kwin = take(NPOS * C)
        prod = take(NPOS * C)
        vwin = take(NPOS * C)
        def tok_weight(at, n):
            return wattn[:, 4096 + at:4096 + at + KC * n].rearrange("p (k n) -> p k n", k=KC)

        g_wq, t_wq, t_proj, g_proj = (tok_weight(i * KC * C, C) for i in range(4))
        t_wkv, g_wkv = tok_weight(4 * KC * C, 2 * C), tok_weight(6 * KC * C, 2 * C)
        t_mod = take(KC * C).rearrange("p (k n) -> p k n", k=KC)
        conv_nat = zT.rearrange("p t k n -> p (t k n)")[:, (ZSLOTS - 1) * C - KC * PIXP:(ZSLOTS - 1) * C].rearrange("p (k n) -> p k n", k=KC)
        zgrp = [take(WS * C) for _ in range(2)]
        red = take(NW * C).rearrange("p (w n) -> p w n", w=NW)
        tmp = take(C)
        lnz = take(C)
        trn = take(C).rearrange("p (k n) -> p k n", k=KC)
        trn2 = take(C).rearrange("p (k n) -> p k n", k=KC)
        trn3 = take(C).rearrange("p (k n) -> p k n", k=KC)
        qwin = take(C)
        agg = take(C)
        lo = take(C)
        gq = take(C)
        gv = take(NW * C)

        psum = ctx.enter_context(nc.psum_tensor("psum", [P, 8 * 512], F32))

        def bank(b, n=512, at=0):
            return psum[:, b * 512 + at:b * 512 + at + n]

        st3, mv3, rs3 = tiny(WS * 6), tiny(WS * 2), tiny(WS)
        rc3 = tiny(WS)
        st1, mv1, rc1, rs1 = tiny(6), tiny(2), tiny(1), tiny(1)
        sc = tiny(NPOS * LH)
        mx8, sm8, rs8 = tiny(LH), tiny(LH), tiny(LH)
        gs = tiny(NW * LH)
        eps_unused = tiny(1)

        ld_conv, ld_ident, ld_vec = sem("ld_conv"), sem("ld_ident"), sem("ld_vec")
        ld_x = [sem(f"ld_x{i}") for i in range(XROWS)]
        ld_cls, ld_tokw, ld_small, ld_attnw, ld_ffn = sem("ld_cls"), sem("ld_tokw"), sem("ld_small"), sem("ld_attnw"), sem("ld_ffn")
        dve_chain, act_chain = sem("dve_chain"), sem("act_chain")
        ones_set = sem("ones_set")
        conv_turned, conv_kept = sem("conv_turned"), sem("conv_kept")
        vec_turned, vec_kept = sem("vec_turned"), sem("vec_kept")
        pads_zero = sem("pads_zero")
        turned, turned_kept_act, turned_kept_dve = sem("turned"), sem("turned_kept_act"), sem("turned_kept_dve")
        packed = sem("packed")
        conv_done, conv_kept_sb = sem("conv_done"), sem("conv_kept_sb")
        var_ready, rstd_ready = sem("var_ready"), sem("rstd_ready")
        z_ready, z_turned, z_kept = sem("z_ready"), sem("z_turned"), sem("z_kept")
        win_ready, win_read = sem("win_ready"), sem("win_read")
        k_ready, k_read, v_ready, v_read = sem("k_ready"), sem("k_read"), sem("v_ready"), sem("v_read")
        ln_var, ln_rstd, ln_z, ln_kept = sem("ln_var"), sem("ln_rstd"), sem("ln_z"), sem("ln_kept")
        shifted, exp_done, probs_ready = sem("shifted"), sem("exp_done"), sem("probs_ready")
        qk_done, pv_done, agg_ready = sem("qk_done"), sem("pv_done"), sem("agg_ready")
        aggT_kept, lo_ready, loT_kept = sem("aggT_kept"), sem("lo_ready"), sem("loT_kept")
        tok_tail = sem("tok_tail")

        block = ctx.enter_context(nc.Block())

        LN = {s: n for n, s in enumerate(s for s in TOK if s[0] in ("cls", "red", "loz"))}
        LNT = {"clsT": "cls", "redT": "red", "lozT": "loz"}
        SM = {s: n for n, s in enumerate(s for s in TOK if s[0] in ("soft", "gsoft"))}
        AGG = {s: n for n, s in enumerate(s for s in TOK if s[0] in ("agg", "gsoft"))}
        AGGT = {s: n for n, s in enumerate(s for s in TOK if s[0] in ("aggT", "gaggT"))}

        def shared(step):
            return SHARED_NO[step], bank(7)

        def pixels(chunk):
            t, j = chunk // NK, chunk % NK
            at = t % WS * PIXP + j * CK
            return xpack[t // WS % 2][:, at:at + CK]

        def kept_by(b):
            dve = sum(DVE_TURNS(i) for i in range(b))
            return b - dve, dve

        def batches_of_pixels_kept(eng, b):
            for done, n in zip((turned_kept_act, turned_kept_dve), kept_by(b)):
                if n:
                    eng.wait_ge(done, n)

        take = area(0)
        ffnT = take(3 * 12 * P)
        hT = take(KC * SLOTS).rearrange("p (k n) -> p k n", k=KC)
        qT = take(8 * SLOTS).rearrange("p (k n) -> p k n", k=8)
        kT = take(8 * SLOTS).rearrange("p (k n) -> p k n", k=8)
        V = take(NT * INNER).rearrange("p (t n) -> p t n", t=NT)
        ctx_area = take(8 * S * P)
        ctxT = ctx_area.rearrange("p (c s n) -> p c s n", c=8, s=S)
        onehot = ctx_area[:, 0:S * P]
        smask = take(2 * NH * 30)
        pexp = hT.rearrange("p k n -> p (k n)")[:, 0:2 * NH * 32]
        pT = [take(NH * P).rearrange("p (h x) -> p h x", h=NH) for _ in range(2)]
        bias = take(S * NH)
        att = take(2 * NH * S)
        att_mx, att_sm = take(2 * NH), take(2 * NH)
        w_q = wattn[:, 0:2048].rearrange("p (k n) -> p k n", k=KC)
        w_k = wattn[:, 2048:4096].rearrange("p (k n) -> p k n", k=KC)
        w_v = wattn[:, 4096:6144].rearrange("p (k n) -> p k n", k=KC)
        w_o = wattn[:, 6144:8192].rearrange("p (k n) -> p k n", k=8)
        upT = ffnT[:, 0:1536].rearrange("p (k n) -> p k n", k=KC)
        gateT = ffnT[:, 1536:3072].rearrange("p (k n) -> p k n", k=KC)
        downT = ffnT[:, 3072:4608].rearrange("p (k n) -> p k n", k=6)
        ffn_abs = tiny(3 * NB)
        ffn_inv = tiny(3 * NB)

        take = area(3 * 12 * P)
        h1T = take(KC * S * P).rearrange("p (k n) -> p k n", k=KC)
        h1q = take(S * C)
        up = take(6 * S * P)
        gate = take(6 * S * P)
        sig = take(6 * S * P)
        l1nat = take(3 * KC * C)
        shnat = take(3 * 4 * C)
        rnat = take(C)
        l1T = take(KC * 3 * C).rearrange("p (k n) -> p k n", k=KC)
        shT = take(2 * KC * SH).rearrange("p (a k n) -> p a k n", a=2, k=KC)
        rT = take(KC * NE).rearrange("p (k n) -> p k n", k=KC)
        e_gate = wattn[:, 0:2048].rearrange("p (k e n) -> p k e n", k=KC, e=NE)
        e_up = wattn[:, 2048:4096].rearrange("p (k e n) -> p k e n", k=KC, e=NE)
        e_down = wattn[:, 4096:6144].rearrange("p (k n) -> p k n", k=8)
        sdT = wattn[:, 6144:7168].rearrange("p (k n) -> p k n", k=4)
        pick = wattn[:, 7168:8192].rearrange("p (k n) -> p k n", k=8)
        take = area(3 * 12 * P)
        h2T = take(KC * S * P).rearrange("p (k n) -> p k n", k=KC)
        qkv = take(S * 3 * C).rearrange("p (s n) -> p s n", s=S)
        h3T = take(KC * S * P).rearrange("p (k n) -> p k n", k=KC)
        hid = take(12 * S * P).rearrange("p (k n) -> p k n", k=12)
        sil = [take(320) for _ in range(2)]
        cmp_a = take(S * NE * NE)
        cmp_b = take(S * NE * NE)
        combT = take(S * P)
        scr = hid.rearrange("p k n -> p (k n)")[:, 0:S * (S + 1) // 2 * C].rearrange("p (i n) -> p i n", n=C)
        assert KC * S * P * 2 + S * 3 * C + 12 * S * P + 640 + 2 * S * NE * NE + S * P <= (
            KC * S * P + S * C + 3 * 6 * S * P + 3 * KC * C + 3 * 4 * C + C)
        msc = tiny(S * S)
        mmx, msm = tiny(S), tiny(S)
        st5, mv5, rc5, rs5 = tiny(3 * 6), tiny(3 * 2), tiny(3), tiny(3)
        pmax, gm, qsc, qinv, fold = tiny(12), tiny(1), tiny(5), tiny(5), tiny(4)

        tok_end_act, tok_end_dve = sem("tok_end_act"), sem("tok_end_dve")
        hT_zero, hT_turned, hT_kept = sem("hT_zero"), sem("hT_turned"), sem("hT_kept")
        bias_mm, bias_ready = sem("bias_mm"), sem("bias_ready")
        qkv_mm, qkv_kept_act, qkv_kept_dve = sem("qkv_mm"), sem("qkv_kept_act"), sem("qkv_kept_dve")
        score_mm, score_read = sem("score_mm"), sem("score_read")
        att_shift, att_exp, pT_ready = sem("att_shift"), sem("att_exp"), sem("pT_ready")
        ctx_mm, ctx_kept_act, ctx_kept_dve = sem("ctx_mm"), sem("ctx_kept_act"), sem("ctx_kept_dve")
        wo_mm, wo_read = sem("wo_mm"), sem("wo_read")
        ffn_scale, ffn_over, ffn_rounded, ffn_quant = (sem("ffn_scale"), sem("ffn_over"), sem("ffn_rounded"),
                                                       sem("ffn_quant"))
        pexp_zero, pT_zero = sem("pexp_zero"), sem("pT_zero")
        wt_turned, wt_kept = sem("wt_turned"), sem("wt_kept")
        rln_var, rln_rstd, h_ready = sem("rln_var"), sem("rln_rstd"), sem("h_ready")
        ld_l1, ld_moe = sem("ld_l1"), sem("ld_moe")
        gmax_part, gmax_row, gmax_one, gmax_all = sem("gmax_part"), sem("gmax_row"), sem("gmax_one"), sem("gmax_all")
        hq_ready, hT2_turned, hT2_kept_act, hT2_kept_dve = (sem("hq_ready"), sem("hT2_turned"),
                                                             sem("hT2_kept_act"), sem("hT2_kept_dve"))
        ff_mm, ff_kept, ff_max = sem("ff_mm"), sem("ff_kept"), sem("ff_max")
        gate_q, sig_ready, o_ready = sem("gate_q"), sem("sig_ready"), sem("o_ready")
        tok_max = sem("tok_max")
        down_mm, down_read = sem("down_mm"), sem("down_read")
        l1_mm, l1_kept, l1_shift, l1_exp = sem("l1_mm"), sem("l1_kept"), sem("l1_shift"), sem("l1_exp")
        r_mm, r_sig, comb_ready, combT_mm, combT_kept = (sem("r_mm"), sem("r_sig"), sem("comb_ready"), sem("combT_mm"),
                                                         sem("combT_kept"))
        moe_mm, moe_sil, moe_hid = sem("moe_mm"), sem("moe_sil"), sem("moe_hid")
        stored = sem("stored")

        def ffn_matrix(m):
            return (ffn_nat[:, m * NB * QB:(m + 1) * NB * QB].rearrange("p (b n) -> p b n", n=QB),
                    slice(m * NB, (m + 1) * NB))

        def weigh_values(tensor_tensor, lo_, hi_):
            n = hi_ - lo_
            return tensor_tensor(prod[:, lo_ * C:hi_ * C].rearrange("p (kh d) -> p kh d", d=LD),
                                 vwin[:, lo_ * C:hi_ * C].rearrange("p (kh d) -> p kh d", d=LD),
                                 sc[:, lo_ * LH:hi_ * LH].unsqueeze(2).to_broadcast([P, n * LH, LD]), ALU.mult)

        def weight_batches():
            def blocks(src, at, width, o, k):
                return src[:, at + o * width + k * P:at + o * width + (k + 1) * P]

            batches = []
            def six(src, at, dst):
                for k in range(KC):
                    batches.append(([blocks(src, at, C, o, k) for o in range(4)], dst[:, k, 0:512]))
                batches.append(([blocks(src, at, C, o, k) for k in range(KC) for o in (4, 5)], dst[:, :, 512:768]))

            def pairs(src, at, width, dst):
                for k in range(0, width // P, 2):
                    batches.append(([blocks(src, at, width, o, kk) for kk in (k, k + 1) for o in range(KC)], dst[:, k:k + 2, :]))

            six(ffn_nat, 0, upT)
            six(ffn_nat, 1536, gateT)
            pairs(ffn_nat, 3072, FF, downT)
            assert len(batches) == FFN_BATCHES
            six(l1nat, 0, l1T)
            for m in range(2):
                for k in range(KC):
                    batches.append(([blocks(shnat, m * 1024, C, o, k) for o in range(4)], shT[:, m, k, :]))
            pairs(shnat, 2048, SH, sdT)
            batches.append(([rnat[0:NE, k * P:(k + 1) * P] for k in range(KC)], rT))
            return batches

        WB = weight_batches()

        def wb_bank(b):
            return (2 if b < FFN_BATCHES else 0) + b % 2

        def turn_batch(pe, b):
            if b >= 2:
                batches_kept(pe, b - 1)
            for i, src in enumerate(WB[b][0]):
                rows = src.shape[0]
                m = pe.transpose(bank(wb_bank(b), rows, i * rows), src, ident[0:rows, 0:rows])
            m.then_inc(wt_turned, 1)

        def keep_batch(eng, copy, b, done):
            eng.wait_ge(wt_turned, b + 1)
            dst = WB[b][1]
            v = bank(wb_bank(b), dst.shape[-1] * (dst.shape[1] if len(dst.shape) == 3 else 1))
            if len(dst.shape) == 3:
                v = v.rearrange("p (k n) -> p k n", k=dst.shape[1])
            copy(dst, v).then_inc(done, 1)

        def batches_kept(eng, n):
            eng.wait_ge(wt_kept, n)

        MOE = []
        for c in range(13):
            for hf in range(2):
                if c < 12:
                    MOE += [("gate", c, hf), ("up", c, hf)]
                if c >= 5:
                    MOE.append(("comb", c - 1, hf))
        FIRST_COMB = [m[0] for m in MOE].index("comb")

        def moe_count(n, kind):
            return sum(m[0] == kind for m in MOE[:n])

        comb_w = tiny(S * NE)

        def tokens_kept(eng, stage, n):
            eng.wait_ge(hT2_kept_dve, stage * 3 + (n + 1) // 2)
            if stage * 2 + n // 2:
                eng.wait_ge(hT2_kept_act, stage * 2 + n // 2)

        def keep_token(eng, copy, dst, stage, s, done):
            eng.wait_ge(hT2_turned, stage * S + s + 1)
            copy(dst[:, :, s * P:(s + 1) * P], bank(s % 2, C).rearrange("p (k n) -> p k n", k=KC)).then_inc(done, 1)

        def qkv_copy(copy, n):
            if n < 32:
                c, w, hf = n // 4, n // 2 % 2, n % 2
                return copy((qT, kT)[w][:, c, hf * 384:(hf + 1) * 384], bank(2 + n % 4, 384))
            t, hf = (n - 32) // 2, n % 2
            return copy(V[:, t, hf * 512:(hf + 1) * 512], bank(2 + n % 4))

        def score_bank(half):
            return psum[:, (0, 6)[half] * 512:(0, 6)[half] * 512 + 1024].rearrange("p (h x) -> p h x", x=P)

        def ctx_copy(copy, eng, done, t, half):
            eng.wait_ge(ctx_mm, 2 * t + half + 1)
            src = bank(2 + t % 2 * 2 + half).rearrange("p (c g x) -> p c g x", g=4, x=32)
            first = 4 * t * GI
            full = min(4, FULLG - 4 * t)
            for c in range(4):
                d = ctxT[:, half * 4 + c, :, :]
                m = copy(d[:, :, first:first + full * GI].rearrange("p s (g i) -> p g i s", i=GI),
                         src[:, c, 0:full, 0:GI * S].rearrange("p g (i s) -> p g i s", s=S))
            if full < 4:
                at = first + full * GI
                m = copy(ctxT[:, half * 4:half * 4 + 4, :, at:at + RESTI].rearrange("p c s i -> p c i s"),
                         src[:, :, full, 0:RESTI * S].rearrange("p c (i s) -> p c i s", s=S))
            m.then_inc(done, 1)

        sb_ = tiny(S * NE)
        pairs = cmp_b
        gsum, grank = tiny(S * 4), tiny(S * 4)
        rank, wsum = tiny(S * NE), tiny(S)

        def route(dve, link):
            s3 = comb_w.rearrange("p (s e) -> p s e", e=NE)
            b3 = sb_.rearrange("p (s e) -> p s e", e=NE)
            b4 = sb_.rearrange("p (g e) -> p g e", e=4)
            link(nc.vector.tensor_tensor(b3, s3, corr[:, :].unsqueeze(1).to_broadcast([P, S, NE]), ALU.add))
            pr = pairs[:, 0:S * 4 * 6].rearrange("p (g x) -> p g x", x=6)
            nc.vector.tensor_tensor(pr[:, :, 0:3], b4[:, :, 0:3], b4[:, :, 1:4], ALU.add)
            nc.vector.tensor_tensor(pr[:, :, 3:5], b4[:, :, 0:2], b4[:, :, 2:4], ALU.add)
            link(nc.vector.tensor_tensor(pr[:, :, 5:6], b4[:, :, 0:1], b4[:, :, 3:4], ALU.add))
            link(nc.vector.tensor_reduce(gsum, pr, AX.X, ALU.max))

            def ranks(v, n, tie, out_):
                x = v.rearrange("p (s e) -> p s e", e=n)
                for s in range(S):
                    ga = cmp_a[:, s * n * n:(s + 1) * n * n].rearrange("p (i j) -> p i j", j=n)
                    gb = cmp_b[:, s * n * n:(s + 1) * n * n].rearrange("p (i j) -> p i j", j=n)
                    other = x[:, s, :].unsqueeze(1).to_broadcast([P, n, n])
                    mine = x[:, s, :].unsqueeze(2).to_broadcast([P, n, n])
                    nc.vector.tensor_tensor(ga, other, mine, ALU.is_gt)
                    m = nc.vector.tensor_tensor(gb, other, mine, ALU.is_equal)
                link(m)
                gb = cmp_b[:, 0:S * n * n].rearrange("p (s x) -> p s x", s=S)
                link(nc.vector.tensor_tensor(gb, gb, tie[:, 0:n * n].unsqueeze(1).to_broadcast([P, S, n * n]), ALU.mult))
                ga = cmp_a[:, 0:S * n * n]
                link(nc.vector.tensor_tensor(ga, ga, cmp_b[:, 0:S * n * n], ALU.add))
                link(nc.vector.tensor_reduce(out_, ga.rearrange("p (i j) -> p i j", j=n), AX.X, ALU.add))

            ranks(gsum, 4, ties4, grank)
            link(nc.vector.tensor_scalar(grank, grank, 2.0, -BIG, ALU.is_ge, ALU.mult))
            link(nc.vector.tensor_tensor(b4, b4, grank.unsqueeze(2).to_broadcast([P, S * 4, 4]), ALU.add))
            ranks(sb_, NE, ties, rank)
            link(nc.vector.tensor_scalar(rank, rank, 4.0, None, ALU.is_lt))
            link(nc.vector.tensor_tensor(comb_w, comb_w, rank, ALU.mult))
            link(nc.vector.tensor_reduce(wsum, s3, AX.X, ALU.add))
            link(nc.vector.tensor_scalar(wsum, wsum, 1e-20, None, ALU.add))
            link(nc.vector.reciprocal(wsum, wsum))
            nc.vector.tensor_tensor(s3, s3, wsum.unsqueeze(2).to_broadcast([P, S, NE]), ALU.mult).then_inc(comb_ready, 1)

        @block.sync
        def _(sp):
            sp.dma_start(ident[:, :], a["c_ident"]).then_inc(ld_ident, 16)
            sp.dma_start(conv_nat[:, :, 0:PIX], a["L0_tok_conv_w"].rearrange("(k p) c r x -> p k (c r x)", p=P)).then_inc(ld_conv, 16)

            def row(r):
                x = a["x"][:, :, r * PS:(r + 1) * PS, :].rearrange("b c r x -> b c (r x)")
                sp.dma_start(xring[r % XROWS].rearrange("p c r x -> p c (r x)"), x).then_inc(ld_x[r % XROWS], 16)

            row(0)
            for i, n in enumerate(("la_ln_q_g", "la_ln_q_b", "la_ln_kv_g", "la_ln_kv_b", "ga_ln_q_g", "ga_ln_q_b",
                                   "ga_ln_kv_g", "ga_ln_kv_b")):
                sp.dma_start(vec_rows[2 * i:2 * i + 2, :], a["L0_tok_" + n].rearrange("(k p) -> k p", p=P)).then_inc(ld_vec, 16)
            sp.dma_start(cls[:, :], a["L0_tok_class_emb"].partition_broadcast(P)).then_inc(ld_cls, 16)
            sp.dma_start(g_wq, a["L0_tok_ga_wq"].rearrange("(k p) n -> p k n", p=P)).then_inc(ld_cls, 16)
            row(1)
            row(2)
            for t, n in ((proj_b, "la_proj_b"), (gproj_b, "ga_proj_b"), (mod_b, "mod_b")):
                sp.dma_start(t[:, :], a["L0_tok_" + n].partition_broadcast(P)).then_inc(ld_tokw, 16)
            for t, n in ((t_wq, "la_wq"), (t_wkv, "la_wkv"), (t_proj, "la_proj_w"), (g_wkv, "ga_wkv"),
                         (g_proj, "ga_proj_w"), (t_mod, "mod_w")):
                sp.dma_start(t, a["L0_tok_" + n].rearrange("(k p) n -> p k n", p=P)).then_inc(ld_tokw, 16)
            for r in range(XROWS, GP):
                sp.wait_ge(packed, WS + r - XROWS + 1)
                row(r)
            sp.dma_start(corr[:, :], a["L1_ffn_correction_bias"].partition_broadcast(P)).then_inc(ld_small, 16)
            sp.dma_start(relb[0:32, :], a["L0_attn_rel_emb"]).then_inc(ld_small, 16)
            sp.dma_start(own[:, :], a["c_own"]).then_inc(ld_small, 16)
            sp.dma_start(ties[:, :], a["c_ties"].rearrange("a n -> (a n)").partition_broadcast(P)).then_inc(ld_small, 16)
            sp.dma_start(ties4[:, :], a["c_ties4"].rearrange("a n -> (a n)").partition_broadcast(P)).then_inc(ld_small, 16)
            for i, n in enumerate(("w_up", "w_gate")):
                sp.dma_start(ffn_nat[:, i * 1536:(i + 1) * 1536].rearrange("p (k n) -> p k n", n=C),
                             a["L0_ffn_" + n].rearrange("(k p) n -> p k n", p=P)).then_inc(ld_ffn, 16)
            sp.dma_start(ffn_nat[:, 3072:4608].rearrange("p (k n) -> p k n", n=FF),
                         a["L0_ffn_w_down"].rearrange("(k p) n -> p k n", p=P)).then_inc(ld_ffn, 16)
            sp.wait_ge(packed, NP_ // WS)
            for t, n in ((w_q, "wq"), (w_k, "wk")):
                sp.dma_start(t, a["L0_attn_" + n].rearrange("(k p) n -> p k n", p=P)).then_inc(ld_attnw, 16)
            sp.wait_ge(tok_end_dve, 1)
            sp.wait_ge(tok_end_act, 1)
            sp.dma_start(onehot[0:32, :], a["c_onehot"]).then_inc(ld_small, 16)
            sp.dma_start(w_v, a["L0_attn_wv"].rearrange("(k p) n -> p k n", p=P)).then_inc(ld_attnw, 16)
            sp.dma_start(w_o, a["L0_attn_wo"].rearrange("(k p) n -> p k n", p=P)).then_inc(ld_attnw, 16)
            sp.wait_ge(ctx_mm, 2 * NT)
            sp.wait_ge(wo_mm, S)
            for i, n in enumerate(("WQ", "WK", "WV")):
                sp.dma_start(l1nat[:, i * 512:(i + 1) * 512].rearrange("p (k n) -> p k n", n=C),
                             a["L1_attn_" + n].rearrange("(k p) n -> p k n", p=P)).then_inc(ld_l1, 16)
            for i, n in enumerate(("gate", "up")):
                sp.dma_start(shnat[:, i * 1024:(i + 1) * 1024].rearrange("p (k n) -> p k n", n=C),
                             a[f"L1_ffn_shared_{n}_w"].rearrange("(k p) n -> p k n", p=P)).then_inc(ld_l1, 16)
            sp.dma_start(shnat[:, 2048:3072].rearrange("p (k n) -> p k n", n=SH),
                         a["L1_ffn_shared_down_w"].rearrange("(k p) n -> p k n", p=P)).then_inc(ld_l1, 16)
            sp.dma_start(rnat[0:NE, :], a["L1_ffn_router_w"]).then_inc(ld_l1, 16)
            for k in range(KC):
                for t, n in ((e_gate, "gate_w"), (e_up, "up_w")):
                    sp.dma_start(t[:, k], a["L1_ffn_" + n][:, k * P:(k + 1) * P, :].rearrange("e p n -> p e n")).then_inc(ld_moe, 16)
            sp.dma_start(e_down, a["L1_ffn_down_w"].rearrange("(k e) h n -> (e h) k n", e=2)).then_inc(ld_moe, 16)
            sp.dma_start(pick[0:NE], a["c_pick"].rearrange("e (k n) -> e k n", k=8)).then_inc(ld_moe, 16)
            for s in range(S):
                sp.wait_ge(h_ready, 3 * S + s + 1)
                sp.dma_start(out[:, s, :], H[0][:, s * C:(s + 1) * C]).then_inc(stored, 16)
            sp.wait_ge(stored, 16 * S)

        @block.gpsimd
        def _(pool):
            nc.gpsimd.memset(ones[:, :], 1.0).then_inc(ones_set, 1)
            for x in xpack:
                nc.gpsimd.memset(x.rearrange("p (t y) -> p t y", t=WS)[:, :, PIX:PIXP], 0.0).then_inc(pads_zero, 1)
            nc.gpsimd.memset(conv_nat[:, :, PIX:PIXP], 0.0).then_inc(pads_zero, 1)
            for step, i in TOK:
                if step == "pack":
                    row, col = group_place(i)
                    pool.wait_ge(ld_x[row % XROWS], 16 * (row // XROWS + 1))
                    if i >= 2:
                        pool.wait_ge(turned, last_batch(WS * (i - 1) - 1) + 1)
                    x = col * PS
                    src = xring[row % XROWS].rearrange("p c r x -> p (c r) x")[:, :, x:x + WS * PS]
                    dst = xpack[i % 2].rearrange("p (t y) -> p t y", t=WS)[:, :, 0:PIX]
                    nc.gpsimd.tensor_copy(dst.rearrange("p t (cr x) -> p t cr x", x=PS),
                                          src.rearrange("p cr (t x) -> p t cr x", x=PS)).then_inc(packed, 1)
                elif step == "quant":
                    pool.wait_ge(ffn_scale, i + 1)
                    w, scales = ffn_matrix(i)
                    nc.gpsimd.tensor_tensor(w, w, ffn_inv[:, scales].unsqueeze(2).to_broadcast([P, NB, QB]),
                                            ALU.mult).then_inc(ffn_over, 1)
                elif step == "round":
                    pool.wait_ge(ffn_rounded, i + 1)
                    w, scales = ffn_matrix(i)
                    nc.gpsimd.tensor_tensor(w, w, ffn_abs[:, scales].unsqueeze(2).to_broadcast([P, NB, QB]),
                                            ALU.mult).then_inc(ffn_quant, 1)
                elif step == "pv":
                    pool.wait_ge(probs_ready, SM[("soft", i)] + 1)
                    pool.wait_ge(v_read, (i + 1) * KVN)
                    if i >= 1:
                        pool.wait_ge(agg_ready, i)
                    weigh_values(nc.gpsimd.tensor_tensor, 0, PV_POOL[i]).then_inc(pv_done, 1)
            pool.wait_ge(turned, NBATCH)
            nc.gpsimd.memset(hT, 0.0).then_inc(hT_zero, 1)
            pool.wait_ge(tok_end_dve, 1)
            pool.wait_ge(tok_end_act, 1)
            for b in pT:
                nc.gpsimd.memset(b, 0.0).then_inc(pT_zero, 1)
            pool.wait_ge(qkv_mm, 44)
            nc.gpsimd.memset(pexp, 0.0).then_inc(pexp_zero, 1)

        @block.tensor
        def _(pe):
            pe.wait_ge(ld_ident, 16)
            pe.wait_ge(ld_conv, 16)
            pe.wait_ge(pads_zero, 3)
            for j in range(NK):
                for k in range(KC):
                    w = conv_nat[:, k, j * CK:(j + 1) * CK]
                    m = pe.transpose(bank(j)[0:CK, k * P:(k + 1) * P], w, ident[:, :])
                m.then_inc(conv_turned, 1)
            pe.wait_ge(ld_vec, 16 * 8)
            pe.transpose(bank(5, 16), vec_rows[0:16, :], ident[0:16, 0:16]).then_inc(vec_turned, 1)
            pe.wait_ge(conv_kept, NK)
            pe.wait_ge(vec_kept, 1)
            for step, i in TOK:
                if step == "turn":
                    pe.wait_ge(packed, (4 * i + 3) // NK // WS + 1)
                    if i >= 2:
                        batches_of_pixels_kept(pe, i - 1)
                    for j in range(4):
                        m = pe.transpose(bank(i % 2, P, j * P)[0:CK, :], pixels(4 * i + j), ident[:, :])
                    m.then_inc(turned, 1)
                elif step == "conv":
                    batches_of_pixels_kept(pe, last_batch(i) + 1)
                    if i >= 2:
                        pe.wait_ge(conv_kept_sb, i - 1)
                    for j in range(NK):
                        b, at = (i * NK + j) // 4, (i * NK + j) % 4 * P
                        m = pe.matmul(bank(2 + i % 2, C), xT[b % XT][0:CK, at:at + P], convT[0:CK, j, :],
                                      start=(j == 0), stop=(j == NK - 1))
                    m.then_inc(conv_done, 1)
                elif step == "zturn":
                    ts = patches_of(i)
                    pe.wait_ge(z_ready, ts[-1] // WS + 1)
                    if i >= 1:
                        pe.wait_ge(z_kept, i)
                    for x, t in enumerate(ts):
                        for k in range(KC):
                            m = pe.transpose(bank(4, P, (k * 2 + x) * P),
                                             zgrp[t // WS % 2][:, (t % WS) * C + k * P:(t % WS) * C + (k + 1) * P], ident[:, :])
                    m.then_inc(z_turned, 1)
                elif step == "kv":
                    w, first = i // KVN, i % KVN * 2
                    ks = range(first, min(first + 2, NPOS))
                    pe.wait_ge(z_kept, i + 1)
                    pe.wait_ge(ld_tokw, 16 * 9)
                    for b, ready, read, at in ((5, k_ready, k_read, 0), (6, v_ready, v_read, C)):
                        if i >= 1:
                            pe.wait_ge(read, i)
                        for x, pos in enumerate(ks):
                            for k in range(KC):
                                m = pe.matmul(bank(b, C, x * C), zT[:, (w * NPOS + pos) % ZSLOTS, k, :],
                                              t_wkv[:, k, at:at + C], start=(k == 0), stop=(k == KC - 1))
                        m.then_inc(ready, 1)
                elif step == "turnw":
                    if i == 0:
                        pe.wait_ge(ffn_quant, 3)
                        pe.wait_ge(conv_kept_sb, NP_)
                    turn_batch(pe, i)
                elif (step, i) in SHARED_NO:
                    n, o = shared((step, i))
                    if n >= 1:
                        pe.wait_ge(win_read, n)
                    if step in LNT:
                        pe.wait_ge(ln_z, LN[(LNT[step], i)] + 1)
                        for k in range(KC):
                            m = pe.transpose(o[:, k * P:(k + 1) * P], lnz[:, k * P:(k + 1) * P], ident[:, :])
                    elif step in ("gq", "q", "gkv"):
                        if step == "gq":
                            pe.wait_ge(ld_cls, 32)
                        else:
                            pe.wait_ge(ld_tokw, 16 * 9)
                        pe.wait_ge(ln_kept, LN[({"gq": "cls", "q": "red", "gkv": "loz"}[step], i)] + 1)
                        w = {"gq": g_wq, "q": t_wq, "gkv": g_wkv}[step]
                        for k in range(KC):
                            m = pe.matmul(o[:, 0:w.shape[2]], trn[:, k, :], w[:, k, :], start=(k == 0), stop=(k == KC - 1))
                    elif step in ("aggT", "gaggT"):
                        pe.wait_ge(agg_ready, AGG[({"aggT": "agg", "gaggT": "gsoft"}[step], i)] + 1)
                        for k in range(KC):
                            m = pe.transpose(o[:, k * P:(k + 1) * P], agg[:, k * P:(k + 1) * P], ident[:, :])
                    elif step in ("proj", "gproj"):
                        pe.wait_ge(aggT_kept, AGGT[({"proj": "aggT", "gproj": "gaggT"}[step], i)] + 1)
                        pe.wait_ge(ld_tokw, 16 * 9)
                        w = t_proj if step == "proj" else g_proj
                        for k in range(KC):
                            m = pe.matmul(o[:, 0:C], trn2[:, k, :], w[:, k, :], start=(k == 0), stop=(k == KC - 1))
                    elif step == "loT":
                        pe.wait_ge(lo_ready, i + 1)
                        for k in range(KC):
                            m = pe.transpose(o[:, k * P:(k + 1) * P], lo[:, k * P:(k + 1) * P], ident[:, :])
                    elif step == "mod":
                        pe.wait_ge(loT_kept, i + 1)
                        for k in range(KC):
                            m = pe.matmul(o[:, 0:C], trn3[:, k, :], t_mod[:, k, :], start=(k == 0), stop=(k == KC - 1))
                    m.then_inc(win_ready, 1)
            pe.wait_ge(tok_end_dve, 1)
            pe.wait_ge(tok_end_act, 1)
            pe.wait_ge(ld_small, 16 * 6)
            for j in range(S):
                m = pe.matmul(bank(2, NH, j * NH), onehot[0:32, j * P:(j + 1) * P], relb[0:32, :], start=True, stop=True)
            m.then_inc(bias_mm, 1)

            for s in range(S):
                if s >= 2:
                    pe.wait_ge(hT_kept, s - 1)
                for k in range(KC):
                    m = pe.transpose(bank(s % 2, P, k * P), H[0][:, s * C + k * P:s * C + (k + 1) * P], ident[:, :])
                m.then_inc(hT_turned, 1)
            pe.wait_ge(hT_kept, S)
            pe.wait_ge(ld_attnw, 64)
            pe.wait_ge(bias_ready, 1)
            n = 0
            for c in range(8):
                for w in (w_q, w_k):
                    for hf in range(2):
                        if n >= 4:
                            pe.wait_ge(qkv_kept_dve if n % 2 else qkv_kept_act, (n - 4) // 2 + 1)
                        o = bank(2 + n % 4, SLOTS // 2)
                        for k in range(KC):
                            m = pe.matmul(o, w[:, k, c * P:(c + 1) * P], hT[:, k, hf * 384:(hf + 1) * 384],
                                          start=(k == 0), stop=(k == KC - 1))
                        m.then_inc(qkv_mm, 1)
                        n += 1
            for t in range(NT):
                for hf in range(2):
                    pe.wait_ge(qkv_kept_dve if n % 2 else qkv_kept_act, (n - 4) // 2 + 1)
                    o = bank(2 + n % 4)
                    for k in range(KC):
                        m = pe.matmul(o, hT[:, k, t * P:(t + 1) * P], w_v[:, k, hf * 512:(hf + 1) * 512],
                                      start=(k == 0), stop=(k == KC - 1))
                    m.then_inc(qkv_mm, 1)
                    n += 1
            pe.wait_ge(qkv_kept_act, n // 2)
            pe.wait_ge(qkv_kept_dve, n // 2)

            def scores(t):
                for half in range(2):
                    if t >= 1:
                        pe.wait_ge(score_read, 2 * t - 1 + half)
                    for c in range(8):
                        r = half * DK
                        sl = slice(t * P, (t + 1) * P)
                        m = pe.matmul(score_bank(half)[:, c, :], qT[r:r + DK, c, sl], kT[r:r + DK, c, sl],
                                      start=True, stop=True)
                    m.then_inc(score_mm, 1)

            def contexts(t):
                pe.wait_ge(pT_ready, t + 1)
                for half in range(2):
                    if t >= 2:
                        pe.wait_ge(ctx_kept_dve if half else ctx_kept_act, t - 1)
                    for c in range(4 * half, 4 * half + 4):
                        for par in range(2):
                            r, h = par * DK, 2 * c + par
                            m = pe.matmul(bank(2 + t % 2 * 2 + half)[r:r + DK, c % 4 * P:(c % 4 + 1) * P],
                                          V[:, t, h * DK:(h + 1) * DK], pT[t % 2][:, par * 8 + c, :], start=True, stop=True)
                    m.then_inc(ctx_mm, 1)

            for u in range(NT // 2 + 1):
                if u < NT // 2:
                    scores(2 * u)
                    scores(2 * u + 1)
                if u >= 1:
                    contexts(2 * u - 2)
                    contexts(2 * u - 1)
            pe.wait_ge(ctx_kept_act, NT)
            pe.wait_ge(ctx_kept_dve, NT)
            for s in range(S):
                if s >= 2:
                    pe.wait_ge(wo_read, s - 1)
                for c in range(8):
                    m = pe.matmul(bank(6 + s % 2, C), ctxT[:, c, s, :], w_o[:, c, :], start=(c == 0), stop=(c == 7))
                m.then_inc(wo_mm, 1)

            def global_max(i):
                pe.wait_ge(gmax_part, i + 1)
                pe.transpose(bank(6)[0:1, 0:P], gm[:, :], ident[:, :]).then_inc(gmax_row, 1)
                pe.wait_ge(gmax_one, i + 1)
                pe.matmul(bank(7, 1), ones[0:1, :], gm[0:1, :], start=True, stop=True).then_inc(gmax_all, 1)

            def turn_token(src, stage, s):
                if s >= 2:
                    tokens_kept(pe, stage, s - 1)
                for k in range(KC):
                    m = pe.transpose(bank(s % 2, P, k * P), src[:, s * C + k * P:s * C + (k + 1) * P], ident[:, :])
                m.then_inc(hT2_turned, 1)

            global_max(0)
            for s in range(S):
                pe.wait_ge(hq_ready, s + 1)
                turn_token(h1q, 0, s)
            batches_kept(pe, FFN_BATCHES)
            tokens_kept(pe, 0, S)
            n = 0
            for w in (upT, gateT):
                for c in range(6):
                    for hf in range(2):
                        if n >= 6:
                            pe.wait_ge(ff_kept, n - 5)
                        for k in range(KC):
                            m = pe.matmul(bank(n % 6, 320), w[:, k, c * P:(c + 1) * P], h1T[:, k, hf * 320:(hf + 1) * 320],
                                          start=(k == 0), stop=(k == KC - 1))
                        m.then_inc(ff_mm, 1)
                        n += 1
                if w is upT:
                    global_max(1)
            global_max(2)
            pe.wait_ge(ff_kept, 24)
            pe.wait_ge(ld_l1, 16 * 7)
            for b in range(FFN_BATCHES, len(WB)):
                turn_batch(pe, b)
            global_max(3)
            global_max(4)
            def down(s):
                pe.wait_ge(o_ready, s + 1)
                if s >= 2:
                    pe.wait_ge(down_read, s - 1)
                for c in range(6):
                    m = pe.matmul(bank(6 + s % 2, C), sig.rearrange("p (c n) -> p c n", c=6)[:, c, s * P:(s + 1) * P],
                                  downT[:, c, :], start=(c == 0), stop=(c == 5))
                m.then_inc(down_mm, 1)

            def project(s):
                tokens_kept(pe, 1, s + 1)
                if s >= 2:
                    pe.wait_ge(l1_kept, 2 * (s - 1))
                for hf, (at, width) in enumerate(((0, 512), (512, 256))):
                    for k in range(KC):
                        m = pe.matmul(bank(2 + 2 * (s % 2) + hf, width), h2T[:, k, s * P:(s + 1) * P],
                                      l1T[:, k, at:at + width], start=(k == 0), stop=(k == KC - 1))
                    m.then_inc(l1_mm, 1)

            batches_kept(pe, len(WB))
            for s in range(S + 2):
                if s < S:
                    down(s)
                if 1 <= s <= S:
                    pe.wait_ge(h_ready, S + s)
                    turn_token(H[0], 1, s - 1)
                if s >= 2:
                    project(s - 2)

            for s in range(S):
                pe.wait_ge(h_ready, 2 * S + s + 1)
                turn_token(H[1], 2, s)
            for s in range(S):
                tokens_kept(pe, 2, s + 1)
                for k in range(KC):
                    m = pe.matmul(bank(7, NE, s * NE), h3T[:, k, s * P:(s + 1) * P], rT[:, k, :],
                                  start=(k == 0), stop=(k == KC - 1))
            m.then_inc(r_mm, 1)
            pe.wait_ge(ld_moe, 16 * 6)
            n = 0

            def moe_bank(n):
                return bank(n % 6, 320)

            for n, (kind, c, hf) in enumerate(MOE):
                if n >= 6:
                    q = n - 6
                    if MOE[q][0] == "gate":
                        pe.wait_ge(moe_sil, moe_count(q + 1, "gate"))
                    else:
                        pe.wait_ge(moe_hid, moe_count(q + 1, "up") + moe_count(q + 1, "comb"))
                o = moe_bank(n)
                sl = slice(hf * 320, (hf + 1) * 320)
                if kind == "comb":
                    if n == FIRST_COMB:
                        pe.wait_ge(combT_kept, 1)
                    m = pe.matmul(o, pick[0:NE, c - 4, :], combT[0:NE, sl], start=True, stop=True)
                else:
                    for k in range(KC):
                        if c < 4:
                            w = shT[:, 0 if kind == "gate" else 1, k, c * P:(c + 1) * P]
                        else:
                            w = (e_gate if kind == "gate" else e_up)[:, k, 2 * (c - 4):2 * (c - 4) + 2, :]
                        m = pe.matmul(o, w, h3T[:, k, sl], start=(k == 0), stop=(k == KC - 1))
                m.then_inc(moe_mm, 1)
                if n == FIRST_COMB - 1:
                    pe.wait_ge(comb_ready, 1)
                    for s in range(S):
                        b, at = (6, s * P) if s < 4 else (7, 0)
                        m = pe.transpose(bank(b)[0:NE, at:at + P], comb_w[:, s * NE:(s + 1) * NE], ident[:, :])
                    m.then_inc(combT_mm, 1)
            pe.wait_ge(moe_hid, moe_count(len(MOE), "up") + moe_count(len(MOE), "comb"))
            pe.wait_ge(moe_sil, moe_count(len(MOE), "gate"))
            for s in range(S):
                if s >= 2:
                    pe.wait_ge(down_read, S + s - 1)
                for c in range(12):
                    w = sdT[:, c, :] if c < 4 else e_down[:, c - 4, :]
                    m = pe.matmul(bank(s % 2, C), hid[:, c, s * P:(s + 1) * P], w, start=(c == 0), stop=(c == 11))
                m.then_inc(down_mm, 1)

        @block.scalar
        def _(act):
            chain = [0]

            def link(ins):
                chain[0] += 1
                ins.then_inc(act_chain, 1)
                act.wait_ge(act_chain, chain[0])

            for j in range(0, NK, 2):
                act.wait_ge(conv_turned, j + 1)
                nc.scalar.copy(convT[0:CK, j, :], bank(j, C)[0:CK]).then_inc(conv_kept, 1)
            for step, i in TOK:
                if step == "turn" and not DVE_TURNS(i):
                    act.wait_ge(turned, i + 1)
                    if i >= XT:
                        act.wait_ge(conv_done, (4 * (i - XT) + 3) // NK + 1)
                    nc.scalar.copy(xT[i % XT][0:CK, :], bank(i % 2)[0:CK]).then_inc(turned_kept_act, 1)
                elif step == "conv":
                    act.wait_ge(conv_done, i + 1)
                    if i // WS >= 2:
                        act.wait_ge(z_ready, i // WS - 1)
                    nc.scalar.copy(pes[i // WS % 2][:, (i % WS) * C:(i % WS + 1) * C], bank(2 + i % 2, C)).then_inc(conv_kept_sb, 1)
                elif step == "turnw":
                    keep_batch(act, nc.scalar.copy, i, wt_kept)
                elif step == "stat root":
                    act.wait_ge(var_ready, i + 1)
                    nc.scalar.activation(rs3, rc3, ACT.Sqrt).then_inc(rstd_ready, 1)
                elif step in ("cls root", "red root", "loz root"):
                    act.wait_ge(ln_var, LN[(step.split()[0], i)] + 1)
                    nc.scalar.activation(rs1, rc1, ACT.Sqrt).then_inc(ln_rstd, 1)
                elif step == "kv":
                    if i % KVN == 0 and i >= KVN:
                        act.wait_ge(qk_done, i // KVN)
                    act.wait_ge(k_ready, i + 1)
                    at, n = i % KVN * 2 * C, min(2, NPOS - i % KVN * 2) * C
                    nc.scalar.copy(kwin[:, at:at + n], bank(5, n)).then_inc(k_read, 1)
                    if i % KVN == 0 and i >= KVN:
                        act.wait_ge(pv_done, i // KVN)
                    act.wait_ge(v_ready, i + 1)
                    nc.scalar.copy(vwin[:, at:at + n], bank(6, n)).then_inc(v_read, 1)
                elif step == "soft exp":
                    act.wait_ge(shifted, SM[("soft", i)] + 1)
                    nc.scalar.activation(sc, sc, ACT.Exp).then_inc(exp_done, 1)
                elif step == "gsoft exp":
                    act.wait_ge(shifted, SM[("gsoft", i)] + 1)
                    nc.scalar.activation(gs, gs, ACT.Exp).then_inc(exp_done, 1)
                elif step == "aggT":
                    n, o = shared((step, i))
                    act.wait_ge(win_ready, n + 1)
                    nc.scalar.copy(trn2, o[:, 0:C].rearrange("p (k n) -> p k n", k=KC)).then_inc(win_read, 1)
                    act.wait_ge(win_read, n + 1)
                    act.sem_inc(aggT_kept, 1)
                elif step == "loT":
                    n, o = shared((step, i))
                    act.wait_ge(win_ready, n + 1)
                    nc.scalar.copy(trn3, o[:, 0:C].rearrange("p (k n) -> p k n", k=KC)).then_inc(win_read, 1)
                    act.wait_ge(win_read, n + 1)
                    act.sem_inc(loT_kept, 1)
            act.wait_ge(win_read, len(SHARED))
            act.sem_inc(tok_end_act, 1)

            for n in range(0, 44, 2):
                act.wait_ge(qkv_mm, n + 1)
                qkv_copy(nc.scalar.copy, n).then_inc(qkv_kept_act, 1)
            def read_scores(t):
                if t % 2 == 0 and t >= 2:
                    act.wait_ge(att_shift, t // 2)
                for half in range(2):
                    act.wait_ge(score_mm, 2 * t + half + 1)
                    for g in range(4):
                        at = (t % 2 * NH + half * 8) * 30
                        m = nc.scalar.copy(smask[g * 32:(g + 1) * 32, at:at + 240].rearrange("p (h x) -> p h x", x=30),
                                           score_bank(half)[g * 32:(g + 1) * 32, :, g * 32:g * 32 + 30])
                    m.then_inc(score_read, 1)

            for u in range(NT // 2 + 1):
                if u < NT // 2:
                    read_scores(2 * u)
                    read_scores(2 * u + 1)
                    act.wait_ge(att_shift, u + 1)
                    nc.scalar.activation(att, att, ACT.Exp).then_inc(att_exp, 1)
                if u >= 1:
                    for t in (2 * u - 2, 2 * u - 1):
                        ctx_copy(nc.scalar.copy, act, ctx_kept_act, t, 0)
            def rstd(n, tokens=1):
                act.wait_ge(rln_var, n + 1)
                nc.scalar.activation(rs5[:, 0:tokens], rc5[:, 0:tokens], ACT.Sqrt).then_inc(rln_rstd, 1)

            for s in range(S):
                rstd(s)
            for s in (1, 3):
                keep_token(act, nc.scalar.copy, h1T, 0, s, hT2_kept_act)
            for n in range(24):
                act.wait_ge(ff_mm, n + 1)
                dst = (up if n < 12 else gate)[:, (n % 12) * 320:(n % 12 + 1) * 320]
                nc.scalar.copy(dst, bank(n % 6, 320)).then_inc(ff_kept, 1)
            for half in range(2):
                act.wait_ge(gate_q, half + 1)
                sl = slice(half * 3 * S * P, (half + 1) * 3 * S * P)
                nc.scalar.activation(sig[:, sl], gate[:, sl], ACT.Sigmoid, scale=qsc[:, 2:3]).then_inc(sig_ready, 1)
            for b in range(FFN_BATCHES, len(WB)):
                keep_batch(act, nc.scalar.copy, b, wt_kept)
            for s in range(S + 2):
                if s < S:
                    rstd(S + s)
                if s in (2, 4):
                    keep_token(act, nc.scalar.copy, h2T, 1, s - 1, hT2_kept_act)
                if s >= 2:
                    t = s - 2
                    for hf, (at, width) in enumerate(((0, 512), (512, 256))):
                        act.wait_ge(l1_mm, 2 * t + hf + 1)
                        nc.scalar.copy(qkv[:, t, at:at + width], bank(2 + 2 * (t % 2) + hf, width)).then_inc(l1_kept, 1)
            act.wait_ge(l1_shift, 1)
            nc.scalar.activation(msc, msc, ACT.Exp).then_inc(l1_exp, 1)
            rstd(2 * S, 3)
            rstd(2 * S + 1, 2)
            for s in (1, 3):
                keep_token(act, nc.scalar.copy, h3T, 2, s, hT2_kept_act)
            act.wait_ge(r_mm, 1)
            nc.scalar.activation(comb_w, bank(7, S * NE), ACT.Sigmoid).then_inc(r_sig, 1)
            g = 0
            for n, (kind, c, hf) in enumerate(MOE):
                if kind == "gate":
                    act.wait_ge(moe_mm, n + 1)
                    if g >= 2:
                        q = [m for m, x in enumerate(MOE) if x[0] == "up"][g - 2]
                        act.wait_ge(moe_hid, moe_count(q + 1, "up") + moe_count(q + 1, "comb"))
                    nc.scalar.activation(sil[g % 2], bank(n % 6, 320), ACT.Silu).then_inc(moe_sil, 1)
                    g += 1
            for s in range(S):
                rstd(2 * S + 2 + s)

        @block.vector
        def _(dve):
            chain = [0]

            def link(ins):
                chain[0] += 1
                ins.then_inc(dve_chain, 1)
                dve.wait_ge(dve_chain, chain[0])

            def moments(x, st, mv, rc, n=1):
                for k in range(n):
                    m = nc.vector.bn_stats(st[:, 6 * k:6 * k + 6], x[:, k * C:(k + 1) * C])
                link(m)
                for k in range(n):
                    m = nc.vector.bn_aggr(mv[:, 2 * k:2 * k + 2], st[:, 6 * k:6 * k + 6])
                link(m)
                v = mv[:, 0:2 * n].rearrange("p (k two) -> p k two", two=2)[:, :, 1]
                link(nc.vector.tensor_scalar(rc, v, EPS, None, ALU.add))
                return nc.vector.reciprocal(rc, rc)

            for j in range(1, NK, 2):
                dve.wait_ge(conv_turned, j + 1)
                nc.vector.tensor_copy(convT[0:CK, j, :], bank(j, C)[0:CK]).then_inc(conv_kept, 1)
            dve.wait_ge(vec_turned, 1)
            nc.vector.tensor_copy(vec[:, :], bank(5, 16)).then_inc(vec_kept, 1)
            dve.wait_ge(vec_kept, 1)

            def softmax_part1(s, n):
                link(nc.vector.tensor_reduce(mx8, s.rearrange("p k h -> p h k"), AX.X, ALU.max))
                nc.vector.tensor_tensor(s, s, mx8.unsqueeze(1).to_broadcast([P, n, LH]), ALU.subtract).then_inc(shifted, 1)

            def softmax_part2(s, n):
                link(nc.vector.tensor_reduce(sm8, s.rearrange("p k h -> p h k"), AX.X, ALU.add))
                link(nc.vector.reciprocal(rs8, sm8))
                return nc.vector.tensor_tensor(s, s, rs8.unsqueeze(1).to_broadcast([P, n, LH]), ALU.mult)

            for step, i in TOK:
                if step == "turn" and DVE_TURNS(i):
                    dve.wait_ge(turned, i + 1)
                    if i >= XT:
                        dve.wait_ge(conv_done, (4 * (i - XT) + 3) // NK + 1)
                    nc.vector.tensor_copy(xT[i % XT][0:CK, :], bank(i % 2)[0:CK]).then_inc(turned_kept_dve, 1)
                elif step == "stat":
                    w, first = i // WS, i % WS == 0
                    dve.wait_ge(conv_kept_sb, WS * (i + 1))
                    emb = pes[i % 2]
                    moments(emb, st3, mv3, rc3, WS).then_inc(var_ready, 1)
                    v = emb.rearrange("p (k n) -> p n k", k=WS)
                    if first:
                        link(nc.vector.tensor_reduce(red[:, w, :], v, AX.X, ALU.add))
                    else:
                        link(nc.vector.tensor_reduce(tmp[:, :], v, AX.X, ALU.add))
                        link(nc.vector.tensor_tensor(red[:, w, :], red[:, w, :], tmp[:, :], ALU.add))
                elif step == "stat z":
                    emb = pes[i % 2]
                    dve.wait_ge(rstd_ready, i + 1)
                    if i >= 2:
                        dve.wait_ge(z_turned, pair_of(WS * (i - 1) - 1) + 1)
                    for k in range(WS):
                        m = nc.vector.tensor_scalar(zgrp[i % 2][:, k * C:(k + 1) * C], emb[:, k * C:(k + 1) * C],
                                                    mv3[:, 2 * k:2 * k + 1], rs3[:, k:k + 1], ALU.subtract, ALU.mult)
                    m.then_inc(z_ready, 1)
                    dve.wait_ge(z_ready, i + 1)
                elif step == "zturn":
                    dve.wait_ge(z_turned, i + 1)
                    if i >= 2 * KVN:
                        dve.wait_ge(v_ready, i - 2 * KVN + 1)
                    slot, n = patches_of(i)[0] % ZSLOTS, len(patches_of(i))
                    for k in range(KC):
                        m = nc.vector.tensor_scalar(zT[:, slot:slot + n, k, :],
                                                    bank(4, n * P, k * 2 * P).rearrange("p (t n) -> p t n", n=P),
                                                    vec[:, 4 + k:5 + k], vec[:, 6 + k:7 + k], ALU.mult, ALU.add)
                    m.then_inc(z_kept, 1)
                elif step in ("cls", "red", "loz"):
                    n = LN[(step, i)]
                    if step == "cls":
                        dve.wait_ge(ld_cls, 32)
                        x = cls[:, :]
                    elif step == "red":
                        link(nc.vector.tensor_scalar(red[:, i, :], red[:, i, :], 1.0 / NPOS, None, ALU.mult))
                        x = red[:, i, :]
                    else:
                        x = lo[:, :]
                    moments(x, st1, mv1, rc1).then_inc(ln_var, 1)
                elif step in ("cls z", "red z", "loz z"):
                    step = step.split()[0]
                    n = LN[(step, i)]
                    x = {"cls": cls[:, :], "red": red[:, i, :], "loz": lo[:, :]}[step]
                    dve.wait_ge(ln_rstd, n + 1)
                    if n >= 1:
                        dve.wait_ge(ln_kept, n)
                    nc.vector.tensor_scalar(lnz[:, :], x, mv1[:, 0:1], rs1[:, 0:1], ALU.subtract, ALU.mult).then_inc(ln_z, 1)
                    dve.wait_ge(ln_z, n + 1)
                elif step == "qk":
                    dve.wait_ge(k_read, (i + 1) * KVN)
                    nc.vector.tensor_tensor(prod.rearrange("p (k n) -> p k n", n=C), kwin.rearrange("p (k n) -> p k n", n=C),
                                            qwin[:, :].unsqueeze(1).to_broadcast([P, NPOS, C]), ALU.mult).then_inc(qk_done, 1)
                    dve.wait_ge(qk_done, i + 1)
                elif (step, i) in SHARED_NO and "d" in READERS[step]:
                    n, o = shared((step, i))
                    dve.wait_ge(win_ready, n + 1)
                    if step in LNT:
                        v = {"clsT": 8, "redT": 0, "lozT": 12}[step]
                        for k in range(KC):
                            m = nc.vector.tensor_scalar(trn[:, k, :], o[:, k * P:(k + 1) * P], vec[:, v + k:v + k + 1],
                                                        vec[:, v + 2 + k:v + 3 + k], ALU.mult, ALU.add)
                        m.then_inc(win_read, 1)
                        dve.wait_ge(win_read, n + 1)
                        dve.sem_inc(ln_kept, 1)
                    elif step == "gq":
                        nc.vector.tensor_scalar(gq[:, :], o[:, 0:C], C ** -0.5, None, ALU.mult).then_inc(win_read, 1)
                    elif step == "q":
                        nc.vector.tensor_scalar(qwin[:, :], o[:, 0:C], C ** -0.5, None, ALU.mult).then_inc(win_read, 1)
                        dve.wait_ge(win_read, n + 1)
                    elif step == "proj":
                        dve.wait_ge(ld_tokw, 16 * 9)
                        link(nc.vector.tensor_tensor(tmp[:, :], o[:, 0:C], red[:, i, :], ALU.add))
                        nc.vector.tensor_tensor(lo[:, :], tmp[:, :], proj_b[:, :], ALU.add).then_inc(lo_ready, 1)
                        dve.wait_ge(lo_ready, i + 1)
                        dve.sem_inc(win_read, 1)
                    elif step == "mod":
                        nc.vector.tensor_tensor(H[0][:, i * C:(i + 1) * C], o[:, 0:C], mod_b[:, :], ALU.add).then_inc(win_read, 1)
                    elif step == "gkv":
                        link(nc.vector.tensor_tensor(tmp[:, :], o[:, 0:C], gq[:, :], ALU.mult))
                        link(nc.vector.tensor_reduce(gs[:, i * LH:(i + 1) * LH], tmp[:, :].rearrange("p (h d) -> p h d", d=LD),
                                                     AX.X, ALU.add))
                        nc.vector.tensor_copy(gv[:, i * C:(i + 1) * C], o[:, C:2 * C]).then_inc(win_read, 1)
                    elif step == "gaggT":
                        nc.vector.tensor_copy(trn2, o[:, 0:C].rearrange("p (k n) -> p k n", k=KC)).then_inc(win_read, 1)
                        dve.wait_ge(win_read, n + 1)
                        dve.sem_inc(aggT_kept, 1)
                    elif step == "gproj":
                        link(nc.vector.tensor_tensor(tmp[:, :], o[:, 0:C], cls[:, :], ALU.add))
                        nc.vector.tensor_tensor(H[0][:, NW * C:S * C], tmp[:, :], gproj_b[:, :], ALU.add).then_inc(win_read, 1)
                elif step == "soft":
                    s = sc.rearrange("p (k h) -> p k h", h=LH)
                    link(nc.vector.tensor_reduce(sc, prod.rearrange("p (kh d) -> p kh d", d=LD), AX.X, ALU.add))
                    softmax_part1(s, NPOS)
                elif step == "soft norm":
                    s = sc.rearrange("p (k h) -> p k h", h=LH)
                    dve.wait_ge(exp_done, SM[("soft", i)] + 1)
                    softmax_part2(s, NPOS).then_inc(probs_ready, 1)
                elif step == "agg":
                    if PV_POOL[i] < NPOS:
                        dve.wait_ge(v_read, (i + 1) * KVN)
                        dve.wait_ge(probs_ready, i + 1)
                        link(weigh_values(nc.vector.tensor_tensor, PV_POOL[i], NPOS))
                    dve.wait_ge(pv_done, i + 1)
                    if i >= 1:
                        dve.wait_ge(aggT_kept, i)
                    nc.vector.tensor_reduce(agg[:, :], prod.rearrange("p (k n) -> p n k", k=NPOS), AX.X, ALU.add).then_inc(agg_ready, 1)
                elif step == "gsoft":
                    s = gs.rearrange("p (k h) -> p k h", h=LH)
                    softmax_part1(s, NW)
                elif step == "gsoft norm":
                    s = gs.rearrange("p (k h) -> p k h", h=LH)
                    dve.wait_ge(exp_done, SM[("gsoft", i)] + 1)
                    link(softmax_part2(s, NW))
                    dve.wait_ge(win_read, SHARED_NO[("gkv", NW - 1)] + 1)
                    g4 = gv[:, :].rearrange("p (kh d) -> p kh d", d=LD)
                    link(nc.vector.tensor_tensor(g4, g4, gs.unsqueeze(2).to_broadcast([P, NW * LH, LD]), ALU.mult))
                    nc.vector.tensor_reduce(agg[:, :], gv[:, :].rearrange("p (k n) -> p n k", k=NW), AX.X, ALU.add).then_inc(agg_ready, 1)
                elif step == "quant":
                    dve.wait_ge(ld_ffn, 48)
                    w, scales = ffn_matrix(i)
                    link(nc.vector.tensor_reduce(ffn_abs[:, scales], w, AX.X, ALU.max, apply_absolute_value=True))
                    link(nc.vector.tensor_scalar(ffn_abs[:, scales], ffn_abs[:, scales], 1.0 / 7.0, 1e-12, ALU.mult, ALU.max))
                    nc.vector.reciprocal(ffn_inv[:, scales], ffn_abs[:, scales]).then_inc(ffn_scale, 1)
                elif step == "round":
                    dve.wait_ge(ffn_over, i + 1)
                    w, _ = ffn_matrix(i)
                    nc.vector.tensor_scalar(w, w, MAGIC, MAGIC, ALU.add, ALU.subtract).then_inc(ffn_rounded, 1)
            dve.wait_ge(win_read, len(SHARED))
            dve.sem_inc(tok_end_dve, 1)

            dve.wait_ge(hT_zero, 1)
            hv = hT.rearrange("p k (g x) -> p k g x", x=32)
            for s in range(S):
                dve.wait_ge(hT_turned, s + 1)
                for k in range(KC):
                    dst = hv[:, k, 0:FULLG, 0:30].rearrange("p g (i s) -> p g i s", s=S)[:, :, :, s]
                    m = nc.vector.tensor_copy(dst, bank(s % 2, P, k * P)[:, 0:FULLG * GI].rearrange("p (g i) -> p g i", i=GI))
                nc.vector.tensor_copy(hv[:, :, FULLG, s:s + S + 1:S],
                                      bank(s % 2, C).rearrange("p (k n) -> p k n", k=KC)[:, :, FULLG * GI:P]).then_inc(hT_kept, 1)
            dve.wait_ge(bias_mm, 1)
            nc.vector.tensor_copy(bias.rearrange("p (a c j) -> p a c j", a=2, j=S),
                                  bank(2, S * NH).rearrange("p (j c a) -> p a c j", j=S, a=2)).then_inc(bias_ready, 1)
            for n in range(1, 44, 2):
                dve.wait_ge(qkv_mm, n + 1)
                qkv_copy(nc.vector.tensor_copy, n).then_inc(qkv_kept_dve, 1)
            dve.wait_ge(bias_ready, 1)
            dve.wait_ge(ld_small, 16 * 6)
            dve.wait_ge(pexp_zero, 1)
            a3 = att.rearrange("p (h j) -> p h j", j=S)

            def att_shifted(u):
                dve.wait_ge(score_read, 4 * u + 4)
                m4 = smask.rearrange("p (h i j) -> p h i j", i=GI, j=S)
                link(nc.vector.tensor_tensor(m4, m4, own[:, :].unsqueeze(1).unsqueeze(3).to_broadcast([P, 2 * NH, GI, S]), ALU.mult))
                link(nc.vector.tensor_reduce(a3, smask.rearrange("p (h i j) -> p h j i", i=GI, j=S), AX.X, ALU.add))
                link(nc.vector.tensor_tensor(att.rearrange("p (t x) -> p t x", t=2), att.rearrange("p (t x) -> p t x", t=2),
                                             bias.unsqueeze(1).to_broadcast([P, 2, NH * S]), ALU.add))
                link(nc.vector.tensor_reduce(att_mx, a3, AX.X, ALU.max))
                nc.vector.tensor_tensor(a3, a3, att_mx.unsqueeze(2).to_broadcast([P, 2 * NH, S]), ALU.subtract).then_inc(att_shift, 1)

            def att_probs(u):
                dve.wait_ge(att_exp, u + 1)
                link(nc.vector.tensor_reduce(att_sm, a3, AX.X, ALU.add))
                link(nc.vector.reciprocal(att_sm, att_sm))
                link(nc.vector.tensor_tensor(a3, a3, att_sm.unsqueeze(2).to_broadcast([P, 2 * NH, S]), ALU.mult))
                o = pexp.rearrange("p (h x) -> p h x", x=32)[:, :, 0:30].rearrange("p h (i j) -> p h i j", j=S)
                link(nc.vector.tensor_tensor(o, a3.unsqueeze(2).to_broadcast([P, 2 * NH, GI, S]),
                                             own[:, :].unsqueeze(1).unsqueeze(3).to_broadcast([P, 2 * NH, GI, S]), ALU.mult))
                for t in (2 * u, 2 * u + 1):
                    if t >= 2:
                        dve.wait_ge(ctx_mm, 2 * (t - 1))
                    else:
                        dve.wait_ge(pT_zero, 2)
                    for g in range(4):
                        q = slice(g * 32, (g + 1) * 32)
                        m = nc.vector.transpose(pT[t % 2][q, :, q], pexp[q, t % 2 * NH * 32:(t % 2 + 1) * NH * 32])
                    m.then_inc(pT_ready, 1)
                dve.wait_ge(pT_ready, 2 * u + 2)

            for u in range(NT // 2 + 1):
                if u < NT // 2:
                    att_shifted(u)
                if u >= 1:
                    ctx_copy(nc.vector.tensor_copy, dve, ctx_kept_dve, 2 * u - 2, 1)
                if u < NT // 2:
                    att_probs(u)
                if u >= 1:
                    ctx_copy(nc.vector.tensor_copy, dve, ctx_kept_dve, 2 * u - 1, 1)

            def res_ln(n, x, dst, tokens=1, behind=None):
                moments(x, st5, mv5, rc5[:, 0:tokens], tokens).then_inc(rln_var, 1)
                if behind is not None:
                    behind()
                dve.wait_ge(rln_rstd, n + 1)
                for k in range(tokens):
                    m = nc.vector.tensor_scalar(dst[:, k * C:(k + 1) * C], x[:, k * C:(k + 1) * C], mv5[:, 2 * k:2 * k + 1],
                                                rs5[:, k:k + 1], ALU.subtract, ALU.mult).then_inc(h_ready, 1)
                    ready[0] += 1
                dve.wait_ge(h_ready, ready[0])

            ready = [0]

            def tok(h, s):
                return h[:, s * C:(s + 1) * C]

            for s in range(S):
                dve.wait_ge(wo_mm, s + 1)
                nc.vector.tensor_tensor(tok(H[1], s), bank(6 + s % 2, C), tok(H[0], s), ALU.add).then_inc(wo_read, 1)
                dve.wait_ge(wo_read, s + 1)
                res_ln(s, tok(H[1], s), tok(H[1], s))
                nc.vector.tensor_reduce(pmax[:, s:s + 1], tok(H[1], s), AX.X, ALU.max, apply_absolute_value=True).then_inc(tok_max, 1)

            def global_max(i, fold_=None):
                dve.wait_ge(gmax_row, i + 1)
                nc.vector.tensor_reduce(gm[0:1, :], bank(6)[0:1, 0:P], AX.X, ALU.max).then_inc(gmax_one, 1)
                dve.wait_ge(gmax_all, i + 1)
                if fold_ is None:
                    link(nc.vector.tensor_scalar(qsc[:, i:i + 1], bank(7, 1), 1.0 / 32767.0, 1e-12, ALU.mult, ALU.max))
                    link(nc.vector.reciprocal(qinv[:, i:i + 1], qsc[:, i:i + 1]))
                else:
                    link(nc.vector.tensor_scalar(qsc[:, i:i + 1], bank(7, 1), fold_, 1.0 / 32767.0, ALU.mult, ALU.mult))
                    link(nc.vector.tensor_scalar(qsc[:, i:i + 1], qsc[:, i:i + 1], 1e-12, None, ALU.max))
                    link(nc.vector.reciprocal(qinv[:, i:i + 1], qsc[:, i:i + 1]))
                    link(nc.vector.tensor_scalar(qinv[:, i:i + 1], qinv[:, i:i + 1], fold_, None, ALU.mult))

            def to_integers(x, i):
                link(nc.vector.tensor_scalar(x, x, qinv[:, i:i + 1], MAGIC, ALU.mult, ALU.add))
                return nc.vector.tensor_scalar(x, x, MAGIC, None, ALU.subtract)

            dve.wait_ge(tok_max, S)
            nc.vector.tensor_reduce(gm, pmax[:, 0:S], AX.X, ALU.max).then_inc(gmax_part, 1)
            global_max(0)
            for s in range(S):
                link(nc.vector.tensor_scalar(tok(h1q, s), tok(H[1], s), qinv[:, 0:1], MAGIC, ALU.mult, ALU.add))
                nc.vector.tensor_scalar(tok(h1q, s), tok(h1q, s), MAGIC, qsc[:, 0:1], ALU.subtract, ALU.mult).then_inc(hq_ready, 1)

            for s in (0, 2, 4):
                keep_token(dve, nc.vector.tensor_copy, h1T, 0, s, hT2_kept_dve)
            for n in range(24):
                dve.wait_ge(ff_kept, n + 1)
                nc.vector.tensor_reduce(pmax[:, n % 12:n % 12 + 1], (up, gate)[n // 12][:, n % 12 * 320:(n % 12 + 1) * 320], AX.X, ALU.max,
                                        apply_absolute_value=True).then_inc(ff_max, 1)
                if n % 12 == 11:
                    dve.wait_ge(ff_max, n + 1)
                    nc.vector.tensor_reduce(gm, pmax, AX.X, ALU.max).then_inc(gmax_part, 1)
                    global_max(1 + n // 12)
                    if n < 12:
                        link(to_integers(up, 1))
            halves = [slice(half * 3 * S * P, (half + 1) * 3 * S * P) for half in range(2)]
            for sl in halves:
                to_integers(gate[:, sl], 2).then_inc(gate_q, 1)
            dve.wait_ge(gate_q, 2)

            for half, sl in enumerate(halves):
                dve.wait_ge(sig_ready, half + 1)
                link(nc.vector.tensor_scalar(sig[:, sl], sig[:, sl], 65536.0, 65535.0, ALU.mult, ALU.min))
                link(nc.vector.tensor_scalar(sig[:, sl], sig[:, sl], MAGIC, MAGIC, ALU.add, ALU.subtract))
                link(nc.vector.tensor_tensor(sig[:, sl], sig[:, sl], gate[:, sl], ALU.mult))

            nc.vector.tensor_reduce(gm, sig, AX.X, ALU.max, apply_absolute_value=True).then_inc(gmax_part, 1)
            link(nc.vector.tensor_scalar(fold[:, 0:1], qsc[:, 2:3], 1.0 / 65536.0, None, ALU.mult))
            global_max(3, fold[:, 0:1])
            for half, sl in enumerate(halves):
                link(to_integers(sig[:, sl], 3))
                link(nc.vector.tensor_tensor(sig[:, sl], sig[:, sl], up[:, sl], ALU.mult))
            nc.vector.tensor_reduce(gm, sig, AX.X, ALU.max, apply_absolute_value=True).then_inc(gmax_part, 1)
            link(nc.vector.tensor_scalar(fold[:, 1:2], qsc[:, 3:4], qsc[:, 1:2], None, ALU.mult))
            global_max(4, fold[:, 1:2])
            sig3 = sig.rearrange("p (c n) -> p c n", c=6)
            link(nc.vector.memset(msc, 0.0))

            def o_token(s):
                to_integers(sig3[:, :, s * P:(s + 1) * P], 4).then_inc(o_ready, 1)

            pair = 0
            for s in range(S + 2):
                if s == 0:
                    o_token(0)
                if s + 1 < S:
                    o_token(s + 1)
                if s < S:
                    dve.wait_ge(down_mm, s + 1)
                    nc.vector.scalar_tensor_tensor(out=tok(H[0], s), in0=bank(6 + s % 2, C), scalar=qsc[:, 4:5],
                                                   in1=tok(H[1], s), op0=ALU.mult, op1=ALU.add).then_inc(down_read, 1)
                    dve.wait_ge(down_read, s + 1)
                    res_ln(S + s, tok(H[0], s), tok(H[0], s))
                if s in (1, 3, 5):
                    keep_token(dve, nc.vector.tensor_copy, h2T, 1, s - 1, hT2_kept_dve)
                if s >= 2:
                    q = s - 2
                    dve.wait_ge(l1_kept, 2 * (q + 1))
                    for k in range(q + 1):
                        m = nc.vector.tensor_tensor_reduce(out=scr[:, pair], in0=qkv[:, q, 0:C], in1=qkv[:, k, C:2 * C],
                                                           scale=C ** -0.5, scalar=0.0, op0=ALU.mult, op1=ALU.add,
                                                           accum_out=msc[:, q * S + k:q * S + k + 1])
                        pair += 1
            link(m)
            m3 = msc.rearrange("p (q k) -> p q k", k=S)
            zero = comb_w[:, 0:S * S]
            link(nc.vector.tensor_scalar(zero, msc, 0.0, -BIG, ALU.is_equal, ALU.mult))
            link(nc.vector.tensor_tensor(msc, msc, zero, ALU.add))
            link(nc.vector.tensor_reduce(mmx, m3, AX.X, ALU.max))
            nc.vector.tensor_tensor(m3, m3, mmx.unsqueeze(2).to_broadcast([P, S, S]), ALU.subtract).then_inc(l1_shift, 1)
            dve.wait_ge(l1_exp, 1)
            link(nc.vector.tensor_reduce(msm, m3, AX.X, ALU.add))
            link(nc.vector.reciprocal(msm, msm))
            link(nc.vector.tensor_tensor(m3, m3, msm.unsqueeze(2).to_broadcast([P, S, S]), ALU.mult))
            def values(qs):
                for k in range(qs[-1] + 1):
                    for q in qs:
                        if q >= k:
                            prev = tok(H[0], q) if k == 0 else tok(H[1], q)
                            m = nc.vector.scalar_tensor_tensor(out=tok(H[1], q), in0=qkv[:, k, 2 * C:3 * C],
                                                               scalar=msc[:, q * S + k:q * S + k + 1], in1=prev,
                                                               op0=ALU.mult, op1=ALU.add)
                    link(m)

            values((0, 1, 2))
            res_ln(2 * S, H[1][:, 0:3 * C], H[1][:, 0:3 * C], 3, lambda: values((3, 4)))
            res_ln(2 * S + 1, H[1][:, 3 * C:5 * C], H[1][:, 3 * C:5 * C], 2)

            for s in (0, 2, 4):
                keep_token(dve, nc.vector.tensor_copy, h3T, 2, s, hT2_kept_dve)
            dve.wait_ge(r_sig, 1)
            route(dve, link)
            hcount = 0
            g = 0
            for n, (kind, c, hf) in enumerate(MOE):
                o = hid[:, c, hf * 320:(hf + 1) * 320]
                if n == FIRST_COMB:
                    dve.wait_ge(combT_mm, 1)
                    link(nc.vector.tensor_copy(combT[0:NE, 0:512], bank(6)[0:NE, :]))
                    nc.vector.tensor_copy(combT[0:NE, 512:640], bank(7)[0:NE, 0:P]).then_inc(combT_kept, 1)
                if kind == "up":
                    dve.wait_ge(moe_mm, n + 1)
                    dve.wait_ge(moe_sil, g + 1)
                    nc.vector.tensor_tensor(o, bank(n % 6, 320), sil[g % 2], ALU.mult).then_inc(moe_hid, 1)
                    g += 1
                    hcount += 1
                elif kind == "comb":
                    dve.wait_ge(moe_mm, n + 1)
                    dve.wait_ge(moe_hid, hcount)
                    nc.vector.tensor_tensor(o, bank(n % 6, 320), o, ALU.mult).then_inc(moe_hid, 1)
                    hcount += 1
            for s in range(S):
                dve.wait_ge(down_mm, S + s + 1)
                nc.vector.tensor_tensor(tok(H[0], s), bank(s % 2, C), tok(H[1], s), ALU.add).then_inc(down_read, 1)
                dve.wait_ge(down_read, S + s + 1)
                res_ln(2 * S + 2 + s, tok(H[0], s), tok(H[0], s))


def constants():
    p = np.arange(P)
    slot = p % 32
    own = ((slot[:, None] // S == np.arange(GI)[None]) & (slot[:, None] < GI * S)).astype(np.float32)
    onehot = np.zeros((32, S, P), np.float32)
    for j in range(S):
        n = slot % S - j
        bucket = np.where(n < 0, 16, 0) + np.abs(n)
        onehot[bucket, j, p] = 1.0
    lower = np.tril(np.ones((NE, NE), np.float32), -1)
    pick = np.zeros((NE, NE // 2, P), np.float32)
    for e in range(NE):
        pick[e, e // 2, (e % 2) * EH:(e % 2 + 1) * EH] = 1.0
    return {"c_ident": np.eye(P, dtype=np.float32), "c_own": own, "c_onehot": onehot.reshape(32, S * P),
            "c_ties": lower, "c_ties4": lower[0:4, 0:4].copy(), "c_pick": pick.reshape(NE, NE // 2 * P)}


_UNUSED = ("L0_tok_pixel_masks",)


def kernel(**inputs):
    import concourse.bacc as _bacc
    from concourse.bass_utils import run_bass_kernel_spmd as _run

    nc = _bacc.Bacc("TRN2", target_bir_lowering=False, num_devices=1)
    arrays, args = {}, {}
    for name, value in list(inputs.items()) + list(constants().items()):
        if name in _UNUSED:
            continue
        v = np.ascontiguousarray(value)
        arrays[f"in_{name}_dram"] = v
        args[name] = nc.dram_tensor(f"in_{name}_dram", v.shape, mybir.dt.from_np(v.dtype), kind="ExternalInput").ap()
    out = nc.dram_tensor("out_0_dram", (P, S, C), F32, kind="ExternalOutput").ap()
    bass_vit_tower(nc, args, out)
    r = _run(nc, [arrays], core_ids=[0])
    return r.results[0]["out_0_dram"]
```

```python
from contextlib import ExitStack

import numpy as np

import concourse.bass as bass
from concourse import mybir

F32 = mybir.dt.float32
F32R = mybir.dt.float32r
ALU = mybir.AluOpType
ACT = mybir.ActivationFunctionType
AX = mybir.AxisListType

P = 128
C = 256
KC = C // P
IMG, CH, PS = 96, 3, 14
GP = IMG // PS
NP_ = GP * GP
WS = 3
NW = (GP // WS) ** 2
NPOS = WS * WS
S = NW + 1
LH, LD = 8, 32
NH, DK = 16, 64
INNER = NH * DK
FF = 768
QB, NB = 32, 48
NE, EH, SH = 16, 64, 512
GI = 6
NG = 24
NT = 6
SLOTS = NG * 32
FULLG = P // GI
RESTI = P - FULLG * GI
EPS = 1e-5
MAGIC = 1.5 * 2.0 ** 23
BIG = 1e30
RW = 35200
XROWS = 3

PIX = CH * PS * PS
NK = -(-PIX // P)
CK = -(-PIX // NK)
PIXP = NK * CK
NBATCH = NP_ * NK // 4
XT = 4
ZSLOTS = 2 * NPOS


KVN = -(-NPOS // 2)

def group_place(g):
    w = g // WS
    return w // (GP // WS) * WS + g % WS, w % (GP // WS) * WS


def last_batch(t):
    return (t * NK + NK - 1) // 4


def patches_of(i):
    first = i // KVN * NPOS + i % KVN * 2
    return range(first, min(first + 2, (i // KVN + 1) * NPOS))


def pair_of(t):
    return t // NPOS * KVN + t % NPOS // 2


def tok_schedule():
    at = [(-1.0, "cls", 0), (-0.99, "cls root", 0), (-0.98, "cls z", 0), (0.05, "clsT", 0), (0.5, "gq", 0)]
    batch = 0
    for t in range(NP_):
        if t == 0:
            at.append((-0.9, "pack", 0))
        if t % WS == 0 and t // WS + 1 < NP_ // WS:
            at.append((t + 0.0, "pack", t // WS + 1))
        while batch <= last_batch(min(t + 1, NP_ - 1)):
            at.append((t + 0.1, "turn", batch))
            batch += 1
        at.append((t + 0.3, "conv", t))
        if t % WS == WS - 1:
            at += [(t + 0.6, "stat", t // WS), (t + 0.61, "stat root", t // WS), (t + 0.62, "stat z", t // WS)] if t == NP_ - 1 else [
                (t + 0.6, "stat", t // WS), (t + 0.6 + 0.4, "stat root", t // WS), (t + 0.6 + 1.0, "stat z", t // WS)]
    turned = []
    for i in range(NW * KVN):
        t = patches_of(i)[-1] // WS * WS + WS - 1 + 2 + 0.7
        if patches_of(i)[-1] // WS == NP_ // WS - 1:
            t = turned[-1] + 0.8
            turned.append(t)
        else:
            turned.append(max(t, turned[-1] + 1) if turned else t)
        at.append((turned[i], "zturn", i))
    for w in range(NW):
        end = (w + 1) * NPOS
        red = end - 0.4 + 0.5
        at += [(red, "red", w), (red + 0.25, "red root", w), (red + 0.3, "red z", w),
               (end + 0.95, "bias", w), (end + 1.2, "redT", w), (end + 1.5, "q", w)]
        for m in range(KVN):
            kv = turned[w * KVN + m] + 0.7
            at.append((kv, "kv", w * KVN + m))
        agg = kv + 2.6
        at += [(kv + 0.6, "qk", w), (kv + 0.9, "soft", w), (kv + 1.2, "soft exp", w), (kv + 1.25, "soft norm", w),
               (kv + 1.26, "pv", w), (agg, "agg", w), (agg + 0.4, "aggT", w), (agg + 1.1, "proj", w),
               (agg + 1.15, "loz", w), (agg + 1.4, "loz root", w), (agg + 1.42, "loz z", w), (agg + 1.44, "loT", w),
               (agg + 2.1, "lozT", w), (agg + 2.4, "mod", w), (agg + 3.1, "gkv", w)]
    at += [(24.5, "bias", NW), (agg + 4, "gsoft", 0), (agg + 4.1, "gsoft exp", 0), (agg + 4.2, "gsoft norm", 0), (agg + 5, "gaggT", 0), (agg + 6, "gproj", 0)]
    at += [(NP_ - 0.3, "hzero", 0), (turned[-3] + 0.75, "hturn", 0), (turned[-2] + 0.6, "hturn", 1), (turned[-1] + 0.5, "hturn", 2),
           (agg + 3.15, "hturn", 3), (agg + 6.5, "hturn", 4)]
    for m in range(3):
        at += [(19.9 + 3 * m, "quant", m), (19.9 + 2 + 3 * m, "round", m)]
    for b in range(FFN_BATCHES):
        at.append((kv + 0.1 if b < 2 else kv + 1.36 if b < 7 else agg + 1.6, "turnw", b))
    at.sort(key=lambda e: e[0])
    steps = [(name, i) for _, name, i in at]
    w, g, m = NW - 1, NP_ // WS - 1, NW * KVN - 1
    tail = [("hzero", 0), ("mod", w - 1), ("zturn", m - 2), ("stat", g), ("stat root", g), ("kv", m - 3), ("stat z", g),
            ("zturn", m - 1), ("red", w), ("red root", w), ("gkv", w - 1), ("kv", m - 2), ("red z", w), ("redT", w),
            ("kv", m - 1), ("zturn", m), ("q", w), ("kv", m), ("bias", w), ("qk", w)]
    weights = [("turnw", b) for b in range(FFN_BATCHES)]
    tail += weights[:TURNW[0]]
    tail += [("soft", w), ("soft exp", w), ("soft norm", w), ("pv", w), ("hturn", 0), ("hturn", 1), ("agg", w)]
    halves = [("split qk", n) for n in range(4)]
    tail += weights[TURNW[0]:TURNW[1]] + [("hturn", 2)]
    tail += [("aggT", w), ("proj", w), ("loz", w), ("loz root", w), ("loz z", w), ("loT", w)] + halves[:2] + weights[TURNW[1]:TURNW[2]]
    tail += [("lozT", w), ("mod", w), ("gkv", w)] + halves[2:] + weights[TURNW[2]:TURNW[3]]
    tail += [("gsoft", 0), ("gsoft exp", 0), ("hturn", 3), ("gsoft norm", 0)] + weights[TURNW[3]:]
    tail += [("gaggT", 0), ("gproj", 0), ("hturn", 4)]
    left = [e for e in steps if e not in tail]
    behind = left.index(("conv", NP_ - 1)) + 1
    assert behind == len(left), left[behind:]
    return left + tail


FFN_BATCHES = 3 * NB * QB // (4 * P)
TURNW = (2,5,7,9)
QK_FIRST = 6
PV_POOL = [NPOS] * (NW - 1) + [3]


def DVE_TURNS(batch):
    return batch % 2 == 1


TOK = tok_schedule()
READERS = {"clsT": "d", "gq": "d", "redT": "d", "q": "d", "aggT": "a", "proj": "d", "loT": "a",
           "mod": "d", "lozT": "d", "gkv": "d", "gaggT": "d", "gproj": "d"}
SHARED = [s for s in TOK if s[0] in READERS]
SHARED_NO = {s: n for n, s in enumerate(SHARED)}


def product3(pe, rounded, out, left, right):
    terms = [(l[i], r[j]) for l, r in zip(left, right) for i, j in ((0, 0), (0, 1), (1, 0))]
    for n, (l, r) in enumerate(terms):
        m = pe.matmul(out, rounded(l), rounded(r), start=(n == 0), stop=(n == len(terms) - 1))
    return m


def bass_vit_tower(nc, a, out):
    with ExitStack() as ctx:
        def sb(name, cols):
            return ctx.enter_context(nc.sbuf_tensor(name, [P, cols], F32))

        names = {}

        def sem(name):
            names[name] = ctx.enter_context(nc.semaphore(name))
            return names[name]

        ident = sb("ident", P)
        own = sb("own", GI)
        ties = sb("ties", NE * NE)
        ties4 = sb("ties4", 16)
        ones = sb("ones", P)
        H = [sb("HA", S * C), sb("HB", S * C)]
        vec_rows = sb("vec_rows", P)
        vec = sb("vec", 16)
        proj_b = sb("proj_b", C)
        gproj_b = sb("gproj_b", C)
        mod_b = sb("mod_b", C)
        cls = sb("cls_row", C)
        corr = sb("corr", NE)
        relb = sb("relb", NE)
        small = sb("small", 880)
        small_at = [0]

        def tiny(n):
            at = small_at[0]
            small_at[0] += n
            assert small_at[0] <= 880
            return small[:, at:at + n]

        ffn_nat = sb("ffn_nat", 3 * NB * QB)

        ATTN = 4 * 2048
        gaps = [0]

        def place(at, n, dtype=F32):
            assert at % 8 == 0 and at + n <= ATTN + RW, (at, n)
            gaps[0] += 1
            with ExitStack() as held:
                if at:
                    held.enter_context(nc.sbuf_tensor(f"gap{gaps[0]}", [P, at], F32))
                return held.enter_context(nc.sbuf_tensor(f"at{at}_{gaps[0]}", [P, n], dtype))[:, :]

        buffers, twins = {}, {}

        def rounded(ap):
            name = ap.tensor.name
            if name not in twins:
                twins[name] = place(*buffers[name], F32R).tensor
            return bass.AP(tensor=twins[name], offset=ap.offset, ap=ap.ap)

        def place_at(at, n):
            v = place(at, n)
            buffers[v.tensor.name] = (at, n)
            return v

        def area(start):
            at = [start]

            def take(n):
                v = place_at(ATTN + at[0], n)
                at[0] += -(-n // 8) * 8
                return v

            take.at = at
            return take

        def at_now(take):
            return take.at[0]

        take = area(0)
        xring = [take(CH * PS * IMG), take(CH * PS * IMG), place_at(0, CH * PS * IMG)]
        xring = [v.rearrange("p (c r x) -> p c r x", c=CH, r=PS) for v in xring]
        xpack = [take(WS * PIXP) for _ in range(2)]
        zT = take(ZSLOTS * C).rearrange("p (t k n) -> p t k n", t=ZSLOTS, k=KC)
        xT = [take(4 * P) for _ in range(XT)]
        pes = [take(WS * C) for _ in range(2)]
        convT = take(NK * C).rearrange("p (k n) -> p k n", k=NK)
        kwin = take(NPOS * C)
        vwin = take(NPOS * C)
        prod = take(NPOS * C)
        def tok_weight(at, n):
            return place_at(4096 + at, KC * n).rearrange("p (k n) -> p k n", k=KC)

        g_wq, t_wq, t_proj, g_proj = (tok_weight(i * KC * C, C) for i in range(4))
        t_wkv, g_wkv = tok_weight(4 * KC * C, 2 * C), tok_weight(6 * KC * C, 2 * C)
        t_mod = take(KC * C).rearrange("p (k n) -> p k n", k=KC)
        conv_nat = zT.rearrange("p t k n -> p (t k n)")[:, (ZSLOTS - 1) * C - KC * PIXP:(ZSLOTS - 1) * C].rearrange("p (k n) -> p k n", k=KC)
        zgrp = [take(WS * C) for _ in range(2)]
        red = take(NW * C).rearrange("p (w n) -> p w n", w=NW)
        tmp = take(C)
        lnz = take(C)
        trn = take(C).rearrange("p (k n) -> p k n", k=KC)
        trn2 = take(C).rearrange("p (k n) -> p k n", k=KC)
        trn3 = take(C).rearrange("p (k n) -> p k n", k=KC)
        qwin = take(C)
        agg = take(C)
        lo = take(C)
        gq = take(C)
        gv = take(NW * C)

        psum = ctx.enter_context(nc.psum_tensor("psum", [P, 8 * 512], F32))

        def bank(b, n=512, at=0):
            return psum[:, b * 512 + at:b * 512 + at + n]

        st3, mv3, rs3 = tiny(WS * 6), tiny(WS * 2), tiny(WS)
        rc3 = tiny(WS)
        st1, mv1, rc1, rs1 = tiny(6), tiny(2), tiny(1), tiny(1)
        sc = tiny(NPOS * LH)
        mx8, sm8, rs8 = tiny(LH), tiny(LH), tiny(LH)
        gs = tiny(NW * LH)
        zero_col = tiny(1)

        ld_conv, ld_ident, ld_vec = sem("ld_conv"), sem("ld_ident"), sem("ld_vec")
        ld_x = [sem(f"ld_x{i}") for i in range(XROWS)]
        ld_cls, ld_tokw, ld_small, ld_attnw, ld_ffn = sem("ld_cls"), sem("ld_tokw"), sem("ld_small"), sem("ld_attnw"), sem("ld_ffn")
        dve_chain, act_chain, zero_set = sem("dve_chain"), sem("act_chain"), sem("zero_set")
        ones_set = sem("ones_set")
        conv_turned, conv_kept = sem("conv_turned"), sem("conv_kept")
        vec_turned, vec_kept = sem("vec_turned"), sem("vec_kept")
        pads_zero = sem("pads_zero")
        turned, turned_kept_act, turned_kept_dve = sem("turned"), sem("turned_kept_act"), sem("turned_kept_dve")
        packed = sem("packed")
        conv_done, conv_kept_sb = sem("conv_done"), sem("conv_kept_sb")
        var_ready, rstd_ready = sem("var_ready"), sem("rstd_ready")
        z_ready, z_turned, z_kept = sem("z_ready"), sem("z_turned"), sem("z_kept")
        win_ready, win_read = sem("win_ready"), sem("win_read")
        k_ready, k_read, v_ready, v_read = sem("k_ready"), sem("k_read"), sem("v_ready"), sem("v_read")
        ln_var, ln_rstd, ln_z, ln_kept = sem("ln_var"), sem("ln_rstd"), sem("ln_z"), sem("ln_kept")
        shifted, exp_done, probs_ready = sem("shifted"), sem("exp_done"), sem("probs_ready")
        qk_done, pv_done, agg_ready = sem("qk_done"), sem("pv_done"), sem("agg_ready")
        aggT_kept, lo_ready, loT_kept = sem("aggT_kept"), sem("lo_ready"), sem("loT_kept")
        tok_tail = sem("tok_tail")

        block = ctx.enter_context(nc.Block())

        LN = {s: n for n, s in enumerate(s for s in TOK if s[0] in ("cls", "red", "loz"))}
        LNT = {"clsT": "cls", "redT": "red", "lozT": "loz"}
        SM = {s: n for n, s in enumerate(s for s in TOK if s[0] in ("soft", "gsoft"))}
        AGG = {s: n for n, s in enumerate(s for s in TOK if s[0] in ("agg", "gsoft"))}
        AGGT = {s: n for n, s in enumerate(s for s in TOK if s[0] in ("aggT", "gaggT"))}

        def shared(step):
            return SHARED_NO[step], bank(7)

        def pixels(chunk):
            t, j = chunk // NK, chunk % NK
            at = t % WS * PIXP + j * CK
            return xpack[t // WS % 2][:, at:at + CK]

        def kept_by(b):
            dve = sum(DVE_TURNS(i) for i in range(b))
            return b - dve, dve

        def batches_of_pixels_kept(eng, b):
            for done, n in zip((turned_kept_act, turned_kept_dve), kept_by(b)):
                if n:
                    eng.wait_ge(done, n)

        take = area(0)
        ffnT = take(3 * 12 * P)
        HT_AT = at_now(take)
        hT = take(KC * SLOTS).rearrange("p (k n) -> p k n", k=KC)
        hT_lo = take(KC * SLOTS).rearrange("p (k n) -> p k n", k=KC)
        qT = take(8 * SLOTS).rearrange("p (k n) -> p k n", k=8)
        kT = take(8 * SLOTS).rearrange("p (k n) -> p k n", k=8)
        V_AT = at_now(take)
        V = take(NT * INNER).rearrange("p (t n) -> p t n", t=NT)
        ctx_area = take(8 * S * P)
        ctxT = ctx_area.rearrange("p (c s n) -> p c s n", c=8, s=S)
        onehot = ctx_area[:, 0:S * P]
        SM_AT = at_now(take)
        smask = take(2 * NH * 30)
        late = area(HT_AT)
        pexp = late(2 * NH * 32)
        PT_AT = at_now(take)
        pT = [t(NH * P).rearrange("p (h x) -> p h x", h=NH) for t in (late, take)]
        assert at_now(late) <= HT_AT + 2 * KC * SLOTS
        bias = take(S * NH)
        att = take(2 * NH * S)
        att_mx, att_sm = take(2 * NH), take(2 * NH)
        take = area(V_AT)
        w_q_hi, w_k_hi = (take(2048).rearrange("p (k n) -> p k n", k=KC) for _ in range(2))
        take = area(PT_AT)
        w_v_hi = take(2048).rearrange("p (k n) -> p k n", k=KC)
        w_q = place_at(0, 2048).rearrange("p (k n) -> p k n", k=KC)
        w_k = place_at(2048, 2048).rearrange("p (k n) -> p k n", k=KC)
        w_v = place_at(4096, 2048).rearrange("p (k n) -> p k n", k=KC)
        w_o = place_at(6144, 2048).rearrange("p (k n) -> p k n", k=8)
        upT = ffnT[:, 0:1536].rearrange("p (k n) -> p k n", k=KC)
        gateT = ffnT[:, 1536:3072].rearrange("p (k n) -> p k n", k=KC)
        downT = ffnT[:, 3072:4608].rearrange("p (k n) -> p k n", k=6)
        ffn_abs = tiny(3 * NB)
        ffn_inv = tiny(3 * NB)

        take = area(3 * 12 * P)
        h1T = take(KC * S * P).rearrange("p (k n) -> p k n", k=KC)
        h1q = take(S * C)
        up = take(6 * S * P)
        gate = take(6 * S * P)
        sig = take(6 * S * P)
        l1nat = take(3 * KC * C)
        shnat = take(3 * 4 * C)
        rnat = take(C)
        l1T = take(KC * 3 * C).rearrange("p (k n) -> p k n", k=KC)
        shT = take(2 * KC * SH).rearrange("p (a k n) -> p a k n", a=2, k=KC)
        rT = take(KC * NE).rearrange("p (k n) -> p k n", k=KC)
        F_AT = at_now(take)
        e_gate = place_at(0, 2048).rearrange("p (k e n) -> p k e n", k=KC, e=NE)
        e_up = place_at(2048, 2048).rearrange("p (k e n) -> p k e n", k=KC, e=NE)
        e_down = place_at(4096, 2048).rearrange("p (k n) -> p k n", k=8)
        sdT = place_at(6144, 1024).rearrange("p (k n) -> p k n", k=4)
        pick = place_at(7168, 1024).rearrange("p (k n) -> p k n", k=8)
        take = area(F_AT)
        h1T_hi = take(KC * S * P).rearrange("p (k n) -> p k n", k=KC)
        take = area(SM_AT)
        ug_hi = take(2 * KC * FF)
        upT_hi, gateT_hi = (ug_hi[:, i * KC * FF:(i + 1) * KC * FF].rearrange("p (k n) -> p k n", k=KC) for i in range(2))
        take = area(F_AT)
        e_gate_hi, e_up_hi = (take(2048).rearrange("p (k e n) -> p k e n", k=KC, e=NE) for _ in range(2))
        shT_hi = take(2 * KC * SH).rearrange("p (a k n) -> p a k n", a=2, k=KC)
        h3T_hi = take(KC * S * P).rearrange("p (k n) -> p k n", k=KC)
        rT_hi = take(KC * NE).rearrange("p (k n) -> p k n", k=KC)
        take = area(3 * 12 * P)
        h2T = take(KC * S * P).rearrange("p (k n) -> p k n", k=KC)
        qkv = take(S * 3 * C).rearrange("p (s n) -> p s n", s=S)
        h3T = take(KC * S * P).rearrange("p (k n) -> p k n", k=KC)
        hid = take(12 * S * P).rearrange("p (k n) -> p k n", k=12)
        sil = [take(320) for _ in range(2)]
        cmp_a = take(S * NE * NE)
        cmp_b = take(S * NE * NE)
        combT = take(S * P)
        front = place_at(ATTN, 7 * S * P).rearrange("p (c n) -> p c n", c=7)
        assert 7 * S * P <= 3 * 12 * P
        behind = place_at(ATTN + 3 * 12 * P, 5 * S * P).rearrange("p (c n) -> p c n", c=5)
        e_down_hi = place_at(ATTN + at_now(take), 2048).rearrange("p (k n) -> p k n", k=8)
        sdT_hi = place_at(ATTN + 3 * 12 * P + 5 * S * P, 1024).rearrange("p (k n) -> p k n", k=4)
        assert 5 * S * P + 1024 <= KC * S * P + S * 3 * C and at_now(take) + 2048 <= F_AT - 2 * KC * SH - KC * NE

        def hid_hi(c):
            return front[:, c] if c < 7 else behind[:, c - 7]

        scr = hid.rearrange("p k n -> p (k n)")[:, 0:S * (S + 1) // 2 * C].rearrange("p (i n) -> p i n", n=C)
        assert KC * S * P * 2 + S * 3 * C + 12 * S * P + 640 + 2 * S * NE * NE + S * P <= (
            KC * S * P + S * C + 3 * 6 * S * P + 3 * KC * C + 3 * 4 * C + C)
        msc = tiny(S * S)
        mmx, msm = tiny(S), tiny(S)
        st5, mv5, rc5, rs5 = tiny(3 * 6), tiny(3 * 2), tiny(3), tiny(3)
        pmax, gm, qsc, qinv, fold = tiny(12), tiny(1), tiny(5), tiny(5), tiny(4)

        tok_end_act, tok_end_dve = sem("tok_end_act"), sem("tok_end_dve")
        hT_zero, hT_turned, hT_hi_set, hT_kept = sem("hT_zero"), sem("hT_turned"), sem("hT_hi_set"), sem("hT_kept")
        bias_mm, bias_ready = sem("bias_mm"), sem("bias_ready")
        qkv_mm, qkv_kept_act, qkv_kept_dve = sem("qkv_mm"), sem("qkv_kept_act"), sem("qkv_kept_dve")
        score_mm, score_read = sem("score_mm"), sem("score_read")
        att_shift, att_exp, pT_ready = sem("att_shift"), sem("att_exp"), sem("pT_ready")
        ctx_mm, ctx_kept_act, ctx_kept_dve = sem("ctx_mm"), sem("ctx_kept_act"), sem("ctx_kept_dve")
        wo_mm, wo_read = sem("wo_mm"), sem("wo_read")
        ffn_scale, ffn_over, ffn_rounded, ffn_quant = (sem("ffn_scale"), sem("ffn_over"), sem("ffn_rounded"),
                                                       sem("ffn_quant"))
        pexp_zero, pT_zero = sem("pexp_zero"), sem("pT_zero")
        ld_qk, qk_hi, qk_lo, v_hi, v_lo = sem("ld_qk"), sem("qk_hi"), sem("qk_lo"), sem("v_hi"), sem("v_lo")
        ug_hi_set, ug_lo_set, ew_hi_set, ew_lo_set = sem("ug_hi_set"), sem("ug_lo_set"), sem("ew_hi_set"), sem("ew_lo_set")
        hid_hi_set, hid_lo_set = sem("hid_hi_set"), sem("hid_lo_set")
        last_hi_set, last_lo_set = sem("last_hi_set"), sem("last_lo_set")
        wt_turned, wt_kept = sem("wt_turned"), sem("wt_kept")
        rln_var, rln_rstd, h_ready = sem("rln_var"), sem("rln_rstd"), sem("h_ready")
        ld_l1, ld_moe = sem("ld_l1"), sem("ld_moe")
        gmax_part, gmax_row, gmax_one, gmax_all = sem("gmax_part"), sem("gmax_row"), sem("gmax_one"), sem("gmax_all")
        hq_ready, hT2_turned, hT2_kept_act, hT2_kept_dve = (sem("hq_ready"), sem("hT2_turned"),
                                                             sem("hT2_kept_act"), sem("hT2_kept_dve"))
        ff_mm, ff_kept, ff_max = sem("ff_mm"), sem("ff_kept"), sem("ff_max")
        gate_q, sig_ready, o_ready = sem("gate_q"), sem("sig_ready"), sem("o_ready")
        tok_max, sig_made, q_third, third_scaled = sem("tok_max"), sem("sig_made"), sem("q_third"), sem("third_scaled")
        down_mm, down_read = sem("down_mm"), sem("down_read")
        l1_mm, l1_kept, l1_shift, l1_exp = sem("l1_mm"), sem("l1_kept"), sem("l1_shift"), sem("l1_exp")
        r_mm, r_sig, comb_ready, combT_mm, combT_kept = (sem("r_mm"), sem("r_sig"), sem("comb_ready"), sem("combT_mm"),
                                                         sem("combT_kept"))
        moe_mm, moe_sil, moe_hid = sem("moe_mm"), sem("moe_sil"), sem("moe_hid")
        stored = sem("stored")

        def ffn_matrix(m):
            return (ffn_nat[:, m * NB * QB:(m + 1) * NB * QB].rearrange("p (b n) -> p b n", n=QB),
                    slice(m * NB, (m + 1) * NB))

        def weigh_values(tensor_tensor, lo_, hi_):
            n = hi_ - lo_
            return tensor_tensor(prod[:, lo_ * C:hi_ * C].rearrange("p (kh d) -> p kh d", d=LD),
                                 vwin[:, lo_ * C:hi_ * C].rearrange("p (kh d) -> p kh d", d=LD),
                                 sc[:, lo_ * LH:hi_ * LH].unsqueeze(2).to_broadcast([P, n * LH, LD]), ALU.mult)

        def weight_batches():
            def blocks(src, at, width, o, k):
                return src[:, at + o * width + k * P:at + o * width + (k + 1) * P]

            batches = []
            def six(src, at, dst):
                for k in range(KC):
                    batches.append(([blocks(src, at, C, o, k) for o in range(4)], dst[:, k, 0:512]))
                batches.append(([blocks(src, at, C, o, k) for k in range(KC) for o in (4, 5)], dst[:, :, 512:768]))

            def pairs(src, at, width, dst):
                for k in range(0, width // P, 2):
                    batches.append(([blocks(src, at, width, o, kk) for kk in (k, k + 1) for o in range(KC)], dst[:, k:k + 2, :]))

            six(ffn_nat, 0, upT)
            six(ffn_nat, 1536, gateT)
            pairs(ffn_nat, 3072, FF, downT)
            assert len(batches) == FFN_BATCHES
            six(l1nat, 0, l1T)
            for m in range(2):
                for k in range(KC):
                    batches.append(([blocks(shnat, m * 1024, C, o, k) for o in range(4)], shT[:, m, k, :]))
            pairs(shnat, 2048, SH, sdT)
            batches.append(([rnat[0:NE, k * P:(k + 1) * P] for k in range(KC)], rT))
            return batches

        WB = weight_batches()

        def wb_bank(b):
            return (2 if b < FFN_BATCHES else 0) + b % 2

        def turn_batch(pe, b):
            if b >= 2:
                batches_kept(pe, b - 1)
            for i, src in enumerate(WB[b][0]):
                rows = src.shape[0]
                m = pe.transpose(bank(wb_bank(b), rows, i * rows), src, ident[0:rows, 0:rows])
            m.then_inc(wt_turned, 1)

        def keep_batch(eng, copy, b, done):
            eng.wait_ge(wt_turned, b + 1)
            dst = WB[b][1]
            v = bank(wb_bank(b), dst.shape[-1] * (dst.shape[1] if len(dst.shape) == 3 else 1))
            if len(dst.shape) == 3:
                v = v.rearrange("p (k n) -> p k n", k=dst.shape[1])
            copy(dst, v).then_inc(done, 1)

        def batches_kept(eng, n):
            eng.wait_ge(wt_kept, n)

        MOE = []
        for c in range(13):
            for hf in range(2):
                if c < 12:
                    MOE += [("gate", c, hf), ("up", c, hf)]
                if c >= 5:
                    MOE.append(("comb", c - 1, hf))
        FINAL = [n for n, (kind, c, hf) in enumerate(MOE) if kind == "comb" or (kind == "up" and c < 4)]
        FIRST_COMB = [m[0] for m in MOE].index("comb")

        def moe_count(n, kind):
            return sum(m[0] == kind for m in MOE[:n])

        comb_w = tiny(S * NE)

        def tokens_kept(eng, stage, n):
            if stage == 1:
                eng.wait_ge(hT2_kept_dve, S + (n + 1) // 2)
                eng.wait_ge(hT2_kept_act, 2 + n // 2)
            else:
                eng.wait_ge(hT2_kept_dve, (0 if stage == 0 else S + 3) + n)

        def keep_token(eng, copy, dst, stage, s, done):
            eng.wait_ge(hT2_turned, stage * S + s + 1)
            return copy(dst[:, :, s * P:(s + 1) * P], bank(s % 2, C).rearrange("p (k n) -> p k n", k=KC)).then_inc(done, 1)

        def ff_bank(n):
            return (n + 2) % 6

        def qk_half(n):
            w, hi = ((w_q, w_q_hi), (w_k, w_k_hi))[n % 2]
            cols = slice(n // 2 * 512, (n // 2 + 1) * 512)
            return w[:, :, cols], hi[:, :, cols]

        def hT_pieces(s):
            hv, lv = (x.rearrange("p k (g x) -> p k g x", x=32) for x in (hT, hT_lo))
            pieces = []
            for k in range(KC):
                hi_, lo_ = (x[:, k, 0:FULLG, 0:30].rearrange("p g (i s) -> p g i s", s=S)[:, :, :, s] for x in (hv, lv))
                pieces.append((hi_, lo_, bank(s % 2, P, k * P)[:, 0:FULLG * GI].rearrange("p (g i) -> p g i", i=GI)))
            hi_, lo_ = (x[:, :, FULLG, s:s + S + 1:S] for x in (hv, lv))
            pieces.append((hi_, lo_, bank(s % 2, C).rearrange("p (k n) -> p k n", k=KC)[:, :, FULLG * GI:P]))
            return pieces

        def qkv_copy(copy, n):
            if n < 32:
                c, w, hf = n // 4, n // 2 % 2, n % 2
                return copy((qT, kT)[w][:, c, hf * 384:(hf + 1) * 384], bank(2 + n % 4, 384))
            t, hf = (n - 32) // 2, n % 2
            return copy(V[:, t, hf * 512:(hf + 1) * 512], bank(2 + n % 4))

        def score_bank(half):
            return psum[:, (0, 6)[half] * 512:(0, 6)[half] * 512 + 1024].rearrange("p (h x) -> p h x", x=P)

        def ctx_copy(copy, eng, done, t, half):
            eng.wait_ge(ctx_mm, 2 * t + half + 1)
            src = bank(2 + t % 2 * 2 + half).rearrange("p (c g x) -> p c g x", g=4, x=32)
            first = 4 * t * GI
            full = min(4, FULLG - 4 * t)
            for c in range(4):
                d = ctxT[:, half * 4 + c, :, :]
                m = copy(d[:, :, first:first + full * GI].rearrange("p s (g i) -> p g i s", i=GI),
                         src[:, c, 0:full, 0:GI * S].rearrange("p g (i s) -> p g i s", s=S))
            if full < 4:
                at = first + full * GI
                m = copy(ctxT[:, half * 4:half * 4 + 4, :, at:at + RESTI].rearrange("p c s i -> p c i s"),
                         src[:, :, full, 0:RESTI * S].rearrange("p c (i s) -> p c i s", s=S))
            m.then_inc(done, 1)

        sb_ = tiny(S * NE)
        pairs = cmp_b
        gsum, grank = tiny(S * 4), tiny(S * 4)
        rank, wsum = tiny(S * NE), tiny(S)

        def route(dve, link):
            s3 = comb_w.rearrange("p (s e) -> p s e", e=NE)
            b3 = sb_.rearrange("p (s e) -> p s e", e=NE)
            b4 = sb_.rearrange("p (g e) -> p g e", e=4)
            link(nc.vector.tensor_tensor(b3, s3, corr[:, :].unsqueeze(1).to_broadcast([P, S, NE]), ALU.add))
            pr = pairs[:, 0:S * 4 * 6].rearrange("p (g x) -> p g x", x=6)
            nc.vector.tensor_tensor(pr[:, :, 0:3], b4[:, :, 0:3], b4[:, :, 1:4], ALU.add)
            nc.vector.tensor_tensor(pr[:, :, 3:5], b4[:, :, 0:2], b4[:, :, 2:4], ALU.add)
            link(nc.vector.tensor_tensor(pr[:, :, 5:6], b4[:, :, 0:1], b4[:, :, 3:4], ALU.add))
            link(nc.vector.tensor_reduce(gsum, pr, AX.X, ALU.max))

            def ranks(v, n, tie, out_):
                x = v.rearrange("p (s e) -> p s e", e=n)
                for s in range(S):
                    ga = cmp_a[:, s * n * n:(s + 1) * n * n].rearrange("p (i j) -> p i j", j=n)
                    gb = cmp_b[:, s * n * n:(s + 1) * n * n].rearrange("p (i j) -> p i j", j=n)
                    other = x[:, s, :].unsqueeze(1).to_broadcast([P, n, n])
                    mine = x[:, s, :].unsqueeze(2).to_broadcast([P, n, n])
                    nc.vector.tensor_tensor(ga, other, mine, ALU.is_gt)
                    m = nc.vector.tensor_tensor(gb, other, mine, ALU.is_equal)
                link(m)
                gb = cmp_b[:, 0:S * n * n].rearrange("p (s x) -> p s x", s=S)
                link(nc.vector.tensor_tensor(gb, gb, tie[:, 0:n * n].unsqueeze(1).to_broadcast([P, S, n * n]), ALU.mult))
                ga = cmp_a[:, 0:S * n * n]
                link(nc.vector.tensor_tensor(ga, ga, cmp_b[:, 0:S * n * n], ALU.add))
                link(nc.vector.tensor_reduce(out_, ga.rearrange("p (i j) -> p i j", j=n), AX.X, ALU.add))

            ranks(gsum, 4, ties4, grank)
            link(nc.vector.tensor_scalar(grank, grank, 2.0, -BIG, ALU.is_ge, ALU.mult))
            link(nc.vector.tensor_tensor(b4, b4, grank.unsqueeze(2).to_broadcast([P, S * 4, 4]), ALU.add))
            ranks(sb_, NE, ties, rank)
            link(nc.vector.tensor_scalar(rank, rank, 4.0, None, ALU.is_lt))
            link(nc.vector.tensor_tensor(comb_w, comb_w, rank, ALU.mult))
            link(nc.vector.tensor_reduce(wsum, s3, AX.X, ALU.add))
            link(nc.vector.tensor_scalar(wsum, wsum, 1e-20, None, ALU.add))
            link(nc.vector.reciprocal(wsum, wsum))
            nc.vector.tensor_tensor(s3, s3, wsum.unsqueeze(2).to_broadcast([P, S, NE]), ALU.mult).then_inc(comb_ready, 1)

        @block.sync
        def _(sp):
            sp.dma_start(ident[:, :], a["c_ident"]).then_inc(ld_ident, 16)
            sp.dma_start(conv_nat[:, :, 0:PIX], a["L0_tok_conv_w"].rearrange("(k p) c r x -> p k (c r x)", p=P)).then_inc(ld_conv, 16)

            def row(r):
                x = a["x"][:, :, r * PS:(r + 1) * PS, :].rearrange("b c r x -> b c (r x)")
                sp.dma_start(xring[r % XROWS].rearrange("p c r x -> p c (r x)"), x).then_inc(ld_x[r % XROWS], 16)

            row(0)
            for i, n in enumerate(("la_ln_q_g", "la_ln_q_b", "la_ln_kv_g", "la_ln_kv_b", "ga_ln_q_g", "ga_ln_q_b",
                                   "ga_ln_kv_g", "ga_ln_kv_b")):
                sp.dma_start(vec_rows[2 * i:2 * i + 2, :], a["L0_tok_" + n].rearrange("(k p) -> k p", p=P)).then_inc(ld_vec, 16)
            sp.dma_start(cls[:, :], a["L0_tok_class_emb"].partition_broadcast(P)).then_inc(ld_cls, 16)
            sp.dma_start(g_wq, a["L0_tok_ga_wq"].rearrange("(k p) n -> p k n", p=P)).then_inc(ld_cls, 16)
            row(1)
            row(2)
            for t, n in ((proj_b, "la_proj_b"), (gproj_b, "ga_proj_b"), (mod_b, "mod_b")):
                sp.dma_start(t[:, :], a["L0_tok_" + n].partition_broadcast(P)).then_inc(ld_tokw, 16)
            for t, n in ((t_wq, "la_wq"), (t_wkv, "la_wkv"), (t_proj, "la_proj_w"), (g_wkv, "ga_wkv"),
                         (g_proj, "ga_proj_w"), (t_mod, "mod_w")):
                sp.dma_start(t, a["L0_tok_" + n].rearrange("(k p) n -> p k n", p=P)).then_inc(ld_tokw, 16)
            for r in range(XROWS, GP):
                sp.wait_ge(packed, WS + r - XROWS + 1)
                row(r)
            sp.dma_start(corr[:, :], a["L1_ffn_correction_bias"].partition_broadcast(P)).then_inc(ld_small, 16)
            sp.dma_start(relb[0:32, :], a["L0_attn_rel_emb"]).then_inc(ld_small, 16)
            sp.dma_start(own[:, :], a["c_own"]).then_inc(ld_small, 16)
            sp.dma_start(ties[:, :], a["c_ties"].rearrange("a n -> (a n)").partition_broadcast(P)).then_inc(ld_small, 16)
            sp.dma_start(ties4[:, :], a["c_ties4"].rearrange("a n -> (a n)").partition_broadcast(P)).then_inc(ld_small, 16)
            for i, n in enumerate(("w_up", "w_gate")):
                sp.dma_start(ffn_nat[:, i * 1536:(i + 1) * 1536].rearrange("p (k n) -> p k n", n=C),
                             a["L0_ffn_" + n].rearrange("(k p) n -> p k n", p=P)).then_inc(ld_ffn, 16)
            sp.dma_start(ffn_nat[:, 3072:4608].rearrange("p (k n) -> p k n", n=FF),
                         a["L0_ffn_w_down"].rearrange("(k p) n -> p k n", p=P)).then_inc(ld_ffn, 16)
            sp.wait_ge(packed, NP_ // WS)
            for t, n in ((w_q, "wq"), (w_k, "wk")):
                sp.dma_start(t, a["L0_attn_" + n].rearrange("(k p) n -> p k n", p=P)).then_inc(ld_qk, 16)
            sp.wait_ge(tok_end_dve, 1)
            sp.wait_ge(tok_end_act, 1)
            sp.dma_start(onehot[0:32, :], a["c_onehot"]).then_inc(ld_small, 16)
            sp.dma_start(w_v, a["L0_attn_wv"].rearrange("(k p) n -> p k n", p=P)).then_inc(ld_attnw, 16)
            sp.dma_start(w_o, a["L0_attn_wo"].rearrange("(k p) n -> p k n", p=P)).then_inc(ld_attnw, 16)
            sp.wait_ge(ctx_mm, 2 * NT)
            sp.wait_ge(wo_mm, S)
            for i, n in enumerate(("WQ", "WK", "WV")):
                sp.dma_start(l1nat[:, i * 512:(i + 1) * 512].rearrange("p (k n) -> p k n", n=C),
                             a["L1_attn_" + n].rearrange("(k p) n -> p k n", p=P)).then_inc(ld_l1, 16)
            for i, n in enumerate(("gate", "up")):
                sp.dma_start(shnat[:, i * 1024:(i + 1) * 1024].rearrange("p (k n) -> p k n", n=C),
                             a[f"L1_ffn_shared_{n}_w"].rearrange("(k p) n -> p k n", p=P)).then_inc(ld_l1, 16)
            sp.dma_start(shnat[:, 2048:3072].rearrange("p (k n) -> p k n", n=SH),
                         a["L1_ffn_shared_down_w"].rearrange("(k p) n -> p k n", p=P)).then_inc(ld_l1, 16)
            sp.dma_start(rnat[0:NE, :], a["L1_ffn_router_w"]).then_inc(ld_l1, 16)
            for k in range(KC):
                for t, n in ((e_gate, "gate_w"), (e_up, "up_w")):
                    sp.dma_start(t[:, k], a["L1_ffn_" + n][:, k * P:(k + 1) * P, :].rearrange("e p n -> p e n")).then_inc(ld_moe, 16)
            sp.dma_start(e_down, a["L1_ffn_down_w"].rearrange("(k e) h n -> (e h) k n", e=2)).then_inc(ld_moe, 16)
            sp.dma_start(pick[0:NE], a["c_pick"].rearrange("e (k n) -> e k n", k=8)).then_inc(ld_moe, 16)
            for s in range(S):
                sp.wait_ge(h_ready, 3 * S + s + 1)
                sp.dma_start(out[:, s, :], H[0][:, s * C:(s + 1) * C]).then_inc(stored, 16)
            sp.wait_ge(stored, 16 * S)

        @block.gpsimd
        def _(pool):
            nc.gpsimd.memset(ones[:, :], 1.0).then_inc(ones_set, 1)
            nc.gpsimd.memset(zero_col, 0.0).then_inc(zero_set, 1)
            pool.wait_ge(zero_set, 1)
            def split(w, hi):
                return nc.gpsimd.tensor_tensor(rounded(w), w, rounded(hi), ALU.subtract)

            for x in xpack:
                nc.gpsimd.memset(x.rearrange("p (t y) -> p t y", t=WS)[:, :, PIX:PIXP], 0.0).then_inc(pads_zero, 1)
            nc.gpsimd.memset(conv_nat[:, :, PIX:PIXP], 0.0).then_inc(pads_zero, 1)
            for step, i in TOK:
                if step == "pack":
                    row, col = group_place(i)
                    pool.wait_ge(ld_x[row % XROWS], 16 * (row // XROWS + 1))
                    if i >= 2:
                        pool.wait_ge(turned, last_batch(WS * (i - 1) - 1) + 1)
                    x = col * PS
                    src = xring[row % XROWS].rearrange("p c r x -> p (c r) x")[:, :, x:x + WS * PS]
                    dst = xpack[i % 2].rearrange("p (t y) -> p t y", t=WS)[:, :, 0:PIX]
                    nc.gpsimd.tensor_copy(dst.rearrange("p t (cr x) -> p t cr x", x=PS),
                                          src.rearrange("p cr (t x) -> p t cr x", x=PS)).then_inc(packed, 1)
                elif step == "split qk":
                    pool.wait_ge(qk_hi, i + 1)
                    split(*qk_half(i)).then_inc(qk_lo, 1)
                elif step == "hzero":
                    pool.wait_ge(turned, NBATCH)
                    for x in (hT, hT_lo):
                        nc.gpsimd.tensor_copy(rounded(x), zero_col.unsqueeze(2).to_broadcast([P, KC, SLOTS])).then_inc(hT_zero, 1)
                elif step == "quant":
                    pool.wait_ge(ffn_scale, i + 1)
                    w, scales = ffn_matrix(i)
                    nc.gpsimd.tensor_tensor(w, w, ffn_inv[:, scales].unsqueeze(2).to_broadcast([P, NB, QB]),
                                            ALU.mult).then_inc(ffn_over, 1)
                elif step == "round":
                    pool.wait_ge(ffn_rounded, i + 1)
                    w, scales = ffn_matrix(i)
                    nc.gpsimd.tensor_tensor(w, w, ffn_abs[:, scales].unsqueeze(2).to_broadcast([P, NB, QB]),
                                            ALU.mult).then_inc(ffn_quant, 1)
                elif step == "pv":
                    pool.wait_ge(probs_ready, SM[("soft", i)] + 1)
                    pool.wait_ge(v_read, (i + 1) * KVN)
                    if i >= 1:
                        pool.wait_ge(agg_ready, i)
                    weigh_values(nc.gpsimd.tensor_tensor, 0, PV_POOL[i]).then_inc(pv_done, 1)
            pool.wait_ge(tok_end_dve, 1)
            pool.wait_ge(tok_end_act, 1)

            pool.wait_ge(v_hi, 1)
            split(w_v, w_v_hi).then_inc(v_lo, 1)
            pool.wait_ge(qkv_mm, 44)
            for b in pT:
                nc.gpsimd.memset(b, 0.0).then_inc(pT_zero, 1)
            nc.gpsimd.memset(pexp, 0.0).then_inc(pexp_zero, 1)
            for i, (w, hi) in enumerate(((upT, upT_hi), (gateT, gateT_hi))):
                pool.wait_ge(ug_hi_set, i + 1)
                split(w, hi).then_inc(ug_lo_set, 1)
            for i, (w, hi) in enumerate(((e_gate, e_gate_hi), (e_up, e_up_hi), (shT, shT_hi), (rT, rT_hi))):
                pool.wait_ge(ew_hi_set, i + 1)
                split(w, hi).then_inc(ew_lo_set, 1)
            for i, (w, hi) in enumerate(((e_down, e_down_hi), (sdT, sdT_hi))):
                pool.wait_ge(last_hi_set, i + 1)
                split(w, hi).then_inc(last_lo_set, 1)
            for n, step in enumerate(FINAL):
                _, c, hf = MOE[step]
                pool.wait_ge(hid_hi_set, n + 1)
                sl = slice(hf * 320, (hf + 1) * 320)
                split(hid[:, c, sl], hid_hi(c)[:, sl]).then_inc(hid_lo_set, 1)

        @block.tensor
        def _(pe):
            pe.wait_ge(ld_ident, 16)
            pe.wait_ge(ld_conv, 16)
            pe.wait_ge(pads_zero, 3)
            for j in range(NK):
                for k in range(KC):
                    w = conv_nat[:, k, j * CK:(j + 1) * CK]
                    m = pe.transpose(bank(j)[0:CK, k * P:(k + 1) * P], w, ident[:, :])
                m.then_inc(conv_turned, 1)
            pe.wait_ge(ld_vec, 16 * 8)
            pe.transpose(bank(5, 16), vec_rows[0:16, :], ident[0:16, 0:16]).then_inc(vec_turned, 1)
            pe.wait_ge(conv_kept, NK)
            pe.wait_ge(vec_kept, 1)
            for step, i in TOK:
                if step == "turn":
                    pe.wait_ge(packed, (4 * i + 3) // NK // WS + 1)
                    if i >= 2:
                        batches_of_pixels_kept(pe, i - 1)
                    for j in range(4):
                        m = pe.transpose(bank(i % 2, P, j * P)[0:CK, :], pixels(4 * i + j), ident[:, :])
                    m.then_inc(turned, 1)
                elif step == "conv":
                    batches_of_pixels_kept(pe, last_batch(i) + 1)
                    if i >= 2:
                        pe.wait_ge(conv_kept_sb, i - 1)
                    for j in range(NK):
                        b, at = (i * NK + j) // 4, (i * NK + j) % 4 * P
                        m = pe.matmul(bank(2 + i % 2, C), xT[b % XT][0:CK, at:at + P], convT[0:CK, j, :],
                                      start=(j == 0), stop=(j == NK - 1))
                    m.then_inc(conv_done, 1)
                elif step == "zturn":
                    ts = patches_of(i)
                    pe.wait_ge(z_ready, ts[-1] // WS + 1)
                    if i >= 1:
                        pe.wait_ge(z_kept, i)
                    for x, t in enumerate(ts):
                        for k in range(KC):
                            m = pe.transpose(bank(4, P, (k * 2 + x) * P),
                                             zgrp[t // WS % 2][:, (t % WS) * C + k * P:(t % WS) * C + (k + 1) * P], ident[:, :])
                    m.then_inc(z_turned, 1)
                elif step == "kv":
                    w, first = i // KVN, i % KVN * 2
                    ks = range(first, min(first + 2, NPOS))
                    pe.wait_ge(z_kept, i + 1)
                    pe.wait_ge(ld_tokw, 16 * 9)
                    for b, ready, read, at in ((5, k_ready, k_read, 0), (6, v_ready, v_read, C)):
                        if i >= 1:
                            pe.wait_ge(read, i)
                        for x, pos in enumerate(ks):
                            for k in range(KC):
                                m = pe.matmul(bank(b, C, x * C), zT[:, (w * NPOS + pos) % ZSLOTS, k, :],
                                              t_wkv[:, k, at:at + C], start=(k == 0), stop=(k == KC - 1))
                        m.then_inc(ready, 1)
                elif step == "hturn":
                    if i == 0:
                        batches_of_pixels_kept(pe, NBATCH)
                    if i >= 2:
                        pe.wait_ge(hT_kept, i - 1)
                    pe.wait_ge(win_read, SHARED_NO[("mod", i) if i < NW else ("gproj", 0)] + 1)
                    for k in range(KC):
                        m = pe.transpose(bank(i % 2, P, k * P), H[0][:, i * C + k * P:i * C + (k + 1) * P], ident[:, :])
                    m.then_inc(hT_turned, 1)
                elif step == "turnw":
                    if i == 0:
                        pe.wait_ge(ffn_quant, 3)
                        pe.wait_ge(conv_kept_sb, NP_)
                    turn_batch(pe, i)
                elif (step, i) in SHARED_NO:
                    n, o = shared((step, i))
                    if n >= 1:
                        pe.wait_ge(win_read, n)
                    if step in LNT:
                        pe.wait_ge(ln_z, LN[(LNT[step], i)] + 1)
                        for k in range(KC):
                            m = pe.transpose(o[:, k * P:(k + 1) * P], lnz[:, k * P:(k + 1) * P], ident[:, :])
                    elif step in ("gq", "q", "gkv"):
                        if step == "gq":
                            pe.wait_ge(ld_cls, 32)
                        else:
                            pe.wait_ge(ld_tokw, 16 * 9)
                        pe.wait_ge(ln_kept, LN[({"gq": "cls", "q": "red", "gkv": "loz"}[step], i)] + 1)
                        w = {"gq": g_wq, "q": t_wq, "gkv": g_wkv}[step]
                        for k in range(KC):
                            m = pe.matmul(o[:, 0:w.shape[2]], trn[:, k, :], w[:, k, :], start=(k == 0), stop=(k == KC - 1))
                    elif step in ("aggT", "gaggT"):
                        pe.wait_ge(agg_ready, AGG[({"aggT": "agg", "gaggT": "gsoft"}[step], i)] + 1)
                        for k in range(KC):
                            m = pe.transpose(o[:, k * P:(k + 1) * P], agg[:, k * P:(k + 1) * P], ident[:, :])
                    elif step in ("proj", "gproj"):
                        pe.wait_ge(aggT_kept, AGGT[({"proj": "aggT", "gproj": "gaggT"}[step], i)] + 1)
                        pe.wait_ge(ld_tokw, 16 * 9)
                        w = t_proj if step == "proj" else g_proj
                        for k in range(KC):
                            m = pe.matmul(o[:, 0:C], trn2[:, k, :], w[:, k, :], start=(k == 0), stop=(k == KC - 1))
                    elif step == "loT":
                        pe.wait_ge(lo_ready, i + 1)
                        for k in range(KC):
                            m = pe.transpose(o[:, k * P:(k + 1) * P], lo[:, k * P:(k + 1) * P], ident[:, :])
                    elif step == "mod":
                        pe.wait_ge(loT_kept, i + 1)
                        for k in range(KC):
                            m = pe.matmul(o[:, 0:C], trn3[:, k, :], t_mod[:, k, :], start=(k == 0), stop=(k == KC - 1))
                    m.then_inc(win_ready, 1)
            pe.wait_ge(hT_kept, S)
            pe.wait_ge(tok_end_dve, 1)
            pe.wait_ge(tok_end_act, 1)
            n = 0
            for c in range(8):
                for i, (w, hi) in enumerate(((w_q, w_q_hi), (w_k, w_k_hi))):
                    pe.wait_ge(qk_lo, c // 4 * 2 + i + 1)
                    for hf in range(2):
                        if n >= 4:
                            pe.wait_ge(qkv_kept_dve if n % 2 else qkv_kept_act, (n - 4) // 2 + 1)
                        rows, slots = slice(c * P, (c + 1) * P), slice(hf * 384, (hf + 1) * 384)
                        product3(pe, rounded, bank(2 + n % 4, SLOTS // 2), [(hi[:, k, rows], w[:, k, rows]) for k in range(KC)],
                                 [(hT[:, k, slots], hT_lo[:, k, slots]) for k in range(KC)]).then_inc(qkv_mm, 1)
                        n += 1
            pe.wait_ge(ld_small, 16 * 6)
            for j in range(S):
                m = pe.matmul(bank(6, NH, j * NH), onehot[0:32, j * P:(j + 1) * P], relb[0:32, :], start=True, stop=True)
            m.then_inc(bias_mm, 1)
            pe.wait_ge(v_lo, 1)
            for t in range(NT):
                for hf in range(2):
                    pe.wait_ge(qkv_kept_dve if n % 2 else qkv_kept_act, (n - 4) // 2 + 1)
                    slots, cols = slice(t * P, (t + 1) * P), slice(hf * 512, (hf + 1) * 512)
                    product3(pe, rounded, bank(2 + n % 4), [(hT[:, k, slots], hT_lo[:, k, slots]) for k in range(KC)],
                             [(w_v_hi[:, k, cols], w_v[:, k, cols]) for k in range(KC)]).then_inc(qkv_mm, 1)
                    n += 1
            pe.wait_ge(qkv_kept_act, n // 2)
            pe.wait_ge(qkv_kept_dve, n // 2)

            pe.wait_ge(bias_ready, 1)

            def scores(t):
                for half in range(2):
                    if t >= 1:
                        pe.wait_ge(score_read, 2 * t - 1 + half)
                    for c in range(8):
                        r = half * DK
                        sl = slice(t * P, (t + 1) * P)
                        m = pe.matmul(score_bank(half)[:, c, :], qT[r:r + DK, c, sl], kT[r:r + DK, c, sl],
                                      start=True, stop=True)
                    m.then_inc(score_mm, 1)

            def contexts(t):
                pe.wait_ge(pT_ready, t + 1)
                for half in range(2):
                    if t >= 2:
                        pe.wait_ge(ctx_kept_dve if half else ctx_kept_act, t - 1)
                    for c in range(4 * half, 4 * half + 4):
                        for par in range(2):
                            r, h = par * DK, 2 * c + par
                            m = pe.matmul(bank(2 + t % 2 * 2 + half)[r:r + DK, c % 4 * P:(c % 4 + 1) * P],
                                          V[:, t, h * DK:(h + 1) * DK], pT[t % 2][:, par * 8 + c, :], start=True, stop=True)
                    m.then_inc(ctx_mm, 1)

            for u in range(NT // 2 + 1):
                if u < NT // 2:
                    scores(2 * u)
                    scores(2 * u + 1)
                if u >= 1:
                    contexts(2 * u - 2)
                    contexts(2 * u - 1)
            pe.wait_ge(ctx_kept_act, NT)
            pe.wait_ge(ctx_kept_dve, NT)
            pe.wait_ge(ld_attnw, 32)
            for s in range(S):
                if s >= 2:
                    pe.wait_ge(wo_read, s - 1)
                for c in range(8):
                    m = pe.matmul(bank(6 + s % 2, C), ctxT[:, c, s, :], w_o[:, c, :], start=(c == 0), stop=(c == 7))
                m.then_inc(wo_mm, 1)

            def global_max(i):
                pe.wait_ge(gmax_part, i + 1)
                pe.transpose(bank(6)[0:1, 0:P], gm[:, :], ident[:, :]).then_inc(gmax_row, 1)
                pe.wait_ge(gmax_one, i + 1)
                pe.matmul(bank(7, 1), ones[0:1, :], gm[0:1, :], start=True, stop=True).then_inc(gmax_all, 1)

            def turn_token(src, stage, s):
                if s >= 2:
                    tokens_kept(pe, stage, s - 1)
                for k in range(KC):
                    m = pe.transpose(bank(s % 2, P, k * P), src[:, s * C + k * P:s * C + (k + 1) * P], ident[:, :])
                m.then_inc(hT2_turned, 1)

            global_max(0)
            for s in range(S):
                pe.wait_ge(hq_ready, s + 1)
                turn_token(h1q, 0, s)
            n = 0
            for w, hi in ((upT, upT_hi), (gateT, gateT_hi)):
                pe.wait_ge(ug_lo_set, n // 12 + 1)
                for c in range(6):
                    for hf in range(2):
                        if n < 2:
                            tokens_kept(pe, 0, 3 if n == 0 else S)
                        if n >= 6:
                            pe.wait_ge(ff_kept, n - 5)
                        rows, cols = slice(c * P, (c + 1) * P), slice(hf * 320, (hf + 1) * 320)
                        product3(pe, rounded, bank(ff_bank(n), 320),
                                 [(hi[:, k, rows], w[:, k, rows]) for k in range(KC)],
                                 [(h1T_hi[:, k, cols], h1T[:, k, cols]) for k in range(KC)]).then_inc(ff_mm, 1)
                        n += 1
                if w is upT:
                    global_max(1)
            global_max(2)
            pe.wait_ge(ff_kept, 24)
            pe.wait_ge(ld_l1, 16 * 7)
            for b in range(FFN_BATCHES, len(WB)):
                turn_batch(pe, b)
            global_max(3)
            global_max(4)
            def down(s):
                pe.wait_ge(o_ready, s + 1)
                if s >= 2:
                    pe.wait_ge(down_read, s - 1)
                for c in range(6):
                    m = pe.matmul(bank(6 + s % 2, C), sig.rearrange("p (c n) -> p c n", c=6)[:, c, s * P:(s + 1) * P],
                                  downT[:, c, :], start=(c == 0), stop=(c == 5))
                m.then_inc(down_mm, 1)

            def project(s):
                tokens_kept(pe, 1, s + 1)
                if s >= 2:
                    pe.wait_ge(l1_kept, 2 * (s - 1))
                for hf, (at, width) in enumerate(((0, 512), (512, 256))):
                    for k in range(KC):
                        m = pe.matmul(bank(2 + 2 * (s % 2) + hf, width), h2T[:, k, s * P:(s + 1) * P],
                                      l1T[:, k, at:at + width], start=(k == 0), stop=(k == KC - 1))
                    m.then_inc(l1_mm, 1)

            batches_kept(pe, len(WB))
            for s in range(S + 2):
                if s < S:
                    down(s)
                if 1 <= s <= S:
                    pe.wait_ge(h_ready, S + s)
                    turn_token(H[0], 1, s - 1)
                if s >= 2:
                    project(s - 2)

            for s in range(S):
                pe.wait_ge(h_ready, 2 * S + s + 1)
                turn_token(H[1], 2, s)
            pe.wait_ge(ew_lo_set, 4)
            for s in range(S):
                tokens_kept(pe, 2, s + 1)
                m = product3(pe, rounded, bank(7, NE, s * NE), [(h3T_hi[:, k, s * P:(s + 1) * P], h3T[:, k, s * P:(s + 1) * P])
                                                       for k in range(KC)], [(rT_hi[:, k, :], rT[:, k, :]) for k in range(KC)])
            m.then_inc(r_mm, 1)
            pe.wait_ge(ld_moe, 16 * 6)
            n = 0

            def moe_bank(n):
                return bank(n % 6, 320)

            for n, (kind, c, hf) in enumerate(MOE):
                if n >= 6:
                    q = n - 6
                    if MOE[q][0] == "gate":
                        pe.wait_ge(moe_sil, moe_count(q + 1, "gate"))
                    else:
                        pe.wait_ge(moe_hid, moe_count(q + 1, "up") + moe_count(q + 1, "comb"))
                o = moe_bank(n)
                sl = slice(hf * 320, (hf + 1) * 320)
                if kind == "comb":
                    if n == FIRST_COMB:
                        pe.wait_ge(combT_kept, 1)
                    m = pe.matmul(o, pick[0:NE, c - 4, :], combT[0:NE, sl], start=True, stop=True)
                else:
                    which = 0 if kind == "gate" else 1
                    if c < 4:
                        w = [(shT_hi[:, which, k, c * P:(c + 1) * P], shT[:, which, k, c * P:(c + 1) * P]) for k in range(KC)]
                    else:
                        e = 2 * (c - 4)
                        high, low = ((e_gate_hi, e_gate), (e_up_hi, e_up))[which]
                        w = [(high[:, k, e:e + 2, :], low[:, k, e:e + 2, :]) for k in range(KC)]
                    m = product3(pe, rounded, o, w, [(h3T_hi[:, k, sl], h3T[:, k, sl]) for k in range(KC)])
                m.then_inc(moe_mm, 1)
                if n == FIRST_COMB - 1:
                    pe.wait_ge(comb_ready, 1)
                    for s in range(S):
                        b, at = (6, s * P) if s < 4 else (7, 0)
                        m = pe.transpose(bank(b)[0:NE, at:at + P], comb_w[:, s * NE:(s + 1) * NE], ident[:, :])
                    m.then_inc(combT_mm, 1)
            pe.wait_ge(last_lo_set, 2)
            pe.wait_ge(moe_hid, moe_count(len(MOE), "up") + moe_count(len(MOE), "comb"))
            pe.wait_ge(moe_sil, moe_count(len(MOE), "gate"))
            for s in range(S):
                if s >= 2:
                    pe.wait_ge(down_read, S + s - 1)
                pe.wait_ge(hid_lo_set, len(FINAL) - 1 if s < 2 else len(FINAL))
                sl = slice(s * P, (s + 1) * P)
                m = product3(pe, rounded, bank(s % 2, C), [(hid_hi(c)[:, sl], hid[:, c, sl]) for c in range(12)],
                             [(sdT_hi[:, c, :], sdT[:, c, :]) if c < 4 else (e_down_hi[:, c - 4, :], e_down[:, c - 4, :])
                              for c in range(12)])
                m.then_inc(down_mm, 1)

        @block.scalar
        def _(act):
            chain = [0]

            def link(ins):
                chain[0] += 1
                ins.then_inc(act_chain, 1)
                act.wait_ge(act_chain, chain[0])

            for j in range(0, NK, 2):
                act.wait_ge(conv_turned, j + 1)
                nc.scalar.copy(convT[0:CK, j, :], bank(j, C)[0:CK]).then_inc(conv_kept, 1)
            for step, i in TOK:
                if step == "turn" and not DVE_TURNS(i):
                    act.wait_ge(turned, i + 1)
                    if i >= XT:
                        act.wait_ge(conv_done, (4 * (i - XT) + 3) // NK + 1)
                    nc.scalar.copy(xT[i % XT][0:CK, :], bank(i % 2)[0:CK]).then_inc(turned_kept_act, 1)
                elif step == "conv":
                    act.wait_ge(conv_done, i + 1)
                    if i // WS >= 2:
                        act.wait_ge(z_ready, i // WS - 1)
                    nc.scalar.copy(pes[i // WS % 2][:, (i % WS) * C:(i % WS + 1) * C], bank(2 + i % 2, C)).then_inc(conv_kept_sb, 1)
                elif step == "hturn":
                    act.wait_ge(hT_zero, 2)
                    act.wait_ge(hT_turned, i + 1)
                    for hi_, _, v in hT_pieces(i):
                        m = nc.scalar.copy(rounded(hi_), v)
                    m.then_inc(hT_hi_set, 1)
                elif step == "split qk":
                    if i == 0:
                        act.wait_ge(ld_qk, 32)
                        act.wait_ge(conv_done, NP_)
                        act.wait_ge(agg_ready, NW)
                    w, hi = qk_half(i)
                    nc.scalar.copy(rounded(hi), w).then_inc(qk_hi, 1)
                elif step == "turnw":
                    keep_batch(act, nc.scalar.copy, i, wt_kept)
                elif step == "stat root":
                    act.wait_ge(var_ready, i + 1)
                    nc.scalar.activation(rs3, rc3, ACT.Sqrt).then_inc(rstd_ready, 1)
                elif step in ("cls root", "red root", "loz root"):
                    act.wait_ge(ln_var, LN[(step.split()[0], i)] + 1)
                    nc.scalar.activation(rs1, rc1, ACT.Sqrt).then_inc(ln_rstd, 1)
                elif step == "kv":
                    if i % KVN == 0 and i >= KVN:
                        act.wait_ge(qk_done, i // KVN)
                    act.wait_ge(k_ready, i + 1)
                    at, n = i % KVN * 2 * C, min(2, NPOS - i % KVN * 2) * C
                    nc.scalar.copy(kwin[:, at:at + n], bank(5, n)).then_inc(k_read, 1)
                    if i % KVN == 0 and i >= KVN:
                        act.wait_ge(pv_done, i // KVN)
                    act.wait_ge(v_ready, i + 1)
                    nc.scalar.copy(vwin[:, at:at + n], bank(6, n)).then_inc(v_read, 1)
                elif step == "soft exp":
                    act.wait_ge(shifted, SM[("soft", i)] + 1)
                    nc.scalar.activation(sc, sc, ACT.Exp).then_inc(exp_done, 1)
                elif step == "gsoft exp":
                    act.wait_ge(shifted, SM[("gsoft", i)] + 1)
                    nc.scalar.activation(gs, gs, ACT.Exp).then_inc(exp_done, 1)
                elif step == "aggT":
                    n, o = shared((step, i))
                    act.wait_ge(win_ready, n + 1)
                    nc.scalar.copy(trn2, o[:, 0:C].rearrange("p (k n) -> p k n", k=KC)).then_inc(win_read, 1)
                    act.wait_ge(win_read, n + 1)
                    act.sem_inc(aggT_kept, 1)
                elif step == "loT":
                    n, o = shared((step, i))
                    act.wait_ge(win_ready, n + 1)
                    nc.scalar.copy(trn3, o[:, 0:C].rearrange("p (k n) -> p k n", k=KC)).then_inc(win_read, 1)
                    act.wait_ge(win_read, n + 1)
                    act.sem_inc(loT_kept, 1)
            act.wait_ge(win_read, len(SHARED))
            act.sem_inc(tok_end_act, 1)

            for n in range(0, 44, 2):
                if n == 8:
                    act.wait_ge(ld_attnw, 32)
                    act.wait_ge(tok_end_dve, 1)
                    nc.scalar.copy(rounded(w_v_hi), w_v).then_inc(v_hi, 1)
                act.wait_ge(qkv_mm, n + 1)
                qkv_copy(nc.scalar.copy, n).then_inc(qkv_kept_act, 1)
            def read_scores(t):
                if t % 2 == 0 and t >= 2:
                    act.wait_ge(att_shift, t // 2)
                for half in range(2):
                    act.wait_ge(score_mm, 2 * t + half + 1)
                    for g in range(4):
                        at = (t % 2 * NH + half * 8) * 30
                        m = nc.scalar.copy(smask[g * 32:(g + 1) * 32, at:at + 240].rearrange("p (h x) -> p h x", x=30),
                                           score_bank(half)[g * 32:(g + 1) * 32, :, g * 32:g * 32 + 30])
                    m.then_inc(score_read, 1)

            for u in range(NT // 2 + 1):
                if u < NT // 2:
                    read_scores(2 * u)
                    read_scores(2 * u + 1)
                    act.wait_ge(att_shift, u + 1)
                    nc.scalar.activation(att, att, ACT.Exp).then_inc(att_exp, 1)
                if u >= 1:
                    for t in (2 * u - 2, 2 * u - 1):
                        ctx_copy(nc.scalar.copy, act, ctx_kept_act, t, 0)
            def rstd(n, tokens=1):
                act.wait_ge(rln_var, n + 1)
                nc.scalar.activation(rs5[:, 0:tokens], rc5[:, 0:tokens], ACT.Sqrt).then_inc(rln_rstd, 1)

            act.wait_ge(ctx_mm, 2 * NT)
            act.wait_ge(pT_ready, NT)
            act.wait_ge(wt_kept, FFN_BATCHES)
            nc.scalar.copy(rounded(upT_hi), upT).then_inc(ug_hi_set, 1)
            for s in range(S):
                rstd(s)
            nc.scalar.copy(rounded(gateT_hi), gateT).then_inc(ug_hi_set, 1)
            for s in (1, 3):
                keep_token(act, nc.scalar.copy, rounded(h1T_hi), 0, s, hT2_kept_act)
            for n in range(24):
                act.wait_ge(ff_mm, n + 1)
                dst = (up if n < 12 else gate)[:, (n % 12) * 320:(n % 12 + 1) * 320]
                nc.scalar.copy(dst, bank(ff_bank(n), 320)).then_inc(ff_kept, 1)
            for half in range(2):
                act.wait_ge(gate_q, half + 1)
                sl = slice(half * 3 * S * P, (half + 1) * 3 * S * P)
                nc.scalar.activation(sig[:, sl], gate[:, sl], ACT.Sigmoid, scale=qsc[:, 2:3]).then_inc(sig_made, 1)
                act.wait_ge(sig_made, half + 1)
                nc.scalar.activation(sig[:, sl], sig[:, sl], ACT.Copy, bias=MAGIC, scale=65536.0).then_inc(sig_ready, 1)
            for b in range(FFN_BATCHES, len(WB)):
                keep_batch(act, nc.scalar.copy, b, wt_kept)
            act.wait_ge(q_third, 1)
            sl = slice(3 * S * P, 6 * S * P)
            nc.scalar.activation(sig[:, sl], sig[:, sl], ACT.Copy, bias=MAGIC, scale=qinv[:, 3:4]).then_inc(third_scaled, 1)
            act.wait_ge(ld_moe, 16 * 6)
            for w, hi in ((e_gate, e_gate_hi), (e_up, e_up_hi)):
                nc.scalar.copy(rounded(hi), w).then_inc(ew_hi_set, 1)
            act.wait_ge(wt_kept, len(WB))
            for w, hi in ((shT, shT_hi), (rT, rT_hi)):
                nc.scalar.copy(rounded(hi), w).then_inc(ew_hi_set, 1)
            for s in range(S + 2):
                if s < S:
                    rstd(S + s)
                if s in (2, 4):
                    keep_token(act, nc.scalar.copy, h2T, 1, s - 1, hT2_kept_act)
                if s >= 2:
                    t = s - 2
                    for hf, (at, width) in enumerate(((0, 512), (512, 256))):
                        act.wait_ge(l1_mm, 2 * t + hf + 1)
                        nc.scalar.copy(qkv[:, t, at:at + width], bank(2 + 2 * (t % 2) + hf, width)).then_inc(l1_kept, 1)
            act.wait_ge(l1_shift, 1)
            nc.scalar.activation(msc, msc, ACT.Exp).then_inc(l1_exp, 1)
            rstd(2 * S, 3)
            rstd(2 * S + 1, 2)
            nc.scalar.copy(rounded(e_down_hi), e_down).then_inc(last_hi_set, 1)
            nc.scalar.copy(rounded(sdT_hi), sdT).then_inc(last_hi_set, 1)
            for s in (1, 3):
                keep_token(act, nc.scalar.copy, rounded(h3T_hi), 2, s, hT2_kept_act)
            act.wait_ge(r_mm, 1)
            nc.scalar.activation(comb_w, bank(7, S * NE), ACT.Sigmoid).then_inc(r_sig, 1)
            g, done = 0, 0
            for n in range(len(MOE) + 3):
                if n < len(MOE) and MOE[n][0] == "gate":
                    act.wait_ge(moe_mm, n + 1)
                    if g >= 2:
                        q = [m for m, x in enumerate(MOE) if x[0] == "up"][g - 2]
                        act.wait_ge(moe_hid, moe_count(q + 1, "up") + moe_count(q + 1, "comb"))
                    nc.scalar.activation(sil[g % 2], bank(n % 6, 320), ACT.Silu).then_inc(moe_sil, 1)
                    g += 1
                if n - 3 in FINAL:
                    _, c, hf = MOE[n - 3]
                    act.wait_ge(moe_hid, moe_count(n - 2, "up") + moe_count(n - 2, "comb"))
                    sl = slice(hf * 320, (hf + 1) * 320)
                    nc.scalar.copy(rounded(hid_hi(c)[:, sl]), hid[:, c, sl]).then_inc(hid_hi_set, 1)
            for s in range(S):
                rstd(2 * S + 2 + s)

        @block.vector
        def _(dve):
            chain = [0]

            def link(ins):
                chain[0] += 1
                ins.then_inc(dve_chain, 1)
                dve.wait_ge(dve_chain, chain[0])

            def moments(x, st, mv, rc, n=1):
                for k in range(n):
                    m = nc.vector.bn_stats(st[:, 6 * k:6 * k + 6], x[:, k * C:(k + 1) * C])
                link(m)
                for k in range(n):
                    m = nc.vector.bn_aggr(mv[:, 2 * k:2 * k + 2], st[:, 6 * k:6 * k + 6])
                link(m)
                v = mv[:, 0:2 * n].rearrange("p (k two) -> p k two", two=2)[:, :, 1]
                link(nc.vector.tensor_scalar(rc, v, EPS, None, ALU.add))
                return nc.vector.reciprocal(rc, rc)

            for j in range(1, NK, 2):
                dve.wait_ge(conv_turned, j + 1)
                nc.vector.tensor_copy(convT[0:CK, j, :], bank(j, C)[0:CK]).then_inc(conv_kept, 1)
            dve.wait_ge(vec_turned, 1)
            nc.vector.tensor_copy(vec[:, :], bank(5, 16)).then_inc(vec_kept, 1)
            dve.wait_ge(vec_kept, 1)

            def softmax_part1(s, n):
                link(nc.vector.tensor_reduce(mx8, s.rearrange("p k h -> p h k"), AX.X, ALU.max))
                nc.vector.tensor_tensor(s, s, mx8.unsqueeze(1).to_broadcast([P, n, LH]), ALU.subtract).then_inc(shifted, 1)

            def softmax_part2(s, n):
                link(nc.vector.tensor_reduce(sm8, s.rearrange("p k h -> p h k"), AX.X, ALU.add))
                link(nc.vector.reciprocal(rs8, sm8))
                return nc.vector.tensor_tensor(s, s, rs8.unsqueeze(1).to_broadcast([P, n, LH]), ALU.mult)

            for step, i in TOK:
                if step == "turn" and DVE_TURNS(i):
                    dve.wait_ge(turned, i + 1)
                    if i >= XT:
                        dve.wait_ge(conv_done, (4 * (i - XT) + 3) // NK + 1)
                    nc.vector.tensor_copy(xT[i % XT][0:CK, :], bank(i % 2)[0:CK]).then_inc(turned_kept_dve, 1)
                elif step == "stat":
                    w, first = i // WS, i % WS == 0
                    dve.wait_ge(conv_kept_sb, WS * (i + 1))
                    emb = pes[i % 2]
                    moments(emb, st3, mv3, rc3, WS).then_inc(var_ready, 1)
                    v = emb.rearrange("p (k n) -> p n k", k=WS)
                    if i == NP_ // WS - 1:
                        continue
                    if first:
                        link(nc.vector.tensor_reduce(red[:, w, :], v, AX.X, ALU.add))
                    else:
                        link(nc.vector.tensor_reduce(tmp[:, :], v, AX.X, ALU.add))
                        link(nc.vector.tensor_tensor(red[:, w, :], red[:, w, :], tmp[:, :], ALU.add))
                elif step == "stat z":
                    emb = pes[i % 2]
                    dve.wait_ge(rstd_ready, i + 1)
                    if i >= 2:
                        dve.wait_ge(z_turned, pair_of(WS * (i - 1) - 1) + 1)
                    for k in range(WS):
                        m = nc.vector.tensor_scalar(zgrp[i % 2][:, k * C:(k + 1) * C], emb[:, k * C:(k + 1) * C],
                                                    mv3[:, 2 * k:2 * k + 1], rs3[:, k:k + 1], ALU.subtract, ALU.mult)
                    m.then_inc(z_ready, 1)
                    dve.wait_ge(z_ready, i + 1)
                    if i == NP_ // WS - 1:
                        link(nc.vector.tensor_reduce(tmp[:, :], emb.rearrange("p (k n) -> p n k", k=WS), AX.X, ALU.add))
                        link(nc.vector.tensor_tensor(red[:, NW - 1, :], red[:, NW - 1, :], tmp[:, :], ALU.add))
                elif step == "zturn":
                    dve.wait_ge(z_turned, i + 1)
                    if i >= 2 * KVN:
                        dve.wait_ge(v_ready, i - 2 * KVN + 1)
                    slot, n = patches_of(i)[0] % ZSLOTS, len(patches_of(i))
                    for k in range(KC):
                        m = nc.vector.tensor_scalar(zT[:, slot:slot + n, k, :],
                                                    bank(4, n * P, k * 2 * P).rearrange("p (t n) -> p t n", n=P),
                                                    vec[:, 4 + k:5 + k], vec[:, 6 + k:7 + k], ALU.mult, ALU.add)
                    m.then_inc(z_kept, 1)
                elif step in ("cls", "red", "loz"):
                    n = LN[(step, i)]
                    if step == "cls":
                        dve.wait_ge(ld_cls, 32)
                        x = cls[:, :]
                    elif step == "red":
                        link(nc.vector.tensor_scalar(red[:, i, :], red[:, i, :], 1.0 / NPOS, None, ALU.mult))
                        x = red[:, i, :]
                    else:
                        x = lo[:, :]
                    moments(x, st1, mv1, rc1).then_inc(ln_var, 1)
                elif step in ("cls z", "red z", "loz z"):
                    step = step.split()[0]
                    n = LN[(step, i)]
                    x = {"cls": cls[:, :], "red": red[:, i, :], "loz": lo[:, :]}[step]
                    dve.wait_ge(ln_rstd, n + 1)
                    if n >= 1:
                        dve.wait_ge(ln_kept, n)
                    nc.vector.tensor_scalar(lnz[:, :], x, mv1[:, 0:1], rs1[:, 0:1], ALU.subtract, ALU.mult).then_inc(ln_z, 1)
                    dve.wait_ge(ln_z, n + 1)
                elif step == "qk" and i == NW - 1:
                    for lo_, hi_, pairs_ in ((0, QK_FIRST, QK_FIRST // 2), (QK_FIRST, NPOS, KVN)):
                        dve.wait_ge(k_read, i * KVN + pairs_)
                        n = hi_ - lo_
                        link(nc.vector.tensor_tensor(prod[:, lo_ * C:hi_ * C].rearrange("p (k n) -> p k n", n=C),
                                                     kwin[:, lo_ * C:hi_ * C].rearrange("p (k n) -> p k n", n=C),
                                                     qwin[:, :].unsqueeze(1).to_broadcast([P, n, C]), ALU.mult))
                        link(nc.vector.tensor_reduce(sc[:, lo_ * LH:hi_ * LH],
                                                     prod[:, lo_ * C:hi_ * C].rearrange("p (kh d) -> p kh d", d=LD), AX.X, ALU.add))
                elif step == "qk":
                    dve.wait_ge(k_read, (i + 1) * KVN)
                    nc.vector.tensor_tensor(prod.rearrange("p (k n) -> p k n", n=C), kwin.rearrange("p (k n) -> p k n", n=C),
                                            qwin[:, :].unsqueeze(1).to_broadcast([P, NPOS, C]), ALU.mult).then_inc(qk_done, 1)
                    dve.wait_ge(qk_done, i + 1)
                elif (step, i) in SHARED_NO and "d" in READERS[step]:
                    n, o = shared((step, i))
                    dve.wait_ge(win_ready, n + 1)
                    if step in LNT:
                        v = {"clsT": 8, "redT": 0, "lozT": 12}[step]
                        for k in range(KC):
                            m = nc.vector.tensor_scalar(trn[:, k, :], o[:, k * P:(k + 1) * P], vec[:, v + k:v + k + 1],
                                                        vec[:, v + 2 + k:v + 3 + k], ALU.mult, ALU.add)
                        m.then_inc(win_read, 1)
                        dve.wait_ge(win_read, n + 1)
                        dve.sem_inc(ln_kept, 1)
                    elif step == "gq":
                        nc.vector.tensor_scalar(gq[:, :], o[:, 0:C], C ** -0.5, None, ALU.mult).then_inc(win_read, 1)
                    elif step == "q":
                        nc.vector.tensor_scalar(qwin[:, :], o[:, 0:C], C ** -0.5, None, ALU.mult).then_inc(win_read, 1)
                        dve.wait_ge(win_read, n + 1)
                    elif step == "proj":
                        nc.vector.tensor_tensor(lo[:, :], o[:, 0:C], red[:, i, :], ALU.add).then_inc(lo_ready, 1)
                        dve.wait_ge(lo_ready, i + 1)
                        dve.sem_inc(win_read, 1)
                    elif step == "mod":
                        nc.vector.tensor_tensor(H[0][:, i * C:(i + 1) * C], o[:, 0:C], mod_b[:, :], ALU.add).then_inc(win_read, 1)
                    elif step == "gkv":
                        link(nc.vector.tensor_tensor(tmp[:, :], o[:, 0:C], gq[:, :], ALU.mult))
                        link(nc.vector.tensor_reduce(gs[:, i * LH:(i + 1) * LH], tmp[:, :].rearrange("p (h d) -> p h d", d=LD),
                                                     AX.X, ALU.add))
                        nc.vector.tensor_copy(gv[:, i * C:(i + 1) * C], o[:, C:2 * C]).then_inc(win_read, 1)
                    elif step == "gaggT":
                        nc.vector.tensor_copy(trn2, o[:, 0:C].rearrange("p (k n) -> p k n", k=KC)).then_inc(win_read, 1)
                        dve.wait_ge(win_read, n + 1)
                        dve.sem_inc(aggT_kept, 1)
                    elif step == "gproj":
                        nc.vector.tensor_tensor(H[0][:, NW * C:S * C], o[:, 0:C], cls[:, :], ALU.add).then_inc(win_read, 1)
                elif step == "soft":
                    s = sc.rearrange("p (k h) -> p k h", h=LH)
                    if i < NW - 1:
                        link(nc.vector.tensor_reduce(sc, prod.rearrange("p (kh d) -> p kh d", d=LD), AX.X, ALU.add))
                    softmax_part1(s, NPOS)
                elif step == "soft norm":
                    s = sc.rearrange("p (k h) -> p k h", h=LH)
                    dve.wait_ge(exp_done, SM[("soft", i)] + 1)
                    softmax_part2(s, NPOS).then_inc(probs_ready, 1)
                elif step == "agg":
                    if PV_POOL[i] < NPOS:
                        dve.wait_ge(v_read, (i + 1) * KVN)
                        dve.wait_ge(probs_ready, i + 1)
                        link(weigh_values(nc.vector.tensor_tensor, PV_POOL[i], NPOS))
                    dve.wait_ge(pv_done, i + 1)
                    if i >= 1:
                        dve.wait_ge(aggT_kept, i)
                    nc.vector.tensor_reduce(agg[:, :], prod.rearrange("p (k n) -> p n k", k=NPOS), AX.X, ALU.add).then_inc(agg_ready, 1)
                elif step == "bias":
                    if i == NW:
                        link(nc.vector.tensor_tensor(cls[:, :], cls[:, :], gproj_b[:, :], ALU.add))
                    else:
                        dve.wait_ge(ld_tokw, 16 * 9)
                        link(nc.vector.tensor_tensor(red[:, i, :], red[:, i, :], proj_b[:, :], ALU.add))
                elif step == "gsoft":
                    s = gs.rearrange("p (k h) -> p k h", h=LH)
                    softmax_part1(s, NW)
                elif step == "gsoft norm":
                    s = gs.rearrange("p (k h) -> p k h", h=LH)
                    dve.wait_ge(exp_done, SM[("gsoft", i)] + 1)
                    link(softmax_part2(s, NW))
                    dve.wait_ge(win_read, SHARED_NO[("gkv", NW - 1)] + 1)
                    g4 = gv[:, :].rearrange("p (kh d) -> p kh d", d=LD)
                    link(nc.vector.tensor_tensor(g4, g4, gs.unsqueeze(2).to_broadcast([P, NW * LH, LD]), ALU.mult))
                    nc.vector.tensor_reduce(agg[:, :], gv[:, :].rearrange("p (k n) -> p n k", k=NW), AX.X, ALU.add).then_inc(agg_ready, 1)
                elif step == "hturn":
                    dve.wait_ge(hT_hi_set, i + 1)
                    for hi_, lo_, v in hT_pieces(i):
                        m = nc.vector.tensor_tensor(rounded(lo_), v, rounded(hi_), ALU.subtract)
                    m.then_inc(hT_kept, 1)
                elif step == "quant":
                    dve.wait_ge(ld_ffn, 48)
                    w, scales = ffn_matrix(i)
                    link(nc.vector.tensor_reduce(ffn_abs[:, scales], w, AX.X, ALU.max, apply_absolute_value=True))
                    link(nc.vector.tensor_scalar(ffn_abs[:, scales], ffn_abs[:, scales], 1.0 / 7.0, 1e-12, ALU.mult, ALU.max))
                    nc.vector.reciprocal(ffn_inv[:, scales], ffn_abs[:, scales]).then_inc(ffn_scale, 1)
                elif step == "round":
                    dve.wait_ge(ffn_over, i + 1)
                    w, _ = ffn_matrix(i)
                    nc.vector.tensor_scalar(w, w, MAGIC, MAGIC, ALU.add, ALU.subtract).then_inc(ffn_rounded, 1)
            dve.wait_ge(win_read, len(SHARED))
            dve.sem_inc(tok_end_dve, 1)

            for n in range(1, 44, 2):
                if n == 33:
                    dve.wait_ge(bias_mm, 1)
                    nc.vector.tensor_copy(bias.rearrange("p (a c j) -> p a c j", a=2, j=S),
                                          bank(6, S * NH).rearrange("p (j c a) -> p a c j", j=S, a=2)).then_inc(bias_ready, 1)
                dve.wait_ge(qkv_mm, n + 1)
                qkv_copy(nc.vector.tensor_copy, n).then_inc(qkv_kept_dve, 1)
            dve.wait_ge(bias_ready, 1)
            dve.wait_ge(ld_small, 16 * 6)
            dve.wait_ge(pexp_zero, 1)
            a3 = att.rearrange("p (h j) -> p h j", j=S)

            def att_shifted(u):
                dve.wait_ge(score_read, 4 * u + 4)
                m4 = smask.rearrange("p (h i j) -> p h i j", i=GI, j=S)
                link(nc.vector.tensor_tensor(m4, m4, own[:, :].unsqueeze(1).unsqueeze(3).to_broadcast([P, 2 * NH, GI, S]), ALU.mult))
                link(nc.vector.tensor_reduce(a3, smask.rearrange("p (h i j) -> p h j i", i=GI, j=S), AX.X, ALU.add))
                link(nc.vector.tensor_tensor(att.rearrange("p (t x) -> p t x", t=2), att.rearrange("p (t x) -> p t x", t=2),
                                             bias.unsqueeze(1).to_broadcast([P, 2, NH * S]), ALU.add))
                link(nc.vector.tensor_reduce(att_mx, a3, AX.X, ALU.max))
                nc.vector.tensor_tensor(a3, a3, att_mx.unsqueeze(2).to_broadcast([P, 2 * NH, S]), ALU.subtract).then_inc(att_shift, 1)

            def att_probs(u):
                dve.wait_ge(att_exp, u + 1)
                link(nc.vector.tensor_reduce(att_sm, a3, AX.X, ALU.add))
                link(nc.vector.reciprocal(att_sm, att_sm))
                link(nc.vector.tensor_tensor(a3, a3, att_sm.unsqueeze(2).to_broadcast([P, 2 * NH, S]), ALU.mult))
                o = pexp.rearrange("p (h x) -> p h x", x=32)[:, :, 0:30].rearrange("p h (i j) -> p h i j", j=S)
                link(nc.vector.tensor_tensor(o, a3.unsqueeze(2).to_broadcast([P, 2 * NH, GI, S]),
                                             own[:, :].unsqueeze(1).unsqueeze(3).to_broadcast([P, 2 * NH, GI, S]), ALU.mult))
                for t in (2 * u, 2 * u + 1):
                    if t >= 2:
                        dve.wait_ge(ctx_mm, 2 * (t - 1))
                    else:
                        dve.wait_ge(pT_zero, 2)
                    for g in range(4):
                        q = slice(g * 32, (g + 1) * 32)
                        m = nc.vector.transpose(pT[t % 2][q, :, q], pexp[q, t % 2 * NH * 32:(t % 2 + 1) * NH * 32])
                    m.then_inc(pT_ready, 1)
                dve.wait_ge(pT_ready, 2 * u + 2)

            for u in range(NT // 2 + 1):
                if u < NT // 2:
                    att_shifted(u)
                if u >= 1:
                    ctx_copy(nc.vector.tensor_copy, dve, ctx_kept_dve, 2 * u - 2, 1)
                if u < NT // 2:
                    att_probs(u)
                if u >= 1:
                    ctx_copy(nc.vector.tensor_copy, dve, ctx_kept_dve, 2 * u - 1, 1)

            def res_ln(n, x, dst, tokens=1, behind=None):
                moments(x, st5, mv5, rc5[:, 0:tokens], tokens).then_inc(rln_var, 1)
                if behind is not None:
                    behind()
                dve.wait_ge(rln_rstd, n + 1)
                for k in range(tokens):
                    m = nc.vector.tensor_scalar(dst[:, k * C:(k + 1) * C], x[:, k * C:(k + 1) * C], mv5[:, 2 * k:2 * k + 1],
                                                rs5[:, k:k + 1], ALU.subtract, ALU.mult).then_inc(h_ready, 1)
                    ready[0] += 1
                dve.wait_ge(h_ready, ready[0])

            ready = [0]

            def tok(h, s):
                return h[:, s * C:(s + 1) * C]

            for s in range(S):
                dve.wait_ge(wo_mm, s + 1)
                nc.vector.tensor_tensor(tok(H[1], s), bank(6 + s % 2, C), tok(H[0], s), ALU.add).then_inc(wo_read, 1)
                dve.wait_ge(wo_read, s + 1)
                res_ln(s, tok(H[1], s), tok(H[1], s))
                nc.vector.tensor_reduce(pmax[:, s:s + 1], tok(H[1], s), AX.X, ALU.max, apply_absolute_value=True).then_inc(tok_max, 1)

            def global_max(i, fold_=None):
                dve.wait_ge(gmax_row, i + 1)
                nc.vector.tensor_reduce(gm[0:1, :], bank(6)[0:1, 0:P], AX.X, ALU.max).then_inc(gmax_one, 1)
                dve.wait_ge(gmax_all, i + 1)
                if fold_ is None:
                    link(nc.vector.tensor_scalar(qsc[:, i:i + 1], bank(7, 1), 1.0 / 32767.0, 1e-12, ALU.mult, ALU.max))
                    link(nc.vector.reciprocal(qinv[:, i:i + 1], qsc[:, i:i + 1]))
                else:
                    link(nc.vector.tensor_scalar(qsc[:, i:i + 1], bank(7, 1), fold_, 1.0 / 32767.0, ALU.mult, ALU.mult))
                    link(nc.vector.tensor_scalar(qsc[:, i:i + 1], qsc[:, i:i + 1], 1e-12, None, ALU.max))
                    link(nc.vector.reciprocal(qinv[:, i:i + 1], qsc[:, i:i + 1]))
                    link(nc.vector.tensor_scalar(qinv[:, i:i + 1], qinv[:, i:i + 1], fold_, None, ALU.mult))

            def to_integers(x, i):
                link(nc.vector.tensor_scalar(x, x, qinv[:, i:i + 1], MAGIC, ALU.mult, ALU.add))
                return nc.vector.tensor_scalar(x, x, MAGIC, None, ALU.subtract)

            dve.wait_ge(tok_max, S)
            nc.vector.tensor_reduce(gm, pmax[:, 0:S], AX.X, ALU.max).then_inc(gmax_part, 1)
            global_max(0)
            def split_token(hi, lo, stage, act_before, s):
                cols = slice(s * P, (s + 1) * P)
                v = bank(s % 2, C).rearrange("p (k n) -> p k n", k=KC)
                if s % 2 == 0:
                    dve.wait_ge(hT2_turned, stage * S + s + 1)
                    link(nc.vector.tensor_copy(rounded(hi[:, :, cols]), v))
                else:
                    dve.wait_ge(hT2_kept_act, act_before + s // 2 + 1)
                nc.vector.tensor_tensor(rounded(lo[:, :, cols]), v, rounded(hi[:, :, cols]), ALU.subtract).then_inc(hT2_kept_dve, 1)

            for s in range(S + 1):
                if s < S:
                    link(nc.vector.tensor_scalar(tok(h1q, s), tok(H[1], s), qinv[:, 0:1], MAGIC, ALU.mult, ALU.add))
                    nc.vector.tensor_scalar(tok(h1q, s), tok(h1q, s), MAGIC, qsc[:, 0:1], ALU.subtract, ALU.mult).then_inc(hq_ready, 1)
                if s >= 1:
                    split_token(h1T_hi, h1T, 0, 0, s - 1)
            for n in range(24):
                dve.wait_ge(ff_kept, n + 1)
                nc.vector.tensor_reduce(pmax[:, n % 12:n % 12 + 1], (up, gate)[n // 12][:, n % 12 * 320:(n % 12 + 1) * 320], AX.X, ALU.max,
                                        apply_absolute_value=True).then_inc(ff_max, 1)
                if n % 12 == 11:
                    dve.wait_ge(ff_max, n + 1)
                    nc.vector.tensor_reduce(gm, pmax, AX.X, ALU.max).then_inc(gmax_part, 1)
                    global_max(1 + n // 12)
                    if n < 12:
                        link(to_integers(up, 1))
            halves = [slice(half * 3 * S * P, (half + 1) * 3 * S * P) for half in range(2)]
            for sl in halves:
                to_integers(gate[:, sl], 2).then_inc(gate_q, 1)
            dve.wait_ge(gate_q, 2)

            for half, sl in enumerate(halves):
                dve.wait_ge(sig_ready, half + 1)
                link(nc.vector.tensor_scalar(sig[:, sl], sig[:, sl], MAGIC + 65535.0, MAGIC, ALU.min, ALU.subtract))
                link(nc.vector.tensor_tensor(sig[:, sl], sig[:, sl], gate[:, sl], ALU.mult))

            nc.vector.tensor_reduce(gm, sig, AX.X, ALU.max, apply_absolute_value=True).then_inc(gmax_part, 1)
            link(nc.vector.tensor_scalar(fold[:, 0:1], qsc[:, 2:3], 1.0 / 65536.0, None, ALU.mult))
            global_max(3, fold[:, 0:1])
            dve.sem_inc(q_third, 1)
            for half, sl in enumerate(halves):
                if half == 0:
                    link(to_integers(sig[:, sl], 3))
                else:
                    dve.wait_ge(third_scaled, 1)
                    link(nc.vector.tensor_scalar(sig[:, sl], sig[:, sl], MAGIC, None, ALU.subtract))
                link(nc.vector.tensor_tensor(sig[:, sl], sig[:, sl], up[:, sl], ALU.mult))
            nc.vector.tensor_reduce(gm, sig, AX.X, ALU.max, apply_absolute_value=True).then_inc(gmax_part, 1)
            link(nc.vector.tensor_scalar(fold[:, 1:2], qsc[:, 3:4], qsc[:, 1:2], None, ALU.mult))
            global_max(4, fold[:, 1:2])
            sig3 = sig.rearrange("p (c n) -> p c n", c=6)
            link(nc.vector.memset(msc, 0.0))

            def o_token(s):
                to_integers(sig3[:, :, s * P:(s + 1) * P], 4).then_inc(o_ready, 1)

            pair = 0
            for s in range(S + 2):
                if s == 0:
                    o_token(0)
                if s + 1 < S:
                    o_token(s + 1)
                if s < S:
                    dve.wait_ge(down_mm, s + 1)
                    nc.vector.scalar_tensor_tensor(out=tok(H[0], s), in0=bank(6 + s % 2, C), scalar=qsc[:, 4:5],
                                                   in1=tok(H[1], s), op0=ALU.mult, op1=ALU.add).then_inc(down_read, 1)
                    dve.wait_ge(down_read, s + 1)
                    res_ln(S + s, tok(H[0], s), tok(H[0], s))
                if s in (1, 3, 5):
                    keep_token(dve, nc.vector.tensor_copy, h2T, 1, s - 1, hT2_kept_dve)
                if s >= 2:
                    q = s - 2
                    dve.wait_ge(l1_kept, 2 * (q + 1))
                    for k in range(q + 1):
                        m = nc.vector.tensor_tensor_reduce(out=scr[:, pair], in0=qkv[:, q, 0:C], in1=qkv[:, k, C:2 * C],
                                                           scale=C ** -0.5, scalar=0.0, op0=ALU.mult, op1=ALU.add,
                                                           accum_out=msc[:, q * S + k:q * S + k + 1])
                        pair += 1
            link(m)
            m3 = msc.rearrange("p (q k) -> p q k", k=S)
            zero = comb_w[:, 0:S * S]
            link(nc.vector.tensor_scalar(zero, msc, 0.0, -BIG, ALU.is_equal, ALU.mult))
            link(nc.vector.tensor_tensor(msc, msc, zero, ALU.add))
            link(nc.vector.tensor_reduce(mmx, m3, AX.X, ALU.max))
            nc.vector.tensor_tensor(m3, m3, mmx.unsqueeze(2).to_broadcast([P, S, S]), ALU.subtract).then_inc(l1_shift, 1)
            dve.wait_ge(l1_exp, 1)
            link(nc.vector.tensor_reduce(msm, m3, AX.X, ALU.add))
            link(nc.vector.reciprocal(msm, msm))
            link(nc.vector.tensor_tensor(m3, m3, msm.unsqueeze(2).to_broadcast([P, S, S]), ALU.mult))
            def values(qs):
                for k in range(qs[-1] + 1):
                    for q in qs:
                        if q >= k:
                            prev = tok(H[0], q) if k == 0 else tok(H[1], q)
                            m = nc.vector.scalar_tensor_tensor(out=tok(H[1], q), in0=qkv[:, k, 2 * C:3 * C],
                                                               scalar=msc[:, q * S + k:q * S + k + 1], in1=prev,
                                                               op0=ALU.mult, op1=ALU.add)
                    link(m)

            values((0, 1, 2))
            res_ln(2 * S, H[1][:, 0:3 * C], H[1][:, 0:3 * C], 3, lambda: values((3, 4)))
            res_ln(2 * S + 1, H[1][:, 3 * C:5 * C], H[1][:, 3 * C:5 * C], 2)

            for s in range(S):
                split_token(h3T_hi, h3T, 2, 4, s)
            dve.wait_ge(r_sig, 1)
            route(dve, link)
            hcount = 0
            g = 0
            for n, (kind, c, hf) in enumerate(MOE):
                o = hid[:, c, hf * 320:(hf + 1) * 320]
                if n == FIRST_COMB:
                    dve.wait_ge(combT_mm, 1)
                    link(nc.vector.tensor_copy(combT[0:NE, 0:512], bank(6)[0:NE, :]))
                    nc.vector.tensor_copy(combT[0:NE, 512:640], bank(7)[0:NE, 0:P]).then_inc(combT_kept, 1)
                if kind == "up":
                    dve.wait_ge(moe_mm, n + 1)
                    dve.wait_ge(moe_sil, g + 1)
                    nc.vector.tensor_tensor(o, bank(n % 6, 320), sil[g % 2], ALU.mult).then_inc(moe_hid, 1)
                    g += 1
                    hcount += 1
                elif kind == "comb":
                    dve.wait_ge(moe_mm, n + 1)
                    dve.wait_ge(moe_hid, hcount)
                    nc.vector.tensor_tensor(o, bank(n % 6, 320), o, ALU.mult).then_inc(moe_hid, 1)
                    hcount += 1
            for s in range(S):
                dve.wait_ge(down_mm, S + s + 1)
                nc.vector.tensor_tensor(tok(H[0], s), bank(s % 2, C), tok(H[1], s), ALU.add).then_inc(down_read, 1)
                dve.wait_ge(down_read, S + s + 1)
                res_ln(2 * S + 2 + s, tok(H[0], s), tok(H[0], s))


def constants():
    p = np.arange(P)
    slot = p % 32
    own = ((slot[:, None] // S == np.arange(GI)[None]) & (slot[:, None] < GI * S)).astype(np.float32)
    onehot = np.zeros((32, S, P), np.float32)
    for j in range(S):
        n = slot % S - j
        bucket = np.where(n < 0, 16, 0) + np.abs(n)
        onehot[bucket, j, p] = 1.0
    lower = np.tril(np.ones((NE, NE), np.float32), -1)
    pick = np.zeros((NE, NE // 2, P), np.float32)
    for e in range(NE):
        pick[e, e // 2, (e % 2) * EH:(e % 2 + 1) * EH] = 1.0
    return {"c_ident": np.eye(P, dtype=np.float32), "c_own": own, "c_onehot": onehot.reshape(32, S * P),
            "c_ties": lower, "c_ties4": lower[0:4, 0:4].copy(), "c_pick": pick.reshape(NE, NE // 2 * P)}


_UNUSED = ("L0_tok_pixel_masks",)


def kernel(**inputs):
    import concourse.bacc as _bacc
    from concourse.bass_utils import run_bass_kernel_spmd as _run

    nc = _bacc.Bacc("TRN2", target_bir_lowering=False, num_devices=1)
    arrays, args = {}, {}
    for name, value in list(inputs.items()) + list(constants().items()):
        if name in _UNUSED:
            continue
        v = np.ascontiguousarray(value)
        arrays[f"in_{name}_dram"] = v
        args[name] = nc.dram_tensor(f"in_{name}_dram", v.shape, mybir.dt.from_np(v.dtype), kind="ExternalInput").ap()
    out = nc.dram_tensor("out_0_dram", (P, S, C), F32, kind="ExternalOutput").ap()
    bass_vit_tower(nc, args, out)
    r = _run(nc, [arrays], core_ids=[0])
    return r.results[0]["out_0_dram"]
```
